# Optimizing a Trainium2 kernel written in Bass

```python
import numpy as np
import jax
import jax.numpy as jnp

def _softmax(x, axis=-1):
    return jax.nn.softmax(x, axis=axis)

def _gelu(x):
    return jax.nn.gelu(x, approximate=True)

def _silu(x):
    return jax.nn.silu(x)

def _sigmoid(x):
    return jax.nn.sigmoid(x)

def _layernorm(x, axis=-1, eps=1e-05):
    m = jnp.mean(x, axis=axis, keepdims=True)
    v = jnp.var(x, axis=axis, keepdims=True)
    return (x - m) / jnp.sqrt(v + eps)

def _scatter_add(tgt, idx, src, axis=0):
    return tgt.at[idx].add(src)

def _segment_sum(src, seg, n):
    return jax.ops.segment_sum(src, seg, n)
kernel_name = 'mk_flamingo_gated_d2_seqx_r4_aa1a4b'

def setup_inputs(seed: int=0):
    np.random.seed(seed)
    _w = jnp.asarray

    def _rec_inputs():
        import jax
        import jax.numpy as jnp
        _rk = jax.random.key(seed)
        x = -0.0002928 + 1 * jax.random.normal(jax.random.fold_in(_rk, 1), (8, 112, 256), jnp.float32)
        _lenS = 112 - jax.random.randint(jax.random.fold_in(_rk, 7), (8,), 0, max(1, 112 // 4) + 1, jnp.int32)
        _lenS2 = 375 - jax.random.randint(jax.random.fold_in(_rk, 8), (8,), 0, max(1, 375 // 4) + 1, jnp.int32)
        _ctx_1024P = jax.random.normal(jax.random.fold_in(_rk, 11), (8, 16, 256), jnp.float32)
        _ctx_1024c = jax.random.dirichlet(jax.random.fold_in(_rk, 511), 0.3 * jnp.ones((16,), jnp.float32), (8, 375))
        _ctx_1024t = jnp.einsum('bsk,bkd->bsd', _ctx_1024c, _ctx_1024P)
        _ctx_1024t = _ctx_1024t * jax.lax.rsqrt(jnp.mean(jnp.square(_ctx_1024t)) + 1e-12) * 0.953939
        ctx_1024 = -1.39393e-06 + 0.999914 * (_ctx_1024t + 0.3 * jax.random.normal(jax.random.fold_in(_rk, 611), (8, 375, 256), jnp.float32))
        _validS = jnp.arange(112)[None, :] < _lenS[:, None]
        _validS2 = jnp.arange(375)[None, :] < _lenS2[:, None]
        _causal = jnp.tril(jnp.ones((112, 112), dtype=bool))
        mask_Bx1xSxS2_ik1 = jnp.where(jnp.broadcast_to(_validS2[:, None, None, :], (8, 1, 112, 375)), 1, 0).astype(jnp.int32)
        mask_BxSxS2_bk1 = jnp.broadcast_to(_validS2[:, None, :], (8, 112, 375))
        _g = jax.random.normal(jax.random.fold_in(_rk, 9001), (2, 2), jnp.float32)
        _g = jnp.sign(_g) * jnp.maximum(jnp.abs(_g), 1.0) + (_g == 0) * 1.0
        g_xattn = _g[0]
        g_ffn = _g[1]
        return (x, ctx_1024, mask_Bx1xSxS2_ik1, mask_BxSxS2_bk1, g_xattn, g_ffn)
    x, ctx_1024, mask_Bx1xSxS2_ik1, mask_BxSxS2_bk1, g_xattn, g_ffn = _rec_inputs()

    def _L0_xattn_setup():
        import jax, jax.numpy as jnp
        import numpy as np
        HIDDEN = 256
        HEADS = 16
        HEAD_DIM = HIDDEN // HEADS
        SCALE = HEAD_DIM ** (-0.5)
        NEG_INF = -1000000000.0

        def _split_heads(x):
            B, S, _ = x.shape
            return x.reshape(B, S, HEADS, HEAD_DIM).transpose(0, 2, 1, 3)
        key = jax.random.key(seed)
        ks = jax.random.split(key, 12)
        B, Sq, Sk = (2, 512, 512)
        inp = {'query': jax.random.normal(ks[0], (B, Sq, HIDDEN), jnp.float32), 'key': jax.random.normal(ks[1], (B, Sk, HIDDEN), jnp.float32), 'value': jax.random.normal(ks[2], (B, Sk, HIDDEN), jnp.float32), 'mask': jax.random.randint(ks[3], (B, 1, Sq, Sk), 0, 2, jnp.int32), 'Wq': jax.random.normal(ks[4], (HIDDEN, HIDDEN), jnp.float32) * 0.02, 'bq': jax.random.normal(ks[5], (HIDDEN,), jnp.float32) * 0.02, 'Wk': jax.random.normal(ks[6], (HIDDEN, HIDDEN), jnp.float32) * 0.02, 'bk': jax.random.normal(ks[7], (HIDDEN,), jnp.float32) * 0.02, 'Wv': jax.random.normal(ks[8], (HIDDEN, HIDDEN), jnp.float32) * 0.02, 'bv': jax.random.normal(ks[9], (HIDDEN,), jnp.float32) * 0.02, 'Wo': jax.random.normal(ks[10], (HIDDEN, HIDDEN), jnp.float32) * 0.02}
        return inp
    _L0_xattn_all = _L0_xattn_setup()
    _L0_xattn_in = {k: v for k, v in _L0_xattn_all.items() if k in ('Wq', 'bq', 'Wk', 'bk', 'Wv', 'bv', 'Wo')}
    del _L0_xattn_all

    def _L0_ffn_setup():
        import jax, jax.numpy as jnp
        import numpy as np
        D = 256
        E = 12
        HS = 2 * D
        HR = 3 * D
        TAU = 1.5

        def _geglu(h):
            a, g = jnp.split(h, 2, axis=-1)
            return a * jax.nn.gelu(g, approximate=False)
        key = jax.random.key(seed)
        ks = jax.random.split(key, 12)

        def xavier(k, shape):
            fan_in, fan_out = (shape[-2], shape[-1])
            lim = jnp.sqrt(6.0 / (fan_in + fan_out))
            return jax.random.uniform(k, shape, jnp.float32, -lim, lim)
        x = jax.random.normal(ks[0], (2, 256, D), jnp.float32)
        Ws1 = xavier(ks[1], (D, 2 * HS))
        bs1 = jnp.zeros((2 * HS,), jnp.float32)
        Ws2 = xavier(ks[2], (HS, D))
        bs2 = jnp.zeros((D,), jnp.float32)
        We1 = xavier(ks[3], (E, D, 2 * HR))
        be1 = jnp.zeros((E, 2 * HR), jnp.float32)
        We2 = xavier(ks[4], (E, HR, D))
        be2 = jnp.zeros((E, D), jnp.float32)
        Wr = xavier(ks[5], (D, E))
        br = jnp.zeros((E,), jnp.float32)
        return {'x': x, 'Ws1': Ws1, 'bs1': bs1, 'Ws2': Ws2, 'bs2': bs2, 'We1': We1, 'be1': be1, 'We2': We2, 'be2': be2, 'Wr': Wr, 'br': br}
    _L0_ffn_all = _L0_ffn_setup()
    _L0_ffn_in = {k: v for k, v in _L0_ffn_all.items() if k in ('Ws1', 'bs1', 'Ws2', 'bs2', 'We1', 'be1', 'We2', 'be2', 'Wr', 'br')}
    del _L0_ffn_all

    def _L1_xattn_setup():
        import jax, jax.numpy as jnp
        import numpy as np
        HEADS = 16
        key = jax.random.key(seed)
        ks = jax.random.split(key, 8)
        B, S, Hd = (2, 512, 256)
        q = jax.random.normal(ks[0], (B, S, Hd), dtype=jnp.float32)
        k = jax.random.normal(ks[1], (B, S, Hd), dtype=jnp.float32)
        v = jax.random.normal(ks[2], (B, S, Hd), dtype=jnp.float32)
        mask = jax.random.randint(ks[3], (B, S, S), 0, 2).astype(jnp.bool_)
        sc = 1.0 / np.sqrt(Hd)
        Wq = jax.random.normal(ks[4], (Hd, Hd), dtype=jnp.float32) * sc
        Wk = jax.random.normal(ks[5], (Hd, Hd), dtype=jnp.float32) * sc
        Wv = jax.random.normal(ks[6], (Hd, Hd), dtype=jnp.float32) * sc
        Wo = jax.random.normal(ks[7], (Hd, Hd), dtype=jnp.float32) * sc
        return {'q': q, 'k': k, 'v': v, 'mask': mask, 'Wq': Wq, 'Wk': Wk, 'Wv': Wv, 'Wo': Wo}
    _L1_xattn_all = _L1_xattn_setup()
    _L1_xattn_in = {k: v for k, v in _L1_xattn_all.items() if k in ('Wq', 'Wk', 'Wv', 'Wo')}
    del _L1_xattn_all

    def _L1_ffn_setup():
        import jax, jax.numpy as jnp
        import numpy as np
        B, S, D_IN, D_OUT, E, GATE_K, TOP_K = (4, 2048, 256, 256, 8, 64, 2)

        def _gate(x, Vg):
            T = x.shape[0]
            xe = jnp.einsum('ti,eir->ter', x, Vg)
            proj = jnp.einsum('ter,eir->tei', xe, Vg)
            residuals = jnp.linalg.norm(x[:, None, :] - proj, axis=-1)
            rw = jax.nn.softmax(-residuals, axis=1)
            thr = 1.0 / E
            mask = rw > thr
            rows = jnp.arange(T)[:, None]
            top1_idx = jnp.argmax(rw, axis=1, keepdims=True)
            top1_mask = jnp.zeros_like(mask).at[rows, top1_idx].set(True)
            mask = jnp.where(jnp.any(mask), mask, top1_mask)
            if TOP_K < E:
                _, topi = jax.lax.top_k(rw, TOP_K)
                topk_mask = jnp.zeros_like(mask).at[rows, topi].set(True)
                mask = mask & topk_mask
            fw = rw * mask.astype(rw.dtype)
            sw = fw.sum(axis=1, keepdims=True)
            sw = jnp.where(sw == 0, jnp.ones_like(sw), sw)
            return fw / sw
        key = jax.random.key(seed)
        ks = jax.random.split(key, 6)
        return {'hidden_states': jax.random.normal(ks[0], (B, S, D_IN), dtype=jnp.float32), 'Wp': jax.random.normal(ks[1], (D_OUT, D_IN), dtype=jnp.float32) * 0.02, 'bp': jax.random.normal(ks[2], (D_OUT,), dtype=jnp.float32) * 0.02, 'We': jax.random.normal(ks[3], (E, D_OUT, D_IN), dtype=jnp.float32) * 0.02, 'be': jax.random.normal(ks[4], (E, D_OUT), dtype=jnp.float32) * 0.02, 'Vg': jax.random.normal(ks[5], (E, D_IN, GATE_K), dtype=jnp.float32) * 0.05}
    _L1_ffn_all = _L1_ffn_setup()
    _L1_ffn_in = {k: v for k, v in _L1_ffn_all.items() if k in ('Wp', 'bp', 'We', 'be', 'Vg')}
    del _L1_ffn_all
    return {'x': x, 'ctx_1024': ctx_1024, 'mask_Bx1xSxS2_ik1': mask_Bx1xSxS2_ik1, 'mask_BxSxS2_bk1': mask_BxSxS2_bk1, 'g_xattn': g_xattn, 'g_ffn': g_ffn, 'L0_xattn_Wq': _L0_xattn_in['Wq'], 'L0_xattn_bq': _L0_xattn_in['bq'], 'L0_xattn_Wk': _L0_xattn_in['Wk'], 'L0_xattn_bk': _L0_xattn_in['bk'], 'L0_xattn_Wv': _L0_xattn_in['Wv'], 'L0_xattn_bv': _L0_xattn_in['bv'], 'L0_xattn_Wo': _L0_xattn_in['Wo'], 'L0_ffn_Ws1': _L0_ffn_in['Ws1'], 'L0_ffn_bs1': _L0_ffn_in['bs1'], 'L0_ffn_Ws2': _L0_ffn_in['Ws2'], 'L0_ffn_bs2': _L0_ffn_in['bs2'], 'L0_ffn_We1': _L0_ffn_in['We1'], 'L0_ffn_be1': _L0_ffn_in['be1'], 'L0_ffn_We2': _L0_ffn_in['We2'], 'L0_ffn_be2': _L0_ffn_in['be2'], 'L0_ffn_Wr': _L0_ffn_in['Wr'], 'L0_ffn_br': _L0_ffn_in['br'], 'L1_xattn_Wq': _L1_xattn_in['Wq'], 'L1_xattn_Wk': _L1_xattn_in['Wk'], 'L1_xattn_Wv': _L1_xattn_in['Wv'], 'L1_xattn_Wo': _L1_xattn_in['Wo'], 'L1_ffn_Wp': _L1_ffn_in['Wp'], 'L1_ffn_bp': _L1_ffn_in['bp'], 'L1_ffn_We': _L1_ffn_in['We'], 'L1_ffn_be': _L1_ffn_in['be'], 'L1_ffn_Vg': _L1_ffn_in['Vg']}

def reference(x, ctx_1024, mask_Bx1xSxS2_ik1, mask_BxSxS2_bk1, g_xattn, g_ffn, L0_xattn_Wq, L0_xattn_bq, L0_xattn_Wk, L0_xattn_bk, L0_xattn_Wv, L0_xattn_bv, L0_xattn_Wo, L0_ffn_Ws1, L0_ffn_bs1, L0_ffn_Ws2, L0_ffn_bs2, L0_ffn_We1, L0_ffn_be1, L0_ffn_We2, L0_ffn_be2, L0_ffn_Wr, L0_ffn_br, L1_xattn_Wq, L1_xattn_Wk, L1_xattn_Wv, L1_xattn_Wo, L1_ffn_Wp, L1_ffn_bp, L1_ffn_We, L1_ffn_be, L1_ffn_Vg):
    import jax
    import jax.numpy as jnp

    def _L0_xattn_ref(query, key, value, mask, Wq, bq, Wk, bk, Wv, bv, Wo):
        import jax, jax.numpy as jnp
        import numpy as np
        HIDDEN = 256
        HEADS = 16
        HEAD_DIM = HIDDEN // HEADS
        SCALE = HEAD_DIM ** (-0.5)
        NEG_INF = -1000000000.0

        def _split_heads(x):
            B, S, _ = x.shape
            return x.reshape(B, S, HEADS, HEAD_DIM).transpose(0, 2, 1, 3)
        B, Sq, _ = query.shape
        q = _split_heads(query @ Wq.T + bq)
        k = _split_heads(key @ Wk.T + bk)
        v = _split_heads(value @ Wv.T + bv)
        scores = jnp.einsum('bhqd,bhkd->bhqk', q, k) * SCALE
        scores = jnp.where(mask == 0, NEG_INF, scores)
        attn = jax.nn.silu(scores)
        out = jnp.einsum('bhqk,bhkd->bhqd', attn, v)
        out = out.transpose(0, 2, 1, 3).reshape(B, Sq, HIDDEN)
        return out @ Wo.T

    def _L0_ffn_ref(x, Ws1, bs1, Ws2, bs2, We1, be1, We2, be2, Wr, br):
        import jax, jax.numpy as jnp
        import numpy as np
        D = 256
        E = 12
        HS = 2 * D
        HR = 3 * D
        TAU = 1.5

        def _geglu(h):
            a, g = jnp.split(h, 2, axis=-1)
            return a * jax.nn.gelu(g, approximate=False)
        B, T, Dm = x.shape
        xf = x.reshape(-1, Dm)
        ys = _geglu(xf @ Ws1 + bs1) @ Ws2 + bs2
        logits = (xf @ Wr + br) / TAU
        top_val, top_idx = jax.lax.top_k(logits, 2)
        top_w = jax.nn.softmax(top_val, axis=-1)
        onehot = jax.nn.one_hot(top_idx, E, dtype=x.dtype)
        w = jnp.einsum('nke,nk->ne', onehot, top_w)
        h = jnp.einsum('nd,edh->enh', xf, We1) + be1[:, None, :]
        act = _geglu(h)
        yE = jnp.einsum('enh,ehd->end', act, We2) + be2[:, None, :]
        yr = jnp.einsum('end,ne->nd', yE, w)
        return (ys + yr).reshape(B, T, Dm)

    def _L1_xattn_ref(q, k, v, mask, Wq, Wk, Wv, Wo):
        import jax, jax.numpy as jnp
        import numpy as np
        HEADS = 16
        B, Sq, Hd = q.shape
        H = HEADS
        d = Hd // H
        scale = 1.0 / np.sqrt(d).astype(np.float32)
        qh = (q @ Wq.T).reshape(B, Sq, H, d).transpose(0, 2, 1, 3)
        kh = (k @ Wk.T).reshape(B, -1, H, d).transpose(0, 2, 1, 3)
        vh = (v @ Wv.T).reshape(B, -1, H, d).transpose(0, 2, 1, 3)
        scores = jnp.einsum('bhqd,bhkd->bhqk', qh, kh)
        scores = jnp.where(mask[:, None, :, :], jnp.float32(-1000000000.0), scores) * scale
        attn = jax.nn.softmax(scores, axis=-1)
        out = jnp.einsum('bhqk,bhkd->bhqd', attn, vh)
        out = out.transpose(0, 2, 1, 3).reshape(B, Sq, Hd)
        return out @ Wo.T

    def _L1_ffn_ref(hidden_states, Wp, bp, We, be, Vg):
        import jax, jax.numpy as jnp
        import numpy as np
        B, S, D_IN, D_OUT, E, GATE_K, TOP_K = (4, 2048, 256, 256, 8, 64, 2)

        def _gate(x, Vg):
            T = x.shape[0]
            xe = jnp.einsum('ti,eir->ter', x, Vg)
            proj = jnp.einsum('ter,eir->tei', xe, Vg)
            residuals = jnp.linalg.norm(x[:, None, :] - proj, axis=-1)
            rw = jax.nn.softmax(-residuals, axis=1)
            thr = 1.0 / E
            mask = rw > thr
            rows = jnp.arange(T)[:, None]
            top1_idx = jnp.argmax(rw, axis=1, keepdims=True)
            top1_mask = jnp.zeros_like(mask).at[rows, top1_idx].set(True)
            mask = jnp.where(jnp.any(mask), mask, top1_mask)
            if TOP_K < E:
                _, topi = jax.lax.top_k(rw, TOP_K)
                topk_mask = jnp.zeros_like(mask).at[rows, topi].set(True)
                mask = mask & topk_mask
            fw = rw * mask.astype(rw.dtype)
            sw = fw.sum(axis=1, keepdims=True)
            sw = jnp.where(sw == 0, jnp.ones_like(sw), sw)
            return fw / sw
        in_shape = hidden_states.shape
        pretrained_out = jnp.einsum('bsi,oi->bso', hidden_states, Wp) + bp
        x = hidden_states.reshape(-1, in_shape[-1])
        w = _gate(x, Vg)
        expert_out = jnp.einsum('ti,eoi->teo', x, We) + be[None]
        final = jnp.einsum('te,teo->to', w, expert_out)
        final = final.reshape(*in_shape[:-1], We.shape[1])
        return pretrained_out + final
    x = x + jnp.tanh(g_xattn[0]) * _L0_xattn_ref(_layernorm(x, axis=-1), ctx_1024, ctx_1024, mask_Bx1xSxS2_ik1, L0_xattn_Wq, L0_xattn_bq, L0_xattn_Wk, L0_xattn_bk, L0_xattn_Wv, L0_xattn_bv, L0_xattn_Wo)
    x = x + jnp.tanh(g_ffn[0]) * _L0_ffn_ref(_layernorm(x, axis=-1), L0_ffn_Ws1, L0_ffn_bs1, L0_ffn_Ws2, L0_ffn_bs2, L0_ffn_We1, L0_ffn_be1, L0_ffn_We2, L0_ffn_be2, L0_ffn_Wr, L0_ffn_br)
    x = x + jnp.tanh(g_xattn[1]) * _L1_xattn_ref(_layernorm(x, axis=-1), ctx_1024, ctx_1024, mask_BxSxS2_bk1, L1_xattn_Wq, L1_xattn_Wk, L1_xattn_Wv, L1_xattn_Wo)
    x = x + jnp.tanh(g_ffn[1]) * _L1_ffn_ref(_layernorm(x, axis=-1), L1_ffn_Wp, L1_ffn_bp, L1_ffn_We, L1_ffn_be, L1_ffn_Vg)
    return x

_drawn_inputs = setup_inputs


def setup_inputs(seed=0):
    import zlib

    import numpy as np

    out = dict(_drawn_inputs(seed))
    spreads = {'g_ffn': (-1.0, 0.6),
     'L0_ffn_bs1': (0.0, 0.1),
     'L0_ffn_bs2': (0.0, 0.1),
     'L0_ffn_be1': (0.0, 0.1),
     'L0_ffn_be2': (0.0, 0.1),
     'L0_ffn_br': (0.0, 0.1)}
    factors = {'L1_ffn_bp': 4.272, 'L1_ffn_be': 6.083}
    for name, (base, spread) in spreads.items():
        noise = np.random.default_rng([zlib.crc32(name.encode()), seed]).standard_normal(out[name].shape)
        drawn = base * np.exp(spread * noise) if base else spread * noise
        out[name] = jnp.asarray(drawn.astype(out[name].dtype))
    for name, factor in factors.items():
        out[name] = (out[name] * factor).astype(out[name].dtype)
    return out
```

```python
from contextlib import ExitStack

import concourse.bass as bass
from concourse import mybir

F32 = mybir.dt.float32
BF16 = mybir.dt.bfloat16
I32 = mybir.dt.int32
U32 = mybir.dt.uint32
U8 = mybir.dt.uint8
ALU = mybir.AluOpType
ACT = mybir.ActivationFunctionType
AX = mybir.AxisListType

B = 8
S = 112
D = 256
KD = D // 128
KEYS = 375
KT = 3
KW = KEYS // KT
H = 16
DH = D // H
HG = H // KD
G = 4
SCALE = float(DH) ** -0.5
EPS = 1e-5
NEG0 = -1e9
NEG1 = -1e30
E0 = 12
HR = 768
HM = HR // 128
HS = 512
SM = HS // 128
TAU = 1.5
SLOT = 128
ET = 2 * B * S // SLOT + E0 - 1
ZR = 5
THR = -(-B * S // SLOT)
E1 = 8
R1 = 64

C_ID = 0
C_TRI = C_ID + 128
C_HEAD = C_TRI + S
C_SPREAD = C_HEAD + HG
C_IOTA = C_SPREAD + G * 128
C_THR = C_IOTA + E0
C_LOW = C_THR + THR
C_TILE = C_LOW + E0 * E0
C_EPS = C_TILE + ET
C_END = C_EPS + 1


def constants():
    import numpy as np
    c = np.zeros((128, C_END), np.float32)
    c[:, C_ID:C_ID + 128] = np.eye(128)
    c[:S, C_TRI:C_TRI + S] = np.triu(np.ones((S, S)), 1)
    for h in range(HG):
        c[h * DH:(h + 1) * DH, C_HEAD + h] = 1
    for g in range(G):
        for j in range(4):
            c[4 * g + j, C_SPREAD + g * 128 + 32 * j:C_SPREAD + g * 128 + 32 * j + 32] = 1
    c[:, C_IOTA:C_IOTA + E0] = np.arange(E0)
    c[:, C_THR:C_THR + THR] = np.arange(THR) * SLOT
    c[:, C_LOW:C_LOW + E0 * E0] = np.tril(np.ones((E0, E0)), -1).reshape(-1)
    c[:, C_TILE:C_TILE + ET] = np.arange(ET)
    c[:, C_EPS] = EPS
    return c


def above(eng, sem, value):
    if not isinstance(value, int) or value > 0:
        eng.wait_ge(sem, value)


def hold(sp, sem, value, passed):
    if not isinstance(value, int) or value > 0:
        sp.wait_ge(sem, value)
        sp.sem_inc(passed, 1)


def pairs(eng, body, n=B // 2):
    for u in range(2):
        body(u, u)
    with eng.Fori(1, n - 1) as i:
        for u in range(2):
            body(2 * i + u, u)
    for u in range(2):
        body(2 * (n - 1) + u, u)


def known(b, value):
    return isinstance(b, int) and b == value


def at(ap, b):
    return ap[:, b:b + 1] if isinstance(b, int) else ap[:, bass.ds(b, 1)]


def spread_over(ap, axis, n):
    a = ap.unsqueeze(axis)
    shape = list(a.shape)
    shape[axis] = n
    return a.broadcast_to(shape)


class Memory:
    pass


def build(nc, d, phases=6):
    with ExitStack() as ctx:
        def sb(name, shape, dt=F32):
            return ctx.enter_context(nc.sbuf_tensor(name, shape, dt))

        m = Memory()
        m.x = sb("x", [S, B, D])
        m.xn = sb("xn", [S, B, D])
        m.xT = sb("xT", [128, KD, B * S])
        m.qT = sb("qT", [128, KD, B * S])
        m.stat = sb("stat", [S, B, 6])
        m.mv = sb("mv", [S, B, 2])
        m.dev = sb("dev", [S, B])
        m.rstd = sb("rstd", [S, B])
        m.const = sb("const", [128, C_END])
        m.identb = sb("identb", [128, 128], BF16)
        m.gates = sb("gates", [128, 4])
        m.graw = sb("graw", [128, 4])
        m.bank = [ctx.enter_context(nc.psum_tensor(f"bank{i}", [128, 512], F32)) for i in range(8)]
        m.passed = ctx.enter_context(nc.semaphore("passed"))
        m.ident = m.const[:, C_ID:C_ID + 128]

        attention_phase(nc, d, m, 0)
        if phases > 1:
            with ExitStack() as ffn:
                experts_phases(nc, d, m, ffn, phases)
        if phases > 3:
            attention_phase(nc, d, m, 1)
        if phases > 4:
            gated_phase(nc, d, m)
        else:
            with nc.semaphore("x_out") as x_out, nc.Block() as block:
                @block.sync
                def _(sp):
                    sp.dma_start(d["out"].rearrange("b s n -> s b n"), m.x[:]).then_inc(x_out, 16)
                    sp.wait_ge(x_out, 16)


def normalise_rows(dve, m, row_stat, row_mv, row_dev, row_rstd, rows_done, x_loaded=None):
    def row(ap, t):
        return ap[:, bass.ds(t, 1)].rearrange("p a n -> p (a n)")
    if x_loaded is not None:
        dve.wait_ge(x_loaded, 16)
    for t in range(B):
        dve.bn_stats(m.stat[:, t, :], m.x[:, t, :]).then_inc(row_stat, 1)
    for t in range(B):
        dve.wait_ge(row_stat, t + 1)
        dve.bn_aggr(m.mv[:, t, :], m.stat[:, t, :]).then_inc(row_mv, 1)
    dve.wait_ge(row_dev, 1)
    dve.reciprocal(m.rstd[:], m.dev[:]).then_inc(row_rstd, 1)
    dve.wait_ge(row_rstd, 1)
    with dve.Fori(0, B) as t:
        dve.tensor_scalar(row(m.xn, t), row(m.x, t), m.mv[:, bass.ds(t, 1), 0], m.rstd[:, bass.ds(t, 1)],
                          ALU.subtract, ALU.mult).then_inc(rows_done, 1)


def deviations(act, m, row_mv, row_dev):
    act.wait_ge(row_mv, B)
    act.activation(m.dev[:], m.mv[:, :, 1], ACT.Sqrt, bias=m.const[:S, C_EPS:C_EPS + 1]).then_inc(row_dev, 1)


def transpose_rows(pe, m, banks, rows_done, turned, turned_copied):
    for t in range(B):
        pe.wait_ge(rows_done, t + 1)
        above(pe, turned_copied, t - 1)
        for k in range(KD):
            mm = pe.transpose(banks[t % 2][:, k * S:(k + 1) * S], m.xn[:, t, k * 128:(k + 1) * 128], m.ident[:S, :S])
        mm.then_inc(turned, 1)


def copy_turned(act, m, banks, turned, turned_copied):
    for t in range(B):
        act.wait_ge(turned, t + 1)
        act.activation(m.xT[:, :, t * S:(t + 1) * S], banks[t % 2][:, 0:KD * S].rearrange("p (k n) -> p k n", k=KD),
                       ACT.Copy).then_inc(turned_copied, 1)


def attention_phase(nc, d, m, layer):
    soft = layer == 1
    with ExitStack() as ctx:
        def sb(name, shape, dt=F32):
            return ctx.enter_context(nc.sbuf_tensor(f"{name}_{layer}", shape, dt))

        def sem(name):
            return ctx.enter_context(nc.semaphore(f"{name}_{layer}"))

        wq, wk, wv = sb("wq", [128, KD, D]), sb("wk", [128, KD, D]), sb("wv", [128, KD, D])
        wo = sb("wo", [128, G, D])
        ctxT = sb("ctxT", [128, 2, KD, KEYS])
        kT = sb("kT", [128, 2, KD, KEYS])
        v = sb("v", [KW, 2, KT, D])
        qd = sb("qd", [128, 2, KD, HG, S])
        oT = sb("oT", [128, 2, G, S])

        w_in, wo_zero, wo_in = sem("w_in"), sem("wo_zero"), sem("wo_in")
        x_in = None
        if layer == 0:
            x_in, const_in, g_in, gates_done, ident_done = (sem(n) for n in
                ("x_in", "const_in", "g_in", "gates_done", "ident_done"))
        ctx_in = [sem("ctx_in0"), sem("ctx_in1")]
        mask_in = [sem("mask_in0"), sem("mask_in1")]
        rows_zero = sem("rows_zero")
        row_stat, row_mv, row_dev, row_rstd, rows_done, turned, turned_copied = (sem(n) for n in
            ("row_stat", "row_mv", "row_dev", "row_rstd", "rows_done", "turned", "turned_copied"))
        q_done, q_copied, qd_done = sem("q_done"), sem("q_copied"), sem("qd_done")
        v_done, v_copied, k_done, k_copied = (sem(n) for n in ("v_done", "v_copied", "k_done", "k_copied"))
        bias_done, score_done, attn_done, pv_done = (sem(n) for n in ("bias_done", "score_done", "attn_done", "pv_done"))
        o_copied, proj_done, x_done = sem("o_copied"), sem("proj_done"), sem("x_done")

        ctx_d, mask_d = d["ctxT"], d[f"mask{layer}"]
        pre = f"L{layer}_xattn_"

        if soft:
            maskr = sb("maskr", [S, 2, KEYS], U8)
            bias = sb("bias", [S, 2, KEYS], BF16)
            PR = 4
            p = sb("p", [S, PR, KEYS])
            pT = sb("pT", [KW, PR, KT, S])
            mx = sb("mx", [S, PR])
            nm = sb("nm", [S, PR])
            rsum = sb("rsum", [S, 2, H])
            rinv = sb("rinv", [S, 2, H])
            rT = sb("rT", [H, 2, S])
            max_done, nmax_done, exp_done, pT_done, pT_copied = (sem(n) for n in
                ("max_done", "nmax_done", "exp_done", "pT_done", "pT_copied"))
            rinv_done, rT_done, rT_copied, rb_done, norm_done = (sem(n) for n in
                ("rinv_done", "rT_done", "rT_copied", "rb_done", "norm_done"))
        else:
            maskr = sb("maskr", [KW, 2, KT, S], I32)
            bias = sb("bias", [KW, 2, KT, S], BF16)
            AR = 6
            attn = sb("attn", [KW, AR, 4, S])
            bqk = sb("bqk", [128, 2, KD])
            bv = sb("bv", [KW, D])

        with nc.Block() as block:
            @block.sync
            def _(sp):
                if layer == 0:
                    sp.dma_start(m.x[:], d["x"].rearrange("b s n -> s b n")).then_inc(x_in, 16)
                    sp.dma_start(m.const[:], d["const"]).then_inc(const_in, 16)
                else:
                    sp.dma_start(wq[:], d[pre + "WqT"].rearrange("(k p) n -> p k n", p=128)).then_inc(w_in, 16)

                def context(b, u):
                    hold(sp, k_done, KD * (b - 1), m.passed)
                    cs = ctx_d[b:b + 1] if isinstance(b, int) else ctx_d[bass.ds(b, 1)]
                    sp.dma_start(ctxT[:, u, :, :], cs.rearrange("a (k p) n -> p (a k) n", p=128)).then_inc(ctx_in[u], 16)
                    hold(sp, bias_done, b - 1, m.passed)
                    ms = mask_d[b:b + 1] if isinstance(b, int) else mask_d[bass.ds(b, 1)]
                    if soft:
                        src = ms.rearrange("a q k -> (a q) k")
                        sp.dma_start(maskr[:, u, :], src).then_inc(mask_in[u], 16)
                    else:
                        src = ms.rearrange("a (t p) q -> p (a t) q", p=KW)
                        sp.dma_start(maskr[:, u, :, :], src).then_inc(mask_in[u], 16)
                pairs(sp, context)

            @block.gpsimd
            def _(pool):
                pool.memset(wo[:], 0.0).then_inc(wo_zero, 1)
                pool.wait_ge(wo_zero, 1)
                for j in range(4):
                    src = d[pre + "WoT"].rearrange("(g j r) n -> j r g n", j=4, r=DH)[j]
                    pool.dma_start(wo[32 * j:32 * j + DH, :, :], src).then_inc(wo_in, 16)

                def spread_queries(b, u):
                    for k in range(KD):
                        above(pool, score_done, (H if soft else 12) * (b - 1))
                        q = m.qT[:, k, b * S:(b + 1) * S] if isinstance(b, int) else m.qT[:, k, bass.ds(b * S, S)]
                        pool.tensor_tensor(qd[:, u, k, :, :], spread_over(q, 1, HG),
                                           spread_over(m.const[:, C_HEAD:C_HEAD + HG], 2, S), ALU.mult).then_inc(qd_done, 1)
                pool.wait_ge(q_copied, 2 * KD)
                if layer == 0:
                    pool.wait_ge(const_in, 16)
                pairs(pool, spread_queries)

            @block.scalar
            def _(act):
                act.dma_start(wk[:], d[pre + "WkT"].rearrange("(k p) n -> p k n", p=128)).then_inc(w_in, 16)
                act.dma_start(wv[:], d[pre + "WvT"].rearrange("(k p) n -> p k n", p=128)).then_inc(w_in, 16)
                if layer == 0:
                    act.dma_start(wq[:], d[pre + "WqT"].rearrange("(k p) n -> p k n", p=128)).then_inc(w_in, 16)
                    act.dma_start(bqk[:, 0, :], d["bqT"]).then_inc(w_in, 16)
                    act.dma_start(bqk[:, 1, :], d["bkT"]).then_inc(w_in, 16)
                    act.dma_start(bv[:], d[pre + "bv"].partition_broadcast(KW)).then_inc(w_in, 16)
                    act.dma_start(m.graw[:, 0:2], d["g_xattn"].partition_broadcast(128)).then_inc(g_in, 16)
                    act.dma_start(m.graw[:, 2:4], d["g_ffn"].partition_broadcast(128)).then_inc(g_in, 16)
                    act.wait_ge(g_in, 32)
                    act.activation(m.gates[:], m.graw[:], ACT.Tanh).then_inc(gates_done, 1)
                    act.wait_ge(w_in, 96)

                def copy_keys(b, u):
                    for k in range(KD):
                        act.wait_ge(k_done, KD * b + k + 1)
                        src = m.bank[3 + k][:, 0:KEYS] if not soft else m.bank[7][:, 0:KEYS]
                        if soft:
                            act.activation(kT[:, u, k, :], src, ACT.Copy).then_inc(k_copied, 1)
                        else:
                            act.activation(kT[:, u, k, :], src, ACT.Identity, bias=bqk[:, 1, k:k + 1]).then_inc(k_copied, 1)

                if layer == 0:
                    act.wait_ge(const_in, 16)
                copy_keys(0, 0)
                deviations(act, m, row_mv, row_dev)
                copy_turned(act, m, m.bank[0:2], turned, turned_copied)
                for n in range(2 * KD):
                    act.wait_ge(q_done, n + 1)
                    dst = m.qT[:, n % KD, (n // KD) * 4 * S:(n // KD + 1) * 4 * S]
                    if soft:
                        act.activation(dst, m.bank[n % 2][:, 0:4 * S], ACT.Copy).then_inc(q_copied, 1)
                    else:
                        act.activation(dst, m.bank[n % 2][:, 0:4 * S], ACT.Identity, bias=bqk[:, 0, n % KD:n % KD + 1]).then_inc(q_copied, 1)

                def silu_batch(b, u):
                    for c in range(G * KT):
                        act.wait_ge(score_done, G * KT * b + c + 1)
                        above(act, pv_done, G * b + c // KT - 1)
                        act.activation(attn[:, c % AR, :, :], m.bank[c % 3][:KW, 0:4 * S].rearrange("p (j n) -> p j n", j=4),
                                       ACT.Silu, scale=SCALE).then_inc(attn_done, 1)
                    if not known(b, B - 1):
                        copy_keys(b + 1, 1 - u)

                def exp_batch(b, u):
                    for h in range(H):
                        n = H * b + h
                        act.wait_ge(nmax_done, n + 1)
                        above(act, pT_done, n - PR + 1)
                        act.activation(p[:, h % PR, :], m.bank[h % 4][:S, 0:KEYS], ACT.Exp, bias=nm[:, h % PR:h % PR + 1],
                                       scale=SCALE, accum_out=rsum[:, u, h:h + 1]).then_inc(exp_done, 1)
                        if h == 5 and not known(b, 0):
                            turn_sums(b - 1, 1 - u)
                        if h == 13 and not known(b, B - 1):
                            copy_keys(b + 1, 1 - u)

                def turn_sums(b, u):
                    act.wait_ge(rT_done, b + 1)
                    act.activation(rT[:, u, :], m.bank[7][:H, 0:S], ACT.Copy).then_inc(rT_copied, 1)

                pairs(act, exp_batch if soft else silu_batch)
                if soft:
                    turn_sums(B - 1, 1)

            @block.vector
            def _(dve):
                if layer == 0:
                    dve.wait_ge(const_in, 16)
                    dve.tensor_copy(m.identb[:], m.ident).then_inc(ident_done, 1)
                for i in ((6,) if soft else (5, 6)):
                    dve.memset(m.bank[i][:], 0.0).then_inc(rows_zero, 1)

                def make_bias(b, u):
                    dve.wait_ge(mask_in[u], 8 * (b - u) + 16)
                    if soft:
                        dve.tensor_scalar(bias[:, u, :], maskr[:, u, :], 0.0, NEG1, ALU.is_gt, ALU.mult).then_inc(bias_done, 1)
                    else:
                        dve.tensor_scalar(bias[:, u, :, :], maskr[:, u, :, :], 0.0, NEG0, ALU.is_equal, ALU.mult).then_inc(bias_done, 1)

                def copy_values(b, u, part):
                    dve.wait_ge(v_done, 2 * b + part + 1)
                    src = m.bank[7] if soft else m.bank[3 + part]
                    for t in ((0, 1) if part == 0 else (2,)):
                        pcol = (t % 2) * D
                        if soft:
                            ins = dve.tensor_copy(v[:, u, t, :], src[:KW, pcol:pcol + D])
                        else:
                            ins = dve.tensor_tensor(v[:, u, t, :], src[:KW, pcol:pcol + D], bv[:], ALU.add)
                    ins.then_inc(v_copied, 1)

                def residual(b, u):
                    dve.wait_ge(proj_done, b + 1)
                    bank = m.bank[7]
                    dve.scalar_tensor_tensor(out=at(m.x, b).rearrange("p a n -> p (a n)"), in0=bank[:S, 0:D], scalar=m.gates[:S, layer:layer + 1],
                                             in1=at(m.x, b).rearrange("p a n -> p (a n)"), op0=ALU.mult, op1=ALU.add).then_inc(x_done, 1)

                if layer == 0:
                    dve.wait_ge(w_in, 96)
                    dve.wait_ge(gates_done, 1)
                copy_values(0, 0, 0)
                copy_values(0, 0, 1)
                make_bias(0, 0)
                normalise_rows(dve, m, row_stat, row_mv, row_dev, row_rstd, rows_done, x_in)

                def after_silu(b, u):
                    if not known(b, B - 1):
                        make_bias(b + 1, 1 - u)
                        copy_values(b + 1, 1 - u, 0)
                        copy_values(b + 1, 1 - u, 1)
                    dve.wait_ge(pv_done, G * (b + 1))
                    dve.tensor_copy(oT[:, u, :, :], m.bank[5 + u][:, 0:G * S].rearrange("p (g n) -> p g n", g=G)).then_inc(o_copied, 1)
                    residual(b, u)

                def copy_probs(n, slot, bank):
                    dve.wait_ge(pT_done, n + 1)
                    above(dve, pv_done, n - PR + 1)
                    dve.tensor_copy(pT[:, slot, :, :], m.bank[bank][:KW, 0:KT * S].rearrange("p (t n) -> p t n", t=KT)).then_inc(pT_copied, 1)

                def invert_sums(b, u):
                    dve.wait_ge(exp_done, H * (b + 1))
                    dve.reciprocal(rinv[:, u, :], rsum[:, u, :]).then_inc(rinv_done, 1)

                def copy_out(b, u):
                    dve.wait_ge(pv_done, H * (b + 1))
                    dve.tensor_copy(oT[:, u, :, :], m.bank[6][:, 0:G * S].rearrange("p (g n) -> p g n", g=G)).then_inc(o_copied, 1)

                def divide(b, u):
                    dve.wait_ge(rb_done, b + 1)
                    dve.wait_ge(o_copied, b + 1)
                    dve.tensor_tensor(oT[:, u, :, :], m.bank[7][:, 0:G * S].rearrange("p (g n) -> p g n", g=G), oT[:, u, :, :],
                                      ALU.mult).then_inc(norm_done, 1)

                def soft_batch(b, u):
                    for h in range(H):
                        n = H * b + h
                        dve.wait_ge(score_done, n + 1)
                        above(dve, nmax_done, n - PR + 1)
                        dve.tensor_reduce(mx[:, h % PR:h % PR + 1], m.bank[h % 4][:S, 0:KEYS], AX.X, ALU.max).then_inc(max_done, 1)
                        if h >= 2 or not known(b, 0):
                            copy_probs(n - 2, (h - 2) % PR, 4 + h % 2)
                        dve.wait_ge(max_done, n + 1)
                        above(dve, exp_done, n - PR + 1)
                        dve.tensor_scalar(nm[:, h % PR:h % PR + 1], mx[:, h % PR:h % PR + 1], -SCALE, None, ALU.mult).then_inc(nmax_done, 1)
                        if not known(b, 0):
                            if h == 1:
                                invert_sums(b - 1, 1 - u)
                            if h == 2:
                                copy_out(b - 1, 1 - u)
                            if h == 5:
                                divide(b - 1, 1 - u)
                            if h == 7:
                                residual(b - 1, 1 - u)
                        if not known(b, B - 1):
                            if h == 8:
                                copy_values(b + 1, 1 - u, 0)
                            if h == 10:
                                copy_values(b + 1, 1 - u, 1)
                            if h == 12:
                                make_bias(b + 1, 1 - u)

                if soft:
                    pairs(dve, soft_batch)
                    for h in range(2):
                        copy_probs(H * B - 2 + h, (h + 2) % PR, 4 + h)
                    invert_sums(B - 1, 1)
                    copy_out(B - 1, 1)
                    divide(B - 1, 1)
                    residual(B - 1, 1)
                else:
                    pairs(dve, after_silu)

            @block.tensor
            def _(pe):
                def project_values(b, u, part):
                    if part == 0:
                        pe.wait_ge(ctx_in[u], 8 * (b - u) + 16)
                    if soft:
                        bank = m.bank[7]
                        if part == 0:
                            above(pe, x_done, b - 1)
                        else:
                            pe.wait_ge(v_copied, 2 * b + 1)
                    else:
                        bank = m.bank[3 + part]
                        above(pe, k_copied, KD * (b - 1) + part + 1)
                    for t in ((0, 1) if part == 0 else (2,)):
                        for k in range(KD):
                            mm = pe.matmul(bank[:KW, (t % 2) * D:(t % 2 + 1) * D], ctxT[:, u, k, t * KW:(t + 1) * KW], wv[:, k, :],
                                           start=k == 0, stop=k == KD - 1)
                    mm.then_inc(v_done, 1)

                def project_keys(b, u, half):
                    if soft:
                        bank = m.bank[7]
                        if half == 0:
                            pe.wait_ge(v_copied, 2 * b + 2)
                        else:
                            pe.wait_ge(k_copied, KD * b + 1)
                    else:
                        bank = m.bank[3 + half]
                        pe.wait_ge(v_copied, 2 * b + half + 1)
                    for k in range(KD):
                        mm = pe.matmul(bank[:, 0:KEYS], wk[:, k, half * 128:(half + 1) * 128], ctxT[:, u, k, :],
                                       start=k == 0, stop=k == KD - 1)
                    mm.then_inc(k_done, 1)

                pe.wait_ge(w_in, 96 if layer == 0 else 48)
                for part in range(2):
                    project_values(0, 0, part)
                for half in range(KD):
                    project_keys(0, 0, half)
                if layer == 0:
                    pe.wait_ge(const_in, 16)
                    pe.wait_ge(ident_done, 1)
                transpose_rows(pe, m, m.bank[0:2], rows_done, turned, turned_copied)
                pe.wait_ge(turned_copied, B)
                for n in range(2 * KD):
                    above(pe, q_copied, n - 1)
                    for k in range(KD):
                        mm = pe.matmul(m.bank[n % 2][:, 0:4 * S], wq[:, k, (n % KD) * 128:(n % KD + 1) * 128],
                                       m.xT[:, k, (n // KD) * 4 * S:(n // KD + 1) * 4 * S], start=k == 0, stop=k == KD - 1)
                    mm.then_inc(q_done, 1)
                pe.wait_ge(q_copied, 2 * KD)
                pe.wait_ge(wo_in, 64)
                pe.wait_ge(rows_zero, 1 if soft else 2)

                def project_out(b, u):
                    bank = m.bank[7]
                    if soft:
                        pe.wait_ge(norm_done, b + 1)
                    else:
                        pe.wait_ge(o_copied, b + 1)
                        above(pe, x_done, b)
                    for g in range(G):
                        mm = pe.matmul(bank[:S, 0:D], oT[:, u, g, :], wo[:, g, :], start=g == 0, stop=g == G - 1)
                    mm.then_inc(proj_done, 1)

                def silu_scores(b, u, g):
                    if g == 0:
                        pe.wait_ge(k_copied, KD * (b + 1))
                        pe.wait_ge(qd_done, KD * (b + 1))
                        pe.wait_ge(bias_done, b + 1)
                    for t in range(KT):
                        c = g * KT + t
                        above(pe, attn_done, G * KT * b + c - 2)
                        out = m.bank[c % 3][:KW, 0:4 * S]
                        pe.matmul(out, m.identb[:KW, :KW], spread_over(bias[:, u, t, :], 1, 4), start=True, stop=False)
                        pe.matmul(out, kT[:, u, g // 2, t * KW:(t + 1) * KW], qd[:, u, g // 2, 4 * (g % 2):4 * (g % 2) + 4, :],
                                  start=False, stop=True).then_inc(score_done, 1)

                def silu_values(b, u, g):
                    if g == 0:
                        pe.wait_ge(v_copied, 2 * (b + 1))
                        above(pe, o_copied, b - 1)
                    pe.wait_ge(attn_done, G * KT * b + (g + 1) * KT)
                    for t in range(KT):
                        for j in range(4):
                            mm = pe.matmul(m.bank[5 + u][32 * j:32 * j + DH, g * S:(g + 1) * S],
                                           v[:, u, t, (4 * g + j) * DH:(4 * g + j + 1) * DH], attn[:, (g * KT + t) % AR, j, :],
                                           start=t == 0, stop=t == KT - 1, tile_position=(0, 32 * j))
                    mm.then_inc(pv_done, 1)

                def silu_batch(b, u):
                    silu_scores(b, u, 0)
                    for g in range(1, G):
                        silu_scores(b, u, g)
                        silu_values(b, u, g - 1)
                    more = not known(b, B - 1)
                    if more:
                        project_values(b + 1, 1 - u, 0)
                        project_values(b + 1, 1 - u, 1)
                    silu_values(b, u, G - 1)
                    if more:
                        project_keys(b + 1, 1 - u, 0)
                        project_keys(b + 1, 1 - u, 1)
                    project_out(b, u)

                def soft_scores(b, u, h):
                    n = H * b + h
                    if h == 0:
                        pe.wait_ge(k_copied, KD * (b + 1))
                        pe.wait_ge(qd_done, KD * (b + 1))
                        pe.wait_ge(bias_done, b + 1)
                    above(pe, exp_done, n - 3)
                    out = m.bank[h % 4][:S, 0:KEYS]
                    pe.matmul(out, m.identb[:S, :S], bias[:, u, :], start=True, stop=False)
                    pe.matmul(out, qd[:, u, h // HG, h % HG, :], kT[:, u, h // HG, :], start=False, stop=True).then_inc(score_done, 1)

                def turn_probs(n, h):
                    pe.wait_ge(exp_done, n + 1)
                    above(pe, pT_copied, n - 1)
                    for t in range(KT):
                        mm = pe.transpose(m.bank[4 + h % 2][:KW, t * S:(t + 1) * S], p[:, h % PR, t * KW:(t + 1) * KW], m.ident[:S, :S])
                    mm.then_inc(pT_done, 1)

                def soft_values(b, u, h):
                    if h == 0:
                        pe.wait_ge(v_copied, 2 * (b + 1))
                        above(pe, o_copied, b)
                    pe.wait_ge(pT_copied, H * b + h + 1)
                    g, j = h // 4, h % 4
                    for t in range(KT):
                        mm = pe.matmul(m.bank[6][32 * j:32 * j + DH, g * S:(g + 1) * S], v[:, u, t, h * DH:(h + 1) * DH],
                                       pT[:, h % PR, t, :], start=t == 0, stop=t == KT - 1, tile_position=(0, 32 * j))
                    mm.then_inc(pv_done, 1)

                def turn_sums(b, u):
                    pe.wait_ge(rinv_done, b + 1)
                    if not known(b, B - 1):
                        above(pe, k_copied, KD * (b + 2))
                    pe.transpose(m.bank[7][:H, 0:S], rinv[:, u, :], m.ident[:S, :S]).then_inc(rT_done, 1)

                def spread_sums(b, u):
                    pe.wait_ge(rT_copied, b + 1)
                    for g in range(G):
                        mm = pe.matmul(m.bank[7][:, g * S:(g + 1) * S], m.const[:H, C_SPREAD + g * 128:C_SPREAD + (g + 1) * 128],
                                       rT[:, u, :], start=True, stop=True)
                    mm.then_inc(rb_done, 1)

                def soft_batch(b, u):
                    first, last = known(b, 0), known(b, B - 1)
                    for h in range(H):
                        soft_scores(b, u, h)
                        if h >= 2 or not first:
                            turn_probs(H * b + h - 2, (h - 2) % H)
                        if h >= 3:
                            soft_values(b, u, h - 3)
                        elif not first:
                            soft_values(b - 1, 1 - u, H + h - 3)
                        if not first:
                            if h == 3:
                                turn_sums(b - 1, 1 - u)
                            if h == 5:
                                spread_sums(b - 1, 1 - u)
                            if h == 7:
                                project_out(b - 1, 1 - u)
                        if not last:
                            if h == 8:
                                project_values(b + 1, 1 - u, 0)
                            if h == 10:
                                project_values(b + 1, 1 - u, 1)
                            if h == 11:
                                project_keys(b + 1, 1 - u, 0)
                            if h == 13:
                                project_keys(b + 1, 1 - u, 1)

                pairs(pe, soft_batch if soft else silu_batch)
                if soft:
                    for h in range(2):
                        turn_probs(H * B - 2 + h, H - 2 + h)
                        soft_values(B - 1, 1, H - 3 + h)
                    soft_values(B - 1, 1, H - 1)
                    turn_sums(B - 1, 1)
                    spread_sums(B - 1, 1)
                    project_out(B - 1, 1)


def experts_phases(nc, d, m, ctx, phases):
    def sb(name, shape, dt=F32):
        return ctx.enter_context(nc.sbuf_tensor(name, shape, dt))

    def sem(name):
        return ctx.enter_context(nc.semaphore(name))

    ys = sb("ys", [S, B, D])
    wts = sb("wts", [S, 2, B])
    pos = sb("pos", [S, 2, B], U32)
    tile_expert = sb("tile_expert", [1, ET], I32)
    xg_d = nc.dram_tensor("xg", [ET * SLOT, D], F32, kind="Internal").ap()
    y_d = nc.dram_tensor("y", [ET * SLOT, D], F32, kind="Internal").ap()

    route_phase(nc, d, m, ys, wts, pos, tile_expert, xg_d)
    expert_phase(nc, d, m, tile_expert, xg_d, y_d)
    combine_phase(nc, d, m, ys, wts, pos, y_d)


def route_phase(nc, d, m, ys, wts, pos, tile_expert, xg_d):
    with ExitStack() as ctx:
        def sb(name, shape, dt=F32):
            return ctx.enter_context(nc.sbuf_tensor(name, shape, dt))

        def sem(name):
            return ctx.enter_context(nc.semaphore(name))

        ws1, ws2, wr = sb("ws1", [128, KD, 2 * HS]), sb("ws2", [128, SM, D]), sb("wr", [128, KD, E0])
        bs1, bs2, br = sb("bs1", [128, 2 * SM]), sb("bs2", [S, D]), sb("br", [S, E0])
        zeros = sb("zeros", [SLOT, ZR * D])
        gel = sb("gel", [128, 2, 4 * S])
        act_s = sb("act_s", [128, SM, B * S])
        logit = sb("logit", [S, B, E0])
        top = sb("top", [S, B, 8])
        topi = sb("topi", [S, B, 8], U32)
        topf = sb("topf", [S, B, 2])
        gap, ex, den = sb("gap", [S, B]), sb("ex", [S, B]), sb("den", [S, B])
        hot = sb("hot", [S, 2, B, E0])
        both = sb("both", [S, B, E0], BF16)
        trib, onesb = sb("trib", [S, S], BF16), sb("onesb", [S, 128], BF16)
        run = sb("run", [128, B + 1, E0])
        over, tiles = sb("over", [128, E0, THR]), sb("tiles", [128, E0])
        low, start, end = sb("low", [128, E0, E0]), sb("start", [128, E0]), sb("end", [128, E0])
        past, owner = sb("past", [1, ET, E0]), sb("owner", [1, ET])
        base, picked, posf = sb("base", [S, B, E0]), sb("picked", [S, 2, B, E0]), sb("posf", [S, 2, B])

        w_in, zero_done, zero_out, scattered = sem("rw_in"), sem("rzero_done"), sem("rzero_out"), sem("scattered")
        row_stat, row_mv, row_dev, row_rstd, rows_done, turned, turned_copied = (sem("r" + n) for n in
            ("row_stat", "row_mv", "row_dev", "row_rstd", "rows_done", "turned", "turned_copied"))
        logit_done, gap_done, ex_done, both_done, count_done, pos_done = (sem(n) for n in
            ("logit_done", "gap_done", "ex_done", "both_done", "count_done", "pos_done"))
        step = sem("route_step")
        h_done, gelu_done, act_done, y_done, y_copied = (sem(n) for n in
            ("sh_done", "sgelu_done", "sact_done", "sy_done", "sy_copied"))

        with nc.Block() as block:
            @block.sync
            def _(sp):
                sp.dma_start(wr[:], d["L0_ffn_Wr"].rearrange("(k p) n -> p k n", p=128)).then_inc(w_in, 16)
                sp.dma_start(br[:], d["L0_ffn_br"].partition_broadcast(S)).then_inc(w_in, 16)
                sp.dma_start(ws1[:], d["L0_ffn_Ws1"].rearrange("(k p) n -> p k n", p=128)).then_inc(w_in, 16)
                sp.dma_start(bs1[:], d["bs1T"]).then_inc(w_in, 16)
                sp.dma_start(ws2[:], d["L0_ffn_Ws2"].rearrange("(k p) n -> p k n", p=128)).then_inc(w_in, 16)
                sp.dma_start(bs2[:], d["L0_ffn_bs2"].partition_broadcast(S)).then_inc(w_in, 16)
                sp.wait_ge(zero_done, 1)
                xz = xg_d.rearrange("(c p r) n -> c p (r n)", p=SLOT, r=ZR)
                for c in range(ET // ZR):
                    sp.dma_start(xz[c], zeros[:]).then_inc(zero_out, 16)

            @block.gpsimd
            def _(pool):
                pool.memset(zeros[:], 0.0).then_inc(zero_done, 1)
                pool.wait_ge(zero_out, 16 * (ET // ZR))
                pool.wait_ge(pos_done, 1)
                for t in range(B):
                    for c in range(2):
                        pool.indirect_dma_start(out=xg_d, out_offset=bass.IndirectOffsetOnAxis(ap=pos[:, c, t:t + 1], axis=0),
                                                in_=m.xn[:, t, :], in_offset=None).then_inc(scattered, 16)
                pool.wait_ge(scattered, 16 * 2 * B)

            @block.scalar
            def _(act):
                deviations(act, m, row_mv, row_dev)
                copy_turned(act, m, m.bank[0:2], turned, turned_copied)
                act.wait_ge(gap_done, 1)
                act.activation(ex[:], gap[:], ACT.Exp).then_inc(ex_done, 1)
                act.wait_ge(w_in, 96)
                for n in range(2 * SM):
                    act.wait_ge(h_done, n + 1)
                    above(act, act_done, n - 1)
                    act.activation(gel[:, n % 2, :], m.bank[3 + 2 * (n % 2)][:, 0:4 * S], ACT.Gelu,
                                   bias=bs1[:, SM + n % SM:SM + n % SM + 1]).then_inc(gelu_done, 1)

            @block.vector
            def _(dve):
                count = [0]

                def then(ins):
                    ins.then_inc(step, 1)
                    count[0] += 1
                    dve.wait_ge(step, count[0])

                dve.tensor_copy(trib[:], m.const[:S, C_TRI:C_TRI + S]).then_inc(both_done, 1)
                dve.memset(onesb[:], 1.0).then_inc(both_done, 1)
                dve.memset(run[:, 0, :], 0.0).then_inc(both_done, 1)
                normalise_rows(dve, m, row_stat, row_mv, row_dev, row_rstd, rows_done)
                dve.wait_ge(w_in, 96)
                dve.wait_ge(logit_done, 1)
                then(dve.tensor_tensor(logit[:], m.bank[7][:S, 0:B * E0].rearrange("p (t e) -> p t e", t=B),
                                       spread_over(br[:], 1, B), ALU.add))
                then(dve.tensor_scalar(logit[:], logit[:], 1.0 / TAU, None, ALU.mult))
                for t in range(B):
                    ins = dve.max(top[:, t, :], logit[:, t, :])
                then(ins)
                dve.tensor_tensor(gap[:], top[:, :, 1], top[:, :, 0], ALU.subtract).then_inc(gap_done, 1)
                for t in range(B):
                    ins = dve.max_index(topi[:, t, :], top[:, t, :], logit[:, t, :])
                then(ins)
                then(dve.tensor_copy(topf[:], topi[:, :, 0:2]))
                for c in range(2):
                    then(dve.tensor_tensor(hot[:, c, :, :], spread_over(m.const[:S, C_IOTA:C_IOTA + E0], 1, B),
                                           spread_over(topf[:, :, c], 2, E0), ALU.is_equal))
                dve.tensor_tensor(both[:], hot[:, 0, :, :], hot[:, 1, :, :], ALU.add).then_inc(both_done, 1)
                dve.wait_ge(ex_done, 1)
                then(dve.tensor_scalar(den[:], ex[:], 1.0, None, ALU.add))
                then(dve.reciprocal(wts[:, 0, :], den[:]))
                then(dve.tensor_tensor(wts[:, 1, :], ex[:], wts[:, 0, :], ALU.mult))
                dve.wait_ge(count_done, 1)
                for t in range(B):
                    then(dve.tensor_tensor(run[:, t + 1, :], m.bank[6][:, t * E0:(t + 1) * E0], run[:, t, :], ALU.add))
                then(dve.tensor_tensor(over[:], spread_over(run[:, B, :], 2, THR),
                                       spread_over(m.const[:, C_THR:C_THR + THR], 1, E0), ALU.is_gt))
                then(dve.tensor_reduce(tiles[:], over[:], AX.X, ALU.add))
                then(dve.tensor_tensor(low[:], spread_over(tiles[:], 1, E0),
                                       m.const[:, C_LOW:C_LOW + E0 * E0].rearrange("p (a b) -> p a b", a=E0), ALU.mult))
                then(dve.tensor_reduce(start[:], low[:], AX.X, ALU.add))
                then(dve.tensor_tensor(end[:], start[:], tiles[:], ALU.add))
                then(dve.tensor_tensor(base[:], m.bank[7][:S, 128:128 + B * E0].rearrange("p (t e) -> p t e", t=B),
                                       run[:S, 0:B, :], ALU.add))
                then(dve.scalar_tensor_tensor(out=base[:], in0=spread_over(start[:S, :], 1, B), scalar=float(SLOT), in1=base[:],
                                              op0=ALU.mult, op1=ALU.add))
                then(dve.tensor_tensor(picked[:], hot[:], spread_over(base[:], 1, 2), ALU.mult))
                then(dve.tensor_reduce(posf[:], picked[:], AX.X, ALU.add))
                dve.tensor_copy(pos[:], posf[:]).then_inc(pos_done, 1)
                then(dve.tensor_tensor(past[:], spread_over(end[0:1, :], 1, ET),
                                       spread_over(m.const[0:1, C_TILE:C_TILE + ET], 2, E0), ALU.is_le))
                then(dve.tensor_reduce(owner[:], past[:], AX.X, ALU.add))
                then(dve.tensor_scalar(tile_expert[:], owner[:], float(E0 - 1), None, ALU.min))
                for n in range(2 * SM):
                    dve.wait_ge(gelu_done, n + 1)
                    dve.scalar_tensor_tensor(out=act_s[:, n % SM, (n // SM) * 4 * S:(n // SM + 1) * 4 * S],
                                             in0=m.bank[2 + 2 * (n % 2)][:, 0:4 * S], scalar=bs1[:, n % SM:n % SM + 1],
                                             in1=gel[:, n % 2, :], op0=ALU.add, op1=ALU.mult).then_inc(act_done, 1)
                for t in range(B):
                    dve.wait_ge(y_done, t + 1)
                    dve.tensor_tensor(ys[:, t, :], m.bank[t % 2][:S, 0:D], bs2[:], ALU.add).then_inc(y_copied, 1)

            @block.tensor
            def _(pe):
                transpose_rows(pe, m, m.bank[0:2], rows_done, turned, turned_copied)
                pe.wait_ge(w_in, 96)
                pe.wait_ge(turned_copied, B)
                for t in range(B):
                    for k in range(KD):
                        mm = pe.matmul(m.bank[7][:S, t * E0:(t + 1) * E0], m.xT[:, k, t * S:(t + 1) * S], wr[:, k, :],
                                       start=k == 0, stop=k == KD - 1)
                mm.then_inc(logit_done, 1)

                def hidden(n):
                    above(pe, act_done, n - 1)
                    half, part = n // SM, n % SM
                    for a in range(2):
                        for k in range(KD):
                            mm = pe.matmul(m.bank[2 + 2 * (n % 2) + a][:, 0:4 * S],
                                           ws1[:, k, (a * SM + part) * 128:(a * SM + part + 1) * 128],
                                           m.xT[:, k, half * 4 * S:(half + 1) * 4 * S], start=k == 0, stop=k == KD - 1)
                    mm.then_inc(h_done, 1)
                hidden(0)
                hidden(1)
                pe.wait_ge(both_done, 4)
                flat = both[:].rearrange("p t e -> p (t e)")
                pe.matmul(m.bank[7][:S, 128:128 + B * E0], trib[:], flat, start=True, stop=True)
                pe.matmul(m.bank[6][:, 0:B * E0], onesb[:], flat, start=True, stop=True).then_inc(count_done, 1)
                for n in range(2, 2 * SM):
                    hidden(n)
                pe.wait_ge(act_done, 2 * SM)
                for t in range(B):
                    above(pe, y_copied, t - 1)
                    for k in range(SM):
                        mm = pe.matmul(m.bank[t % 2][:S, 0:D], act_s[:, k, t * S:(t + 1) * S], ws2[:, k, :],
                                       start=k == 0, stop=k == SM - 1)
                    mm.then_inc(y_done, 1)


def expert_phase(nc, d, m, tile_expert, xg_d, y_d):
    with ExitStack() as ctx:
        def sb(name, shape, dt=F32):
            return ctx.enter_context(nc.sbuf_tensor(name, shape, dt))

        def sem(name):
            return ctx.enter_context(nc.semaphore(name))

        w1, w2 = sb("w1", [128, 2, KD, 2 * HR]), sb("w2", [128, 2, HM, D])
        b1, b2 = sb("b1", [128, 2, 2 * HM]), sb("b2", [128, 2, D])
        xg, xgT = sb("xg_rows", [128, 2, D]), sb("xgT", [128, 2, KD, SLOT])
        gel, act_e = sb("gel_e", [128, 3, 2, SLOT]), sb("act_e", [128, 2, HM, SLOT])
        y = sb("y_rows", [128, 2, D])

        x_in, w1_in, b1_in, w2_in, b2_in, y_out = ([sem(f"{n}{u}") for u in range(2)] for n in
            ("ex_in", "ew1_in", "eb1_in", "ew2_in", "eb2_in", "ey_out"))
        turned, turned_copied, h_done, gelu_done, act_done, y_done, y_copied = (sem("e" + n) for n in
            ("turned", "turned_copied", "h_done", "gelu_done", "act_done", "y_done", "y_copied"))
        C = HM // 2

        def expert_tiles(eng, body):
            body(0, 0)
            body(1, 1)
            with eng.Fori(1, ET // 2) as i:
                body(2 * i, 0)
                body(2 * i + 1, 1)
            body(ET - 1, 0)

        def landed(j, u):
            return 8 * (j - u) + 16

        def row(ap, j):
            return ap[j:j + 1] if isinstance(j, int) else ap[bass.ds(j, 1)]

        with nc.Block() as block:
            @block.sync
            def _(sp):
                def load(j, u):
                    col = tile_expert[0:1, j:j + 1] if isinstance(j, int) else tile_expert[0:1, bass.ds(j, 1)]
                    e = sp.value_load(col, min_val=0, max_val=E0 - 1)
                    rows = xg_d[j * SLOT:(j + 1) * SLOT, :] if isinstance(j, int) else xg_d[bass.ds(j * SLOT, SLOT), :]
                    hold(sp, turned, j - 1, m.passed)
                    sp.dma_start(xg[:, u, :], rows).then_inc(x_in[u], 16)
                    hold(sp, h_done, C * (j - 1), m.passed)
                    sp.dma_start(w1[:, u, :, :], d["L0_ffn_We1"][bass.ds(e, 1)].rearrange("a (k p) n -> p (a k) n", p=128)).then_inc(w1_in[u], 16)
                    hold(sp, act_done, C * (j - 1), m.passed)
                    sp.dma_start(b1[:, u, :], d["be1T"][bass.ds(e, 1)].rearrange("a p n -> (a p) n")).then_inc(b1_in[u], 16)
                    hold(sp, y_copied, j - 1, m.passed)
                    sp.dma_start(w2[:, u, :, :], d["L0_ffn_We2"][bass.ds(e, 1)].rearrange("a (k p) n -> p (a k) n", p=128)).then_inc(w2_in[u], 16)
                    sp.dma_start(b2[:, u, :], d["L0_ffn_be2"][bass.ds(e, 1)].rearrange("a n -> (a n)").partition_broadcast(128)).then_inc(b2_in[u], 16)
                expert_tiles(sp, load)

            @block.gpsimd
            def _(pool):
                def store(j, u):
                    pool.wait_ge(y_copied, j + 1)
                    rows = y_d[j * SLOT:(j + 1) * SLOT, :] if isinstance(j, int) else y_d[bass.ds(j * SLOT, SLOT), :]
                    pool.dma_start(rows, y[:, u, :]).then_inc(y_out[u], 16)
                expert_tiles(pool, store)
                pool.wait_ge(y_out[0], landed(ET - 1, 0))
                pool.wait_ge(y_out[1], landed(ET - 2, 1))

            @block.scalar
            def _(act):
                def copy_turned_slots(j, u):
                    act.wait_ge(turned, j + 1)
                    act.activation(xgT[:, u, :, :], m.bank[3][:, 0:KD * SLOT].rearrange("p (k n) -> p k n", k=KD),
                                   ACT.Copy).then_inc(turned_copied, 1)

                def gelus(j, u):
                    act.wait_ge(b1_in[u], landed(j, u))
                    for c in range(C):
                        act.wait_ge(h_done, C * j + c + 1)
                        above(act, act_done, C * (j - 1) + c + 1)
                        for i in range(2):
                            ins = act.activation(gel[:, c, i, :], m.bank[c][:, (2 + i) * SLOT:(3 + i) * SLOT], ACT.Gelu,
                                                 bias=b1[:, u, HM + 2 * c + i:HM + 2 * c + i + 1])
                        ins.then_inc(gelu_done, 1)
                    if not known(j, ET - 1):
                        copy_turned_slots(j + 1, 1 - u)
                copy_turned_slots(0, 0)
                expert_tiles(act, gelus)

            @block.vector
            def _(dve):
                def copy_y(j, u):
                    dve.wait_ge(y_done, j + 1)
                    dve.wait_ge(b2_in[u], landed(j, u))
                    if not (isinstance(j, int) and j < 2):
                        dve.wait_ge(y_out[u], landed(j - 2, u))
                    dve.tensor_tensor(y[:, u, :], m.bank[4 + u][:, 0:D], b2[:, u, :], ALU.add).then_inc(y_copied, 1)

                def multiply(j, u):
                    dve.wait_ge(b1_in[u], landed(j, u))
                    for c in range(C):
                        dve.wait_ge(gelu_done, C * j + c + 1)
                        above(dve, y_done, j - 1)
                        for i in range(2):
                            ins = dve.scalar_tensor_tensor(out=act_e[:, u, 2 * c + i, :], in0=m.bank[c][:, i * SLOT:(i + 1) * SLOT],
                                                           scalar=b1[:, u, 2 * c + i:2 * c + i + 1], in1=gel[:, c, i, :],
                                                           op0=ALU.add, op1=ALU.mult)
                        ins.then_inc(act_done, 1)
                        if c == 0 and not known(j, 0):
                            copy_y(j - 1, 1 - u)
                expert_tiles(dve, multiply)
                copy_y(ET - 1, 0)

            @block.tensor
            def _(pe):
                def turn(j, u):
                    pe.wait_ge(x_in[u], landed(j, u))
                    above(pe, turned_copied, j)
                    for k in range(KD):
                        mm = pe.transpose(m.bank[3][:, k * SLOT:(k + 1) * SLOT], xg[:, u, k * 128:(k + 1) * 128], m.ident)
                    mm.then_inc(turned, 1)

                def hidden(j, u, c):
                    above(pe, act_done, C * (j - 1) + c + 1)
                    for i in range(4):
                        part = (i // 2) * HM + 2 * c + i % 2
                        for k in range(KD):
                            mm = pe.matmul(m.bank[c][:, i * SLOT:(i + 1) * SLOT], w1[:, u, k, part * 128:(part + 1) * 128],
                                           xgT[:, u, k, :], start=k == 0, stop=k == KD - 1)
                    mm.then_inc(h_done, 1)

                def output(j, u):
                    pe.wait_ge(act_done, C * (j + 1))
                    pe.wait_ge(w2_in[u], landed(j, u))
                    above(pe, y_copied, j - 1)
                    for k in range(HM):
                        mm = pe.matmul(m.bank[4 + u][:, 0:D], act_e[:, u, k, :], w2[:, u, k, :], start=k == 0, stop=k == HM - 1)
                    mm.then_inc(y_done, 1)

                def tile(j, u):
                    pe.wait_ge(turned_copied, j + 1)
                    pe.wait_ge(w1_in[u], landed(j, u))
                    hidden(j, u, 0)
                    if not known(j, 0):
                        output(j - 1, 1 - u)
                    for c in range(1, C):
                        hidden(j, u, c)
                    if not known(j, ET - 1):
                        turn(j + 1, 1 - u)
                turn(0, 0)
                expert_tiles(pe, tile)
                output(ET - 1, 0)


def combine_phase(nc, d, m, ys, wts, pos, y_d):
    with ExitStack() as ctx:
        yg = ctx.enter_context(nc.sbuf_tensor("yg", [S, 2, B, D], F32))
        got = [ctx.enter_context(nc.semaphore(f"got{t}")) for t in range(B)]
        added = ctx.enter_context(nc.semaphore("c_added"))
        with nc.Block() as block:
            @block.gpsimd
            def _(pool):
                for t in range(B):
                    for c in range(2):
                        pool.indirect_dma_start(out=yg[:, c, t, :], out_offset=None, in_=y_d,
                                                in_offset=bass.IndirectOffsetOnAxis(ap=pos[:, c, t:t + 1], axis=0)).then_inc(got[t], 16)

            @block.vector
            def _(dve):
                for t in range(B):
                    dve.wait_ge(got[t], 32)
                    dve.scalar_tensor_tensor(out=ys[:, t, :], in0=yg[:, 0, t, :], scalar=wts[:, 0, t:t + 1], in1=ys[:, t, :],
                                             op0=ALU.mult, op1=ALU.add).then_inc(added, 1)
                    dve.wait_ge(added, 3 * t + 1)
                    dve.scalar_tensor_tensor(out=ys[:, t, :], in0=yg[:, 1, t, :], scalar=wts[:, 1, t:t + 1], in1=ys[:, t, :],
                                             op0=ALU.mult, op1=ALU.add).then_inc(added, 1)
                    dve.wait_ge(added, 3 * t + 2)
                    dve.scalar_tensor_tensor(out=m.x[:, t, :], in0=ys[:, t, :], scalar=m.gates[:S, 2:3], in1=m.x[:, t, :],
                                             op0=ALU.mult, op1=ALU.add).then_inc(added, 1)


def gated_phase(nc, d, m):
    with ExitStack() as ctx:
        def sb(name, shape, dt=F32):
            return ctx.enter_context(nc.sbuf_tensor(name, shape, dt))

        def sem(name):
            return ctx.enter_context(nc.semaphore(name))

        EP = E1 // 2
        vg, vd = sb("vg", [128, KD, E1 * R1]), sb("vd", [128, EP, 2, D])
        we, wp = sb("we", [128, KD, E1 * D]), sb("wp", [128, KD, D])
        bb = sb("bb", [E1 + 1, D])
        xe = sb("xe", [128, EP, B * S])
        diff = sb("diff", [S, 2, 2, D])
        junk = sb("junk", [S, 2, D])
        r2, res = sb("r2", [S, B, E1]), sb("res", [S, B, E1])
        rmin, rsum, rinv = sb("rmin", [S, B]), sb("rsum", [S, B]), sb("rinv", [S, B])
        gap, ex, rw = sb("gap1", [S, B, E1]), sb("ex1", [S, B, E1]), sb("rw", [S, B, E1])
        top, topi, topf = sb("top1", [S, B, 8]), sb("topi1", [S, B, 8], U32), sb("topf1", [S, B, 2])
        hot = sb("hot1", [S, 2, B, E1])
        over, overb, onesb = sb("over1", [S, B, E1]), sb("overb", [S, B, E1], BF16), sb("ones1", [S, S], BF16)
        cnt, some, none = sb("cnt", [S, 1]), sb("some", [S, 1]), sb("none", [S, 1])
        mask, fw, sw, swz = sb("mask1", [S, B, E1]), sb("fw", [S, B, E1]), sb("sw", [S, B]), sb("swz", [S, B])
        w9, w9T = sb("w9", [S, B, E1 + 1]), sb("w9T", [E1 + 1, B, S])
        acc, res_out = sb("acc", [S, 2, D]), sb("res_out", [S, 2, D])

        w_in, vd_zero, vd_in = sem("gw_in"), sem("vd_zero"), sem("vd_in")
        row_stat, row_mv, row_dev, row_rstd, rows_done, turned, turned_copied = (sem("g" + n) for n in
            ("row_stat", "row_mv", "row_dev", "row_rstd", "rows_done", "turned", "turned_copied"))
        xe_done, xe_copied, proj_done, diff_done, sq_done = (sem(n) for n in
            ("xe_done", "xe_copied", "gproj_done", "diff_done", "sq_done"))
        gap_done, ex_done, over_done, cnt_done, w_done, wT_done, wT_copied = (sem(n) for n in
            ("ggap_done", "gex_done", "over_done", "cnt_done", "w_done", "wT_done", "wT_copied"))
        base_done, base_copied, e_done, e_added, tile_done = (sem(n) for n in
            ("base_done", "base_copied", "e_done", "e_added", "tile_done"))
        step, res_done = sem("gate_step"), sem("res_done")
        out_done = [sem("out_done0"), sem("out_done1")]

        with nc.Block() as block:
            @block.sync
            def _(sp):
                sp.dma_start(vg[:], d["VgT"].rearrange("(k p) n -> p k n", p=128)).then_inc(w_in, 16)
                sp.wait_ge(vd_zero, 1)
                for a in range(2):
                    sp.dma_start(vd[64 * a:64 * a + 64, :, a, :], d["VgR"].rearrange("(q a r) n -> a r q n", a=2, r=R1)[a]).then_inc(vd_in, 16)
                sp.dma_start(wp[:], d["WpT"].rearrange("(k p) n -> p k n", p=128)).then_inc(w_in, 16)
                sp.dma_start(we[:], d["WeT"].rearrange("(k p) n -> p k n", p=128)).then_inc(w_in, 16)
                sp.dma_start(bb[0:E1, :], d["L1_ffn_be"]).then_inc(w_in, 16)
                sp.dma_start(bb[E1:E1 + 1, :], d["L1_ffn_bp"].partition_broadcast(1)).then_inc(w_in, 16)
                for t in range(B):
                    sp.wait_ge(tile_done, t + 1)
                    sp.dma_start(d["out"][t], m.x[:, t, :]).then_inc(out_done[t % 2], 16)
                for u in range(2):
                    sp.wait_ge(out_done[u], 16 * B // 2)

            @block.gpsimd
            def _(pool):
                pool.memset(vd[:], 0.0).then_inc(vd_zero, 1)

            @block.scalar
            def _(act):
                deviations(act, m, row_mv, row_dev)
                copy_turned(act, m, m.bank[0:2], turned, turned_copied)
                for n in range(2 * EP):
                    act.wait_ge(xe_done, n + 1)
                    act.activation(xe[:, n % EP, (n // EP) * 4 * S:(n // EP + 1) * 4 * S], m.bank[2 + n % 2][:, 0:4 * S],
                                   ACT.Copy).then_inc(xe_copied, 1)
                for n in range(B * EP):
                    act.wait_ge(diff_done, n + 1)
                    for a in range(2):
                        ins = act.activation(junk[:, a, :], diff[:, n % 2, a, :], ACT.Square,
                                             accum_out=r2[:, n // EP, 2 * (n % EP) + a:2 * (n % EP) + a + 1])
                        ins.then_inc(sq_done, 1)
                        act.wait_ge(sq_done, 2 * n + a + 1)
                act.activation(res[:], r2[:], ACT.Sqrt).then_inc(res_done, 1)
                act.wait_ge(gap_done, 1)
                act.activation(ex[:], gap[:], ACT.Exp, scale=-1.0).then_inc(ex_done, 1)
                act.wait_ge(wT_done, 1)
                act.activation(w9T[:, 0:4, :], m.bank[0][:E1 + 1, 0:4 * S].rearrange("p (t n) -> p t n", t=4), ACT.Copy).then_inc(wT_copied, 1)
                act.activation(w9T[:, 4:8, :], m.bank[1][:E1 + 1, 0:4 * S].rearrange("p (t n) -> p t n", t=4), ACT.Copy).then_inc(wT_copied, 1)
                for t in range(B):
                    act.wait_ge(base_done, t + 1)
                    above(act, tile_done, t - 1)
                    act.activation(acc[:, t % 2, :], m.bank[2 + t % 2][:S, 0:D], ACT.Copy).then_inc(base_copied, 1)

            @block.vector
            def _(dve):
                count = [0]

                def then(ins):
                    ins.then_inc(step, 1)
                    count[0] += 1
                    dve.wait_ge(step, count[0])

                dve.memset(onesb[:], 1.0).then_inc(over_done, 1)
                dve.memset(w9[:], 1.0).then_inc(over_done, 1)
                normalise_rows(dve, m, row_stat, row_mv, row_dev, row_rstd, rows_done)
                dve.wait_ge(rows_done, B)
                for n in range(B * EP):
                    dve.wait_ge(proj_done, n + 1)
                    above(dve, sq_done, 2 * (n - 1))
                    dve.tensor_tensor(diff[:, n % 2, :, :], m.bank[4 + n % 4][:S, :].rearrange("p (a n) -> p a n", a=2),
                                      spread_over(m.xn[:, n // EP, :], 1, 2), ALU.subtract).then_inc(diff_done, 1)
                dve.wait_ge(res_done, 1)
                then(dve.tensor_reduce(rmin[:], res[:], AX.X, ALU.min))
                dve.tensor_tensor(gap[:], res[:], spread_over(rmin[:], 2, E1), ALU.subtract).then_inc(gap_done, 1)
                dve.wait_ge(ex_done, 1)
                then(dve.tensor_reduce(rsum[:], ex[:], AX.X, ALU.add))
                then(dve.reciprocal(rinv[:], rsum[:]))
                then(dve.tensor_tensor(rw[:], ex[:], spread_over(rinv[:], 2, E1), ALU.mult))
                then(dve.tensor_scalar(over[:], rw[:], 1.0 / E1, None, ALU.is_gt))
                dve.tensor_copy(overb[:], over[:]).then_inc(over_done, 1)
                for t in range(B):
                    ins = dve.max(top[:, t, :], rw[:, t, :])
                then(ins)
                for t in range(B):
                    ins = dve.max_index(topi[:, t, :], top[:, t, :], rw[:, t, :])
                then(ins)
                then(dve.tensor_copy(topf[:], topi[:, :, 0:2]))
                for c in range(2):
                    then(dve.tensor_tensor(hot[:, c, :, :], spread_over(m.const[:S, C_IOTA:C_IOTA + E1], 1, B),
                                           spread_over(topf[:, :, c], 2, E1), ALU.is_equal))
                dve.wait_ge(cnt_done, 1)
                then(dve.tensor_reduce(cnt[:], m.bank[2][:S, 0:B * E1], AX.X, ALU.max))
                then(dve.tensor_scalar(some[:], cnt[:], 0.0, None, ALU.is_gt))
                then(dve.tensor_scalar(none[:], cnt[:], 0.0, None, ALU.is_equal))
                then(dve.tensor_scalar(mask[:], over[:], some[:, 0:1], None, ALU.mult))
                then(dve.scalar_tensor_tensor(out=mask[:], in0=hot[:, 0, :, :], scalar=none[:, 0:1], in1=mask[:],
                                              op0=ALU.mult, op1=ALU.add))
                then(dve.tensor_tensor(fw[:], rw[:], mask[:], ALU.mult))
                then(dve.tensor_tensor(mask[:], hot[:, 0, :, :], hot[:, 1, :, :], ALU.add))
                then(dve.tensor_tensor(fw[:], fw[:], mask[:], ALU.mult))
                then(dve.tensor_reduce(sw[:], fw[:], AX.X, ALU.add))
                then(dve.tensor_scalar(swz[:], sw[:], 0.0, None, ALU.is_equal))
                then(dve.tensor_tensor(sw[:], sw[:], swz[:], ALU.add))
                then(dve.reciprocal(rinv[:], sw[:]))
                dve.tensor_tensor(w9[:, :, 0:E1], fw[:], spread_over(rinv[:], 2, E1), ALU.mult).then_inc(w_done, 1)
                dve.wait_ge(w_done, 1)
                n = 0
                for t in range(B):
                    dve.wait_ge(base_copied, t + 1)
                    for q in range(EP):
                        dve.wait_ge(e_done, EP * t + q + 1)
                        for a in range(2):
                            e = 2 * q + a
                            ins = dve.scalar_tensor_tensor(out=acc[:, t % 2, :], in0=m.bank[4 + q][:S, a * D:(a + 1) * D],
                                                           scalar=w9[:, t, e:e + 1], in1=acc[:, t % 2, :], op0=ALU.mult, op1=ALU.add)
                            ins.then_inc(e_added, 1)
                            n += 1
                            dve.wait_ge(e_added, n)
                    dve.scalar_tensor_tensor(out=m.x[:, t, :], in0=acc[:, t % 2, :], scalar=m.gates[:S, 3:4], in1=m.x[:, t, :],
                                             op0=ALU.mult, op1=ALU.add).then_inc(tile_done, 1)

            @block.tensor
            def _(pe):
                transpose_rows(pe, m, m.bank[0:2], rows_done, turned, turned_copied)
                pe.wait_ge(turned_copied, B)
                pe.wait_ge(w_in, 80)
                for n in range(2 * EP):
                    above(pe, xe_copied, n - 1)
                    for k in range(KD):
                        mm = pe.matmul(m.bank[2 + n % 2][:, 0:4 * S], vg[:, k, (n % EP) * 128:(n % EP + 1) * 128],
                                       m.xT[:, k, (n // EP) * 4 * S:(n // EP + 1) * 4 * S], start=k == 0, stop=k == KD - 1)
                    mm.then_inc(xe_done, 1)
                pe.wait_ge(vd_in, 32)
                pe.wait_ge(xe_copied, 2 * EP)
                for n in range(B * EP):
                    above(pe, diff_done, n - 3)
                    pe.matmul(m.bank[4 + n % 4][:S, :], xe[:, n % EP, (n // EP) * S:(n // EP + 1) * S], vd[:, n % EP, :, :],
                              start=True, stop=True).then_inc(proj_done, 1)
                pe.wait_ge(over_done, 3)
                pe.matmul(m.bank[2][:S, 0:B * E1], onesb[:], overb[:].rearrange("p t e -> p (t e)"), start=True, stop=True).then_inc(cnt_done, 1)
                pe.wait_ge(w_done, 1)
                for t in range(B):
                    mm = pe.transpose(m.bank[t // 4][:E1 + 1, (t % 4) * S:(t % 4 + 1) * S], w9[:, t, :], m.ident[:S, :S])
                mm.then_inc(wT_done, 1)
                pe.wait_ge(wT_copied, 2)
                for t in range(B):
                    above(pe, base_copied, t - 1)
                    for k in range(KD):
                        pe.matmul(m.bank[2 + t % 2][:S, 0:D], m.xT[:, k, t * S:(t + 1) * S], wp[:, k, :], start=k == 0, stop=False)
                    pe.matmul(m.bank[2 + t % 2][:S, 0:D], w9T[:, t, :], bb[:], start=False, stop=True).then_inc(base_done, 1)
                    for q in range(EP):
                        above(pe, e_added, 2 * (EP * (t - 1) + q + 1))
                        for k in range(KD):
                            mm = pe.matmul(m.bank[4 + q][:S, :], m.xT[:, k, t * S:(t + 1) * S], we[:, k, q * 2 * D:(q + 1) * 2 * D],
                                           start=k == 0, stop=k == KD - 1)
                        mm.then_inc(e_done, 1)


def kernel(x, ctx_1024, mask_Bx1xSxS2_ik1, mask_BxSxS2_bk1, g_xattn, g_ffn,
           L0_xattn_Wq, L0_xattn_bq, L0_xattn_Wk, L0_xattn_bk, L0_xattn_Wv, L0_xattn_bv, L0_xattn_Wo,
           L0_ffn_Ws1, L0_ffn_bs1, L0_ffn_Ws2, L0_ffn_bs2, L0_ffn_We1, L0_ffn_be1, L0_ffn_We2, L0_ffn_be2,
           L0_ffn_Wr, L0_ffn_br, L1_xattn_Wq, L1_xattn_Wk, L1_xattn_Wv, L1_xattn_Wo,
           L1_ffn_Wp, L1_ffn_bp, L1_ffn_We, L1_ffn_be, L1_ffn_Vg):
    import numpy as np
    import concourse.bacc as bacc
    from concourse.bass_utils import run_bass_kernel_spmd

    a = np.asarray
    arrays = {
        "x": a(x),
        "ctxT": a(ctx_1024).transpose(0, 2, 1),
        "mask0": a(mask_Bx1xSxS2_ik1)[:, 0].transpose(0, 2, 1),
        "mask1": a(mask_BxSxS2_bk1),
        "g_xattn": a(g_xattn),
        "g_ffn": a(g_ffn),
        "L0_xattn_WqT": a(L0_xattn_Wq).T, "L0_xattn_WkT": a(L0_xattn_Wk).T,
        "L0_xattn_WvT": a(L0_xattn_Wv).T, "L0_xattn_WoT": a(L0_xattn_Wo).T,
        "bqT": a(L0_xattn_bq).reshape(KD, 128).T, "bkT": a(L0_xattn_bk).reshape(KD, 128).T, "L0_xattn_bv": a(L0_xattn_bv),
        "L1_xattn_WqT": a(L1_xattn_Wq).T, "L1_xattn_WkT": a(L1_xattn_Wk).T,
        "L1_xattn_WvT": a(L1_xattn_Wv).T, "L1_xattn_WoT": a(L1_xattn_Wo).T,
        "L0_ffn_Ws1": a(L0_ffn_Ws1), "bs1T": a(L0_ffn_bs1).reshape(2 * SM, 128).T, "L0_ffn_Ws2": a(L0_ffn_Ws2), "L0_ffn_bs2": a(L0_ffn_bs2),
        "L0_ffn_We1": a(L0_ffn_We1), "L0_ffn_We2": a(L0_ffn_We2), "L0_ffn_be2": a(L0_ffn_be2),
        "be1T": a(L0_ffn_be1).reshape(E0, 2 * HM, 128).transpose(0, 2, 1),
        "L0_ffn_Wr": a(L0_ffn_Wr), "L0_ffn_br": a(L0_ffn_br),
        "WpT": a(L1_ffn_Wp).T, "L1_ffn_bp": a(L1_ffn_bp), "L1_ffn_be": a(L1_ffn_be),
        "WeT": a(L1_ffn_We).transpose(2, 0, 1).reshape(D, E1 * D),
        "VgT": a(L1_ffn_Vg).transpose(1, 0, 2).reshape(D, E1 * R1),
        "VgR": a(L1_ffn_Vg).transpose(0, 2, 1).reshape(E1 * R1, D),
        "const": constants(),
    }
    arrays = {"in_" + k: np.ascontiguousarray(v) for k, v in arrays.items()}
    nc = bacc.Bacc("TRN2", target_bir_lowering=False, num_devices=1)
    d = {k[3:]: nc.dram_tensor(k, v.shape, mybir.dt.from_np(v.dtype), kind="ExternalInput").ap() for k, v in arrays.items()}
    d["out"] = nc.dram_tensor("out", (B, S, D), F32, kind="ExternalOutput").ap()
    build(nc, d)
    r = run_bass_kernel_spmd(nc, [arrays], core_ids=[0])
    return r.results[0]["out"]
```

```python
from contextlib import ExitStack

import concourse.bass as bass
from concourse import mybir

F32 = mybir.dt.float32
BF16 = mybir.dt.bfloat16
I32 = mybir.dt.int32
U32 = mybir.dt.uint32
U8 = mybir.dt.uint8
ALU = mybir.AluOpType
ACT = mybir.ActivationFunctionType
AX = mybir.AxisListType

B = 8
S = 112
D = 256
KD = D // 128
KEYS = 375
KT = 3
KW = KEYS // KT
H = 16
DH = D // H
HG = H // KD
G = 4
SCALE = float(DH) ** -0.5
EPS = 1e-5
NEG1 = -1e30
NEG_MAX = -3e38
E0 = 12
HR = 768
HM = HR // 128
HS = 512
SM = HS // 128
TAU = 1.5
SLOT = 128
ET = 2 * B * S // SLOT + E0
XROWS = ET + 2
ZR = 4
THR = -(-B * S // SLOT)
E1 = 8
R1 = 64

C_ID = 0
C_TRI = C_ID + 128
C_HEAD = C_TRI + S
C_SPREAD = C_HEAD + HG
C_IOTA = C_SPREAD + G * 128
C_THR = C_IOTA + E0
C_LOW = C_THR + THR
C_EPS = C_LOW + E0 * E0
C_END = C_EPS + 1

LATER = 13 * 16


def constants():
    import numpy as np
    c = np.zeros((128, C_END), np.float32)
    c[:, C_ID:C_ID + 128] = np.eye(128)
    c[:S, C_TRI:C_TRI + S] = np.triu(np.ones((S, S)), 1)
    for h in range(HG):
        c[h * DH:(h + 1) * DH, C_HEAD + h] = 1
    for g in range(G):
        for j in range(4):
            c[4 * g + j, C_SPREAD + g * 128 + 32 * j:C_SPREAD + g * 128 + 32 * j + 32] = 1
    c[:, C_IOTA:C_IOTA + E0] = np.arange(E0)
    c[:, C_THR:C_THR + THR] = np.arange(THR) * SLOT
    c[:, C_LOW:C_LOW + E0 * E0] = np.tril(np.ones((E0, E0)), -1).reshape(-1)
    c[:, C_EPS] = EPS
    return c


def above(eng, sem, value):
    if not isinstance(value, int) or value > 0:
        eng.wait_ge(sem, value)


def hold(eng, sem, value, passed):
    if not isinstance(value, int) or value > 0:
        eng.wait_ge(sem, value)
        eng.sem_inc(passed, 1)


def pairs(eng, body, n=B // 2):
    for u in range(2):
        body(u, u)
    with eng.Fori(1, n - 1) as i:
        for u in range(2):
            body(2 * i + u, u)
    for u in range(2):
        body(2 * (n - 1) + u, u)


def known(b, value):
    return isinstance(b, int) and b == value


def at(ap, b):
    return ap[:, b:b + 1] if isinstance(b, int) else ap[:, bass.ds(b, 1)]


def spread_over(ap, axis, n):
    a = ap.unsqueeze(axis)
    shape = list(a.shape)
    shape[axis] = n
    return a.broadcast_to(shape)


class Memory:

    def __init__(self):
        self.live = None
        self.spent = None

    def open_phase(self, nc):
        self.spent, self.live = self.live, (ExitStack(), [])
        stack, handles = self.live

        def sem(name):
            handles.append(stack.enter_context(nc.semaphore(name)))
            return handles[-1]
        return sem

    def clear_spent(self, pool):
        if self.spent is not None:
            for s in self.spent[1]:
                pool.sem_clear(s)

    def close_phase(self):
        if self.spent is not None:
            self.spent[0].close()


def build(nc, d, phases=6):
    with ExitStack() as ctx:
        def sb(name, shape, dt=F32, stack=ctx):
            return stack.enter_context(nc.sbuf_tensor(name, shape, dt))

        m = Memory()
        m.x = sb("x", [S, B, D])
        m.xn = sb("xn", [S, B, D])
        m.xT = sb("xT", [128, KD, B * S])
        m.qT = sb("qT", [128, KD, B * S])
        m.stat = sb("stat", [S, B, 6])
        m.mv = sb("mv", [S, B, 2])
        m.dev = sb("dev", [S, B])
        m.rstd = sb("rstd", [S, B])
        m.const = sb("const", [128, C_END])
        m.gates = sb("gates", [128, 4])
        m.graw = sb("graw", [128, 4])
        m.ws1, m.ws2, m.wr = sb("ws1", [128, KD, 2 * HS]), sb("ws2", [128, SM, D]), sb("wr", [128, KD, E0])
        m.bs1, m.bs2, m.br = sb("bs1", [128, 2 * SM]), sb("bs2", [S, D]), sb("br", [S, E0])
        m.wq1, m.wk1, m.wv1 = sb("wq1", [128, KD, D]), sb("wk1", [128, KD, D]), sb("wv1", [128, KD, D])
        m.wo1 = sb("wo1", [128, G, D])
        m.bank = [ctx.enter_context(nc.psum_tensor(f"bank{i}", [128, 512], F32)) for i in range(8)]
        m.passed = ctx.enter_context(nc.semaphore("passed"))
        m.later_in = ctx.enter_context(nc.semaphore("later_in"))
        m.expert_in = [[ctx.enter_context(nc.semaphore(f"{n}{u}_in")) for u in range(2)] for n in ("w1_", "b1_", "w2_", "b2_")]
        m.ident = m.const[:, C_ID:C_ID + 128]

        silu_attention_phase(nc, d, m)
        if phases > 1:
            with ExitStack() as kv:
                m.ctxT = sb("ctxT", [128, 2, KD, KEYS], F32, kv)
                m.kT = sb("kT", [128, KD, B, KEYS], F32, kv)
                m.v = sb("v", [KW, B, KT, D], F32, kv)
                m.ys = sb("ys", [S, B, D], F32, kv)
                m.wts = sb("wts", [S, 2, B], F32, kv)
                m.pos = sb("pos", [S, 2, B], U32, kv)
                m.first_tile = sb("first_tile", [1, E0 + 2], I32, kv)
                m.xg_d = nc.dram_tensor("xg", [XROWS * SLOT, D], F32, kind="Internal").ap()
                m.y_d = nc.dram_tensor("y", [(ET + 1) * SLOT, D], F32, kind="Internal").ap()
                with ExitStack() as ex:
                    m.w1, m.w2 = sb("w1", [128, 2, KD, 2 * HR], F32, ex), sb("w2", [128, 2, HM, D], F32, ex)
                    m.b1, m.b2 = sb("b1", [128, 2, 2 * HM], F32, ex), sb("b2", [128, 2, D], F32, ex)
                    route_phase(nc, d, m)
                    expert_phase(nc, d, m)
                soft_attention_phase(nc, d, m)
        if phases > 4:
            gated_phase(nc, d, m)
        else:
            with nc.semaphore("x_out") as x_out, nc.Block() as block:
                @block.sync
                def _(sp):
                    sp.dma_start(d["out"].rearrange("b s n -> s b n"), m.x[:]).then_inc(x_out, 16)
                    sp.wait_ge(x_out, 16)
        m.close_phase()
        m.live[0].close()


def load_expert(sp, d, m, e, u):
    def of(ap):
        return ap[e:e + 1] if isinstance(e, int) else ap[bass.ds(e, 1)]
    w1_in, b1_in, w2_in, b2_in = m.expert_in
    sp.dma_start(m.w1[:, u, :, :], of(d["L0_ffn_We1"]).rearrange("a (k p) n -> p (a k) n", p=128)).then_inc(w1_in[u], 16)
    sp.dma_start(m.b1[:, u, :], of(d["be1T"]).rearrange("a p n -> (a p) n")).then_inc(b1_in[u], 16)
    sp.dma_start(m.w2[:, u, :, :], of(d["L0_ffn_We2"]).rearrange("a (k p) n -> p (a k) n", p=128)).then_inc(w2_in[u], 16)
    sp.dma_start(m.b2[:, u, :], of(d["L0_ffn_be2"]).rearrange("a n -> (a n)").partition_broadcast(128)).then_inc(b2_in[u], 16)


class ContextProjection:

    def __init__(self, m, d, first, n, banks, ctx_in, kv_done, kv_copied):
        self.m, self.d, self.first, self.n, self.banks = m, d, first, n, banks
        self.ctx_in, self.kv_done, self.kv_copied = ctx_in, kv_done, kv_copied

    def rounds(self, eng, body):
        body(0, 0)
        body(1, 1)
        if self.n > 2:
            with eng.Fori(1, self.n // 2) as i:
                body(2 * i, 0)
                body(2 * i + 1, 1)

    def load(self, sp):
        def one(i, u):
            hold(sp, self.kv_done, 4 * (i - 1), self.m.passed)
            b = self.first + i
            src = self.d["ctxT"][b:b + 1] if isinstance(b, int) else self.d["ctxT"][bass.ds(b, 1)]
            sp.dma_start(self.m.ctxT[:, u, :, :], src.rearrange("a (k p) n -> p (a k) n", p=128)).then_inc(self.ctx_in[u], 16)
        self.rounds(sp, one)

    def project(self, pe):
        m = self.m

        def one(i, u):
            pe.wait_ge(self.ctx_in[u], 8 * (i - u) + 16)
            for part in range(4):
                above(pe, self.kv_copied, 4 * (i - 1) + part + 1)
                bank = self.banks[part]
                if part < 2:
                    for t in ((0, 1) if part == 0 else (2,)):
                        for k in range(KD):
                            mm = pe.matmul(bank[:KW, (t % 2) * D:(t % 2 + 1) * D], m.ctxT[:, u, k, t * KW:(t + 1) * KW],
                                           m.wv1[:, k, :], start=k == 0, stop=k == KD - 1)
                else:
                    for k in range(KD):
                        mm = pe.matmul(bank[:, 0:KEYS], m.wk1[:, k, (part - 2) * 128:(part - 1) * 128], m.ctxT[:, u, k, :],
                                       start=k == 0, stop=k == KD - 1)
                mm.then_inc(self.kv_done, 1)
        self.rounds(pe, one)

    def copy(self, act, i):
        m, b = self.m, self.first + i
        vb = m.v[:, b:b + 1] if isinstance(b, int) else m.v[:, bass.ds(b, 1)]
        kb = [m.kT[:, k, b:b + 1, :] if isinstance(b, int) else m.kT[:, k, bass.ds(b, 1), :] for k in range(KD)]
        for part in range(4):
            act.wait_ge(self.kv_done, 4 * i + part + 1)
            if part == 0:
                dst, src = vb[:, :, 0:2, :].rearrange("p a t n -> p (a t) n"), self.banks[0][:KW, :].rearrange("p (t n) -> p t n", t=2)
            elif part == 1:
                dst, src = vb[:, :, 2, :].rearrange("p a n -> p (a n)"), self.banks[1][:KW, 0:D]
            else:
                dst, src = kb[part - 2].rearrange("p a n -> p (a n)"), self.banks[part][:, 0:KEYS]
            act.activation(dst, src, ACT.Copy).then_inc(self.kv_copied, 1)

def normalise_rows(dve, m, row_stat, row_mv, row_dev, row_rstd, rows_done, x_loaded=None):
    def row(ap, t):
        return ap[:, bass.ds(t, 1)].rearrange("p a n -> p (a n)")
    if x_loaded is not None:
        dve.wait_ge(x_loaded, 16)
    for t in range(B):
        dve.bn_stats(m.stat[:, t, :], m.x[:, t, :]).then_inc(row_stat, 1)
    for t in range(B):
        dve.wait_ge(row_stat, t + 1)
        dve.bn_aggr(m.mv[:, t, :], m.stat[:, t, :]).then_inc(row_mv, 1)
    dve.wait_ge(row_dev, 1)
    dve.reciprocal(m.rstd[:], m.dev[:]).then_inc(row_rstd, 1)
    dve.wait_ge(row_rstd, 1)
    with dve.Fori(0, B) as t:
        dve.tensor_scalar(row(m.xn, t), row(m.x, t), m.mv[:, bass.ds(t, 1), 0], m.rstd[:, bass.ds(t, 1)],
                          ALU.subtract, ALU.mult).then_inc(rows_done, 1)


def deviations(act, m, row_mv, row_dev):
    act.wait_ge(row_mv, B)
    act.activation(m.dev[:], m.mv[:, :, 1], ACT.Sqrt, bias=m.const[:S, C_EPS:C_EPS + 1]).then_inc(row_dev, 1)


def transpose_rows(pe, m, banks, rows_done, turned, turned_copied):
    for t in range(B):
        pe.wait_ge(rows_done, t + 1)
        above(pe, turned_copied, t - 1)
        for k in range(KD):
            mm = pe.transpose(banks[t % 2][:, k * S:(k + 1) * S], m.xn[:, t, k * 128:(k + 1) * 128], m.ident[:S, :S])
        mm.then_inc(turned, 1)


def copy_turned(act, m, banks, turned, turned_copied):
    for t in range(B):
        act.wait_ge(turned, t + 1)
        act.activation(m.xT[:, :, t * S:(t + 1) * S], banks[t % 2][:, 0:KD * S].rearrange("p (k n) -> p k n", k=KD),
                       ACT.Copy).then_inc(turned_copied, 1)


def silu_attention_phase(nc, d, m):
    sem = m.open_phase(nc)
    with ExitStack() as ctx:
        def sb(name, shape, dt=F32):
            return ctx.enter_context(nc.sbuf_tensor(name, shape, dt))

        wq, wk, wv = sb("wq", [128, KD, D]), sb("wk", [128, KD, D]), sb("wv", [128, KD, D])
        wo = sb("wo", [128, G, D])
        bqk = sb("bqk", [128, 2, KD])
        bv = sb("bv", [KW, D])
        ctxT = sb("ctxT0", [128, 2, KD, KEYS])
        kT = sb("kT0", [128, 2, KD, KEYS])
        v = sb("v0", [KW, 2, KT, D])
        qd = sb("qd0", [128, 2, KD, HG, S])
        oT = sb("oT0", [128, 2, G, S])
        maskr = sb("maskr0", [KW, 2, KT, S], I32)
        keep = sb("keep0", [KW, 2, KT, S])
        AR = 6
        attn = sb("attn", [KW, AR, 4, S])
        C = G * KT

        wv_in, wk_in, wq_in, bqk_in, bv_in, wo_zero, wo_in = (sem(n) for n in
            ("wv_in", "wk_in", "wq_in", "bqk_in", "bv_in", "wo_zero", "wo_in"))
        x_in, const_in, g_in, gates_done, rows_zero = (sem(n) for n in ("x_in", "const_in", "g_in", "gates_done", "rows_zero"))
        ctx_in = [sem("ctx_in0"), sem("ctx_in1")]
        mask_in = [sem("mask_in0"), sem("mask_in1")]
        row_stat, row_mv, row_dev, row_rstd, rows_done, turned, turned_copied = (sem(n) for n in
            ("row_stat", "row_mv", "row_dev", "row_rstd", "rows_done", "turned", "turned_copied"))
        q_done, q_copied, qd_done = sem("q_done"), sem("q_copied"), sem("qd_done")
        v_done, v_copied, k_done, k_copied = (sem(n) for n in ("v_done", "v_copied", "k_done", "k_copied"))
        keep_done, score_done, silu_done, attn_done, pv_done = (sem(n) for n in
            ("keep_done", "score_done", "silu_done", "attn_done", "pv_done"))
        o_copied, proj_done, x_done = sem("o_copied"), sem("proj_done"), sem("x_done")

        with nc.Block() as block:
            @block.sync
            def _(sp):
                sp.dma_start(wv[:], d["L0_xattn_WvT"].rearrange("(k p) n -> p k n", p=128)).then_inc(wv_in, 16)

                def context(b, u):
                    hold(sp, k_done, KD * (b - 1), m.passed)
                    cs = d["ctxT"][b:b + 1] if isinstance(b, int) else d["ctxT"][bass.ds(b, 1)]
                    sp.dma_start(ctxT[:, u, :, :], cs.rearrange("a (k p) n -> p (a k) n", p=128)).then_inc(ctx_in[u], 16)
                    hold(sp, keep_done, b - 1, m.passed)
                    ms = d["mask0"][b:b + 1] if isinstance(b, int) else d["mask0"][bass.ds(b, 1)]
                    sp.dma_start(maskr[:, u, :, :], ms.rearrange("a (t p) q -> p (a t) q", p=KW)).then_inc(mask_in[u], 16)
                pairs(sp, context)

            @block.gpsimd
            def _(pool):
                pool.memset(wo[:], 0.0).then_inc(wo_zero, 1)
                pool.memset(m.wo1[:], 0.0).then_inc(wo_zero, 1)
                pool.wait_ge(wo_zero, 2)
                for j in range(4):
                    src = d["L0_xattn_WoT"].rearrange("(g j r) n -> j r g n", j=4, r=DH)[j]
                    pool.dma_start(wo[32 * j:32 * j + DH, :, :], src).then_inc(wo_in, 16)

                def spread_queries(b, u):
                    for k in range(KD):
                        above(pool, score_done, C * (b - 1))
                        q = m.qT[:, k, b * S:(b + 1) * S] if isinstance(b, int) else m.qT[:, k, bass.ds(b * S, S)]
                        pool.tensor_tensor(qd[:, u, k, :, :], spread_over(q, 1, HG),
                                           spread_over(m.const[:, C_HEAD:C_HEAD + HG], 2, S), ALU.mult).then_inc(qd_done, 1)
                    if known(b, 1):
                        load_later_weights()

                def load_later_weights():
                    for dst, src in ((m.wk1, "L1_xattn_WkT"), (m.wv1, "L1_xattn_WvT"), (m.wq1, "L1_xattn_WqT"),
                                     (m.wr, "L0_ffn_Wr"), (m.ws1, "L0_ffn_Ws1"), (m.ws2, "L0_ffn_Ws2")):
                        pool.dma_start(dst[:], d[src].rearrange("(k p) n -> p k n", p=128)).then_inc(m.later_in, 16)
                    pool.dma_start(m.br[:], d["L0_ffn_br"].partition_broadcast(S)).then_inc(m.later_in, 16)
                    pool.dma_start(m.bs2[:], d["L0_ffn_bs2"].partition_broadcast(S)).then_inc(m.later_in, 16)
                    pool.dma_start(m.bs1[:], d["bs1T"]).then_inc(m.later_in, 16)
                    for j in range(4):
                        src = d["L1_xattn_WoT"].rearrange("(g j r) n -> j r g n", j=4, r=DH)[j]
                        pool.dma_start(m.wo1[32 * j:32 * j + DH, :, :], src).then_inc(m.later_in, 16)
                pool.wait_ge(q_copied, 2 * KD)
                pool.wait_ge(const_in, 16)
                pairs(pool, spread_queries)
                pool.wait_ge(m.later_in, LATER)

            @block.scalar
            def _(act):
                act.dma_start(m.x[:], d["x"].rearrange("b s n -> s b n")).then_inc(x_in, 16)
                act.dma_start(m.const[:], d["const"]).then_inc(const_in, 16)
                act.dma_start(wk[:], d["L0_xattn_WkT"].rearrange("(k p) n -> p k n", p=128)).then_inc(wk_in, 16)
                act.dma_start(bqk[:, 0, :], d["bqT"]).then_inc(bqk_in, 16)
                act.dma_start(bqk[:, 1, :], d["bkT"]).then_inc(bqk_in, 16)
                act.dma_start(bv[:], d["L0_xattn_bv"].partition_broadcast(KW)).then_inc(bv_in, 16)
                act.dma_start(wq[:], d["L0_xattn_WqT"].rearrange("(k p) n -> p k n", p=128)).then_inc(wq_in, 16)
                act.dma_start(m.graw[:, 0:2], d["g_xattn"].partition_broadcast(128)).then_inc(g_in, 16)
                act.dma_start(m.graw[:, 2:4], d["g_ffn"].partition_broadcast(128)).then_inc(g_in, 16)
                act.wait_ge(const_in, 16)
                deviations(act, m, row_mv, row_dev)
                act.wait_ge(bqk_in, 32)

                def copy_keys(b, u):
                    for k in range(KD):
                        act.wait_ge(k_done, KD * b + k + 1)
                        act.activation(kT[:, u, k, :], m.bank[3 + k][:, 0:KEYS], ACT.Identity, bias=bqk[:, 1, k:k + 1]).then_inc(k_copied, 1)

                copy_turned(act, m, m.bank[0:2], turned, turned_copied)
                copy_keys(0, 0)
                for n in range(2 * KD):
                    act.wait_ge(q_done, n + 1)
                    act.activation(m.qT[:, n % KD, (n // KD) * 4 * S:(n // KD + 1) * 4 * S], m.bank[n % 2][:, 0:4 * S],
                                   ACT.Identity, bias=bqk[:, 0, n % KD:n % KD + 1]).then_inc(q_copied, 1)
                act.wait_ge(g_in, 32)
                act.activation(m.gates[:], m.graw[:], ACT.Tanh).then_inc(gates_done, 1)

                def silu_batch(b, u):
                    for c in range(C):
                        act.wait_ge(score_done, C * b + c + 1)
                        above(act, pv_done, G * b + c // KT - 1)
                        act.activation(attn[:, c % AR, :, :], m.bank[c % 3][:KW, 0:4 * S].rearrange("p (j n) -> p j n", j=4),
                                       ACT.Silu, scale=SCALE).then_inc(silu_done, 1)
                    if not known(b, B - 1):
                        copy_keys(b + 1, 1 - u)
                pairs(act, silu_batch)

            @block.vector
            def _(dve):
                normalise_rows(dve, m, row_stat, row_mv, row_dev, row_rstd, rows_done, x_in)
                for i in (5, 6):
                    dve.memset(m.bank[i][:], 0.0).then_inc(rows_zero, 1)

                def turn_mask(b, u):
                    dve.wait_ge(mask_in[u], 8 * (b - u) + 16)
                    dve.tensor_scalar(keep[:, u, :, :], maskr[:, u, :, :], 0.0, None, ALU.not_equal).then_inc(keep_done, 1)

                def copy_values(b, u):
                    for t in range(KT):
                        dve.wait_ge(v_done, 2 * b + t // 2 + 1)
                        ins = dve.tensor_tensor(v[:, u, t, :], m.bank[3 + t // 2][:KW, (t % 2) * D:(t % 2 + 1) * D], bv[:], ALU.add)
                        if t > 0:
                            ins.then_inc(v_copied, 1)

                def mask_chunks(b, u, g):
                    for t in range(KT):
                        slot = attn[:, (g * KT + t) % AR, :, :]
                        dve.wait_ge(silu_done, C * b + g * KT + t + 1)
                        dve.tensor_tensor(slot, slot, spread_over(keep[:, u, t, :], 1, 4), ALU.mult).then_inc(attn_done, 1)

                dve.wait_ge(bv_in, 16)
                copy_values(0, 0)
                turn_mask(0, 0)
                dve.wait_ge(gates_done, 1)

                def batch(b, u):
                    dve.wait_ge(keep_done, b + 1)
                    for g in range(G - 1):
                        mask_chunks(b, u, g)
                    if not known(b, B - 1):
                        turn_mask(b + 1, 1 - u)
                    mask_chunks(b, u, G - 1)
                    if not known(b, B - 1):
                        copy_values(b + 1, 1 - u)
                    dve.wait_ge(pv_done, G * (b + 1))
                    dve.tensor_copy(oT[:, u, :, :], m.bank[5 + u][:, 0:G * S].rearrange("p (g n) -> p g n", g=G)).then_inc(o_copied, 1)
                    dve.wait_ge(proj_done, b + 1)
                    xb = at(m.x, b).rearrange("p a n -> p (a n)")
                    dve.scalar_tensor_tensor(out=xb, in0=m.bank[7][:S, 0:D], scalar=m.gates[:S, 0:1], in1=xb,
                                             op0=ALU.mult, op1=ALU.add).then_inc(x_done, 1)
                pairs(dve, batch)

            @block.tensor
            def _(pe):
                def project_values(b, u):
                    pe.wait_ge(ctx_in[u], 8 * (b - u) + 16)
                    for t in range(KT):
                        if t != 1:
                            above(pe, k_copied, KD * (b - 1) + t // 2 + 1)
                        for k in range(KD):
                            mm = pe.matmul(m.bank[3 + t // 2][:KW, (t % 2) * D:(t % 2 + 1) * D], ctxT[:, u, k, t * KW:(t + 1) * KW],
                                           wv[:, k, :], start=k == 0, stop=k == KD - 1)
                        if t > 0:
                            mm.then_inc(v_done, 1)

                def project_keys(b, u):
                    for half in range(KD):
                        pe.wait_ge(v_copied, 2 * b + half + 1)
                        for k in range(KD):
                            mm = pe.matmul(m.bank[3 + half][:, 0:KEYS], wk[:, k, half * 128:(half + 1) * 128], ctxT[:, u, k, :],
                                           start=k == 0, stop=k == KD - 1)
                        mm.then_inc(k_done, 1)

                pe.wait_ge(wv_in, 16)
                project_values(0, 0)
                pe.wait_ge(const_in, 16)
                transpose_rows(pe, m, m.bank[0:2], rows_done, turned, turned_copied)
                pe.wait_ge(wk_in, 16)
                project_keys(0, 0)
                pe.wait_ge(wq_in, 16)
                pe.wait_ge(turned_copied, B)
                for n in range(2 * KD):
                    above(pe, q_copied, n - 1)
                    for k in range(KD):
                        mm = pe.matmul(m.bank[n % 2][:, 0:4 * S], wq[:, k, (n % KD) * 128:(n % KD + 1) * 128],
                                       m.xT[:, k, (n // KD) * 4 * S:(n // KD + 1) * 4 * S], start=k == 0, stop=k == KD - 1)
                    mm.then_inc(q_done, 1)
                pe.wait_ge(q_copied, 2 * KD)
                pe.wait_ge(wo_in, 64)
                pe.wait_ge(rows_zero, 2)

                def scores(b, u, g):
                    if g == 0:
                        pe.wait_ge(k_copied, KD * (b + 1))
                        pe.wait_ge(qd_done, KD * (b + 1))
                    for t in range(KT):
                        c = g * KT + t
                        above(pe, silu_done, C * b + c - 2)
                        pe.matmul(m.bank[c % 3][:KW, 0:4 * S], kT[:, u, g // 2, t * KW:(t + 1) * KW],
                                  qd[:, u, g // 2, 4 * (g % 2):4 * (g % 2) + 4, :], start=True, stop=True).then_inc(score_done, 1)

                def values(b, u, g):
                    if g == 0:
                        pe.wait_ge(v_copied, 2 * (b + 1))
                        above(pe, o_copied, b - 1)
                    pe.wait_ge(attn_done, C * b + (g + 1) * KT)
                    for t in range(KT):
                        for j in range(4):
                            mm = pe.matmul(m.bank[5 + u][32 * j:32 * j + DH, g * S:(g + 1) * S],
                                           v[:, u, t, (4 * g + j) * DH:(4 * g + j + 1) * DH], attn[:, (g * KT + t) % AR, j, :],
                                           start=t == 0, stop=t == KT - 1, tile_position=(0, 32 * j))
                    mm.then_inc(pv_done, 1)

                def batch(b, u):
                    scores(b, u, 0)
                    for g in range(1, G):
                        scores(b, u, g)
                        values(b, u, g - 1)
                    more = not known(b, B - 1)
                    if more:
                        project_values(b + 1, 1 - u)
                    values(b, u, G - 1)
                    if more:
                        project_keys(b + 1, 1 - u)
                    pe.wait_ge(o_copied, b + 1)
                    above(pe, x_done, b)
                    for g in range(G):
                        mm = pe.matmul(m.bank[7][:S, 0:D], oT[:, u, g, :], wo[:, g, :], start=g == 0, stop=g == G - 1)
                    mm.then_inc(proj_done, 1)
                pairs(pe, batch)
    m.close_phase()


def route_phase(nc, d, m):
    sem = m.open_phase(nc)
    wr, br, ws1, bs1, ws2, bs2, ys, wts, pos, xg_d = m.wr, m.br, m.ws1, m.bs1, m.ws2, m.bs2, m.ys, m.wts, m.pos, m.xg_d
    with ExitStack() as ctx:
        def sb(name, shape, dt=F32):
            return ctx.enter_context(nc.sbuf_tensor(name, shape, dt))

        zeros = sb("zeros", [SLOT, ZR * D])
        gel = sb("gel", [128, 2, 4 * S])
        act_s = sb("act_s", [128, SM, B * S])
        logit = sb("logit", [S, B, E0])
        top = sb("top", [S, B, 8])
        topi = sb("topi", [S, B, 8], U32)
        topf = sb("topf", [S, B, 2])
        gap, ex, den = sb("gap", [S, B]), sb("ex", [S, B]), sb("den", [S, B])
        hot = sb("hot", [S, 2, B, E0])
        both = sb("both", [S, B, E0], BF16)
        trib, onesb = sb("trib", [S, S], BF16), sb("onesb", [S, 128], BF16)
        run = sb("run", [128, B + 1, E0])
        over, tiles = sb("over", [128, E0, THR]), sb("tiles", [128, E0])
        low, start, end = sb("low", [128, E0, E0]), sb("start", [128, E0]), sb("end", [128, E0])
        base, picked, posf = sb("base", [S, B, E0]), sb("picked", [S, 2, B, E0]), sb("posf", [S, 2, B])

        zero_done, zero_out, scattered = sem("rzero_done"), sem("rzero_out"), sem("scattered")
        row_stat, row_mv, row_dev, row_rstd, rows_done, turned, turned_copied = (sem("r" + n) for n in
            ("row_stat", "row_mv", "row_dev", "row_rstd", "rows_done", "turned", "turned_copied"))
        logit_done, gap_done, ex_done, both_done, count_done, pos_done = (sem(n) for n in
            ("logit_done", "gap_done", "ex_done", "both_done", "count_done", "pos_done"))
        step = sem("route_step")
        h_done, gelu_done, act_done, y_done, y_copied = (sem(n) for n in
            ("sh_done", "sgelu_done", "sact_done", "sy_done", "sy_copied"))

        first = ContextProjection(m, d, 0, 2, m.bank[2:6], [sem("rctx0"), sem("rctx1")], sem("rkv_done"), sem("rkv_copied"))

        with nc.Block() as block:
            @block.sync
            def _(sp):
                first.load(sp)
                for e in range(2):
                    load_expert(sp, d, m, e, e)
                sp.wait_ge(zero_done, 1)
                xz = xg_d.rearrange("(c p r) n -> c p (r n)", p=SLOT, r=ZR)
                for c in range(XROWS // ZR):
                    sp.dma_start(xz[c], zeros[:]).then_inc(zero_out, 16)

            @block.gpsimd
            def _(pool):
                m.clear_spent(pool)
                pool.memset(zeros[:], 0.0).then_inc(zero_done, 1)
                pool.wait_ge(zero_out, 16 * (XROWS // ZR))
                pool.wait_ge(pos_done, 1)
                for t in range(B):
                    for c in range(2):
                        pool.indirect_dma_start(out=xg_d, out_offset=bass.IndirectOffsetOnAxis(ap=pos[:, c, t:t + 1], axis=0),
                                                in_=m.xn[:, t, :], in_offset=None).then_inc(scattered, 16)
                pool.wait_ge(scattered, 16 * 2 * B)

            @block.scalar
            def _(act):
                first.copy(act, 0)
                deviations(act, m, row_mv, row_dev)
                first.copy(act, 1)
                copy_turned(act, m, m.bank[0:2], turned, turned_copied)
                act.wait_ge(gap_done, 1)
                act.activation(ex[:], gap[:], ACT.Exp).then_inc(ex_done, 1)
                for n in range(2 * SM):
                    act.wait_ge(h_done, n + 1)
                    above(act, act_done, n - 1)
                    act.activation(gel[:, n % 2, :], m.bank[3 + 2 * (n % 2)][:, 0:4 * S], ACT.Gelu,
                                   bias=bs1[:, SM + n % SM:SM + n % SM + 1]).then_inc(gelu_done, 1)

            @block.vector
            def _(dve):
                count = [0]

                def then(ins):
                    ins.then_inc(step, 1)
                    count[0] += 1
                    dve.wait_ge(step, count[0])

                dve.tensor_copy(trib[:], m.const[:S, C_TRI:C_TRI + S]).then_inc(both_done, 1)
                dve.memset(onesb[:], 1.0).then_inc(both_done, 1)
                dve.memset(run[:, 0, :], 0.0).then_inc(both_done, 1)
                normalise_rows(dve, m, row_stat, row_mv, row_dev, row_rstd, rows_done)
                dve.wait_ge(logit_done, 1)
                then(dve.tensor_tensor(logit[:], m.bank[7][:S, 0:B * E0].rearrange("p (t e) -> p t e", t=B),
                                       spread_over(br[:], 1, B), ALU.add))
                then(dve.tensor_scalar(logit[:], logit[:], 1.0 / TAU, None, ALU.mult))
                for t in range(B):
                    ins = dve.max(top[:, t, :], logit[:, t, :])
                then(ins)
                dve.tensor_tensor(gap[:], top[:, :, 1], top[:, :, 0], ALU.subtract).then_inc(gap_done, 1)
                for t in range(B):
                    ins = dve.max_index(topi[:, t, :], top[:, t, :], logit[:, t, :])
                then(ins)
                then(dve.tensor_copy(topf[:], topi[:, :, 0:2]))
                for c in range(2):
                    then(dve.tensor_tensor(hot[:, c, :, :], spread_over(m.const[:S, C_IOTA:C_IOTA + E0], 1, B),
                                           spread_over(topf[:, :, c], 2, E0), ALU.is_equal))
                dve.tensor_tensor(both[:], hot[:, 0, :, :], hot[:, 1, :, :], ALU.add).then_inc(both_done, 1)
                dve.wait_ge(ex_done, 1)
                then(dve.tensor_scalar(den[:], ex[:], 1.0, None, ALU.add))
                then(dve.reciprocal(wts[:, 0, :], den[:]))
                then(dve.tensor_tensor(wts[:, 1, :], ex[:], wts[:, 0, :], ALU.mult))
                dve.wait_ge(count_done, 1)
                for t in range(B):
                    then(dve.tensor_tensor(run[:, t + 1, :], m.bank[6][:, t * E0:(t + 1) * E0], run[:, t, :], ALU.add))
                then(dve.tensor_tensor(over[:], spread_over(run[:, B, :], 2, THR),
                                       spread_over(m.const[:, C_THR:C_THR + THR], 1, E0), ALU.is_gt))
                then(dve.tensor_reduce(tiles[:], over[:], AX.X, ALU.add))
                then(dve.tensor_scalar(tiles[:], tiles[:], 1.0, None, ALU.max))
                then(dve.tensor_tensor(low[:], spread_over(tiles[:], 1, E0),
                                       m.const[:, C_LOW:C_LOW + E0 * E0].rearrange("p (a b) -> p a b", a=E0), ALU.mult))
                then(dve.tensor_reduce(start[:], low[:], AX.X, ALU.add))
                then(dve.tensor_tensor(end[:], start[:], tiles[:], ALU.add))
                then(dve.tensor_tensor(base[:], m.bank[7][:S, 128:128 + B * E0].rearrange("p (t e) -> p t e", t=B),
                                       run[:S, 0:B, :], ALU.add))
                then(dve.scalar_tensor_tensor(out=base[:], in0=spread_over(start[:S, :], 1, B), scalar=float(SLOT), in1=base[:],
                                              op0=ALU.mult, op1=ALU.add))
                then(dve.tensor_tensor(picked[:], hot[:], spread_over(base[:], 1, 2), ALU.mult))
                then(dve.tensor_reduce(posf[:], picked[:], AX.X, ALU.add))
                dve.tensor_copy(pos[:], posf[:]).then_inc(pos_done, 1)
                then(dve.tensor_copy(m.first_tile[:, 0:E0], start[0:1, :]))
                then(dve.tensor_copy(m.first_tile[:, E0:E0 + 1], end[0:1, E0 - 1:E0]))
                then(dve.tensor_scalar(m.first_tile[:, E0 + 1:E0 + 2], end[0:1, E0 - 1:E0], -1.0, float(ET + 1), ALU.mult, ALU.add))
                for n in range(2 * SM):
                    dve.wait_ge(gelu_done, n + 1)
                    dve.scalar_tensor_tensor(out=act_s[:, n % SM, (n // SM) * 4 * S:(n // SM + 1) * 4 * S],
                                             in0=m.bank[2 + 2 * (n % 2)][:, 0:4 * S], scalar=bs1[:, n % SM:n % SM + 1],
                                             in1=gel[:, n % 2, :], op0=ALU.add, op1=ALU.mult).then_inc(act_done, 1)
                for t in range(B):
                    dve.wait_ge(y_done, t + 1)
                    dve.tensor_tensor(ys[:, t, :], m.bank[t % 2][:S, 0:D], bs2[:], ALU.add).then_inc(y_copied, 1)

            @block.tensor
            def _(pe):
                first.project(pe)
                transpose_rows(pe, m, m.bank[0:2], rows_done, turned, turned_copied)
                pe.wait_ge(turned_copied, B)
                for t in range(B):
                    for k in range(KD):
                        mm = pe.matmul(m.bank[7][:S, t * E0:(t + 1) * E0], m.xT[:, k, t * S:(t + 1) * S], wr[:, k, :],
                                       start=k == 0, stop=k == KD - 1)
                mm.then_inc(logit_done, 1)

                pe.wait_ge(first.kv_copied, 8)

                def hidden(n):
                    above(pe, act_done, n - 1)
                    half, part = n // SM, n % SM
                    for a in range(2):
                        for k in range(KD):
                            mm = pe.matmul(m.bank[2 + 2 * (n % 2) + a][:, 0:4 * S],
                                           ws1[:, k, (a * SM + part) * 128:(a * SM + part + 1) * 128],
                                           m.xT[:, k, half * 4 * S:(half + 1) * 4 * S], start=k == 0, stop=k == KD - 1)
                    mm.then_inc(h_done, 1)
                hidden(0)
                hidden(1)
                pe.wait_ge(both_done, 4)
                flat = both[:].rearrange("p t e -> p (t e)")
                pe.matmul(m.bank[7][:S, 128:128 + B * E0], trib[:], flat, start=True, stop=True)
                pe.matmul(m.bank[6][:, 0:B * E0], onesb[:], flat, start=True, stop=True).then_inc(count_done, 1)
                for n in range(2, 2 * SM):
                    hidden(n)
                pe.wait_ge(act_done, 2 * SM)
                for t in range(B):
                    above(pe, y_copied, t - 1)
                    for k in range(SM):
                        mm = pe.matmul(m.bank[t % 2][:S, 0:D], act_s[:, k, t * S:(t + 1) * S], ws2[:, k, :],
                                       start=k == 0, stop=k == SM - 1)
                    mm.then_inc(y_done, 1)
    m.close_phase()


def expert_phase(nc, d, m):
    sem = m.open_phase(nc)
    with ExitStack() as ctx:
        def sb(name, shape, dt=F32):
            return ctx.enter_context(nc.sbuf_tensor(name, shape, dt))

        xg, xgT = sb("xg_rows", [128, D]), sb("xgT", [128, KD, SLOT])
        C = HM // 2
        gel, act_e = sb("gel_e", [128, C, 2, SLOT]), sb("act_e", [128, HM, SLOT])
        y, none = sb("y_rows", [128, D]), sb("no_rows", [128, D])

        x_in, turned, turned_copied, h_done, gelu_done, act_done, y_done, y_copied, y_out = (sem("e" + n) for n in
            ("x_in", "turned", "turned_copied", "h_done", "gelu_done", "act_done", "y_done", "y_copied", "y_out"))
        none_done, none_out = sem("none_done"), sem("none_out")
        w1_in, b1_in, w2_in, b2_in = m.expert_in

        def experts(eng, expert, tile, after=None):
            def one(i, u, more):
                first = eng.value_load(m.first_tile[0:1, bass.ds(2 * i + u, 1)], min_val=0, max_val=ET)
                end = eng.value_load(m.first_tile[0:1, bass.ds(2 * i + u + 1, 1)], min_val=1, max_val=ET)
                expert(i, u)
                with eng.Fori(first, end) as j:
                    tile(j, u)
                if more and after is not None:
                    after(i, u)

            with eng.Fori(0, E0 // 2 - 1) as i:
                one(i, 0, True)
                one(i, 1, True)
            one(E0 // 2 - 1, 0, False)
            one(E0 // 2 - 1, 1, False)

        with nc.Block() as block:
            @block.sync
            def _(sp):
                sp.sem_inc(y_out, 16)

                def store(j, u):
                    hold(sp, y_copied, j + 2, m.passed)
                    sp.dma_start(m.y_d[bass.ds(j * SLOT, SLOT), :], y[:]).then_inc(y_out, 16)
                experts(sp, lambda i, u: None, store, lambda i, u: load_expert(sp, d, m, 2 * i + u + 2, u))
                end = sp.value_load(m.first_tile[0:1, E0:E0 + 1], min_val=1, max_val=ET)
                hold(sp, y_out, 16 * end + 16, m.passed)

            @block.gpsimd
            def _(pool):
                m.clear_spent(pool)
                pool.memset(none[:], 0.0).then_inc(none_done, 1)
                pool.wait_ge(none_done, 1)
                end = pool.value_load(m.first_tile[0:1, E0:E0 + 1], min_val=1, max_val=ET)
                with pool.Fori(end, ET + 1) as j:
                    pool.dma_start(m.y_d[bass.ds(j * SLOT, SLOT), :], none[:]).then_inc(none_out, 16)
                spare = pool.value_load(m.first_tile[0:1, E0 + 1:E0 + 2], min_val=1, max_val=ET + 1)
                pool.wait_ge(none_out, 16 * spare)

            @block.scalar
            def _(act):
                def load_slots(j):
                    rows = m.xg_d[j * SLOT:(j + 1) * SLOT, :] if isinstance(j, int) else m.xg_d[bass.ds(j * SLOT, SLOT), :]
                    act.dma_start(xg[:], rows).then_inc(x_in, 16)

                def copy_turned_slots(j):
                    act.wait_ge(turned, j + 1)
                    act.activation(xgT[:], m.bank[3][:, 0:KD * SLOT].rearrange("p (k n) -> p k n", k=KD), ACT.Copy).then_inc(turned_copied, 1)
                    load_slots(j + 1)

                load_slots(0)
                copy_turned_slots(0)

                def gelus(j, u):
                    for c in range(C):
                        act.wait_ge(h_done, C * j + c + 1)
                        act.wait_ge(act_done, C * j + c + 1)
                        for i in range(2):
                            ins = act.activation(gel[:, c, i, :], m.bank[c][:, (2 + i) * SLOT:(3 + i) * SLOT], ACT.Gelu,
                                                 bias=m.b1[:, u, HM + 2 * c + i:HM + 2 * c + i + 1])
                        ins.then_inc(gelu_done, 1)
                    copy_turned_slots(j + 1)
                experts(act, lambda i, u: hold(act, b1_in[u], 16 * i + 16, m.passed), gelus)
                end = act.value_load(m.first_tile[0:1, E0:E0 + 1], min_val=1, max_val=ET)
                hold(act, x_in, 16 * end + 32, m.passed)

            @block.vector
            def _(dve):
                dve.sem_inc(act_done, C)
                dve.sem_inc(y_copied, 1)

                def multiply(j, u):
                    for c in range(C):
                        dve.wait_ge(gelu_done, C * j + c + 1)
                        dve.wait_ge(y_done, j + 1)
                        for i in range(2):
                            ins = dve.scalar_tensor_tensor(out=act_e[:, 2 * c + i, :], in0=m.bank[c][:, i * SLOT:(i + 1) * SLOT],
                                                           scalar=m.b1[:, u, 2 * c + i:2 * c + i + 1], in1=gel[:, c, i, :],
                                                           op0=ALU.add, op1=ALU.mult)
                        ins.then_inc(act_done, 1)
                    dve.wait_ge(y_done, j + 2)
                    dve.wait_ge(y_out, 16 * j + 16)
                    dve.tensor_tensor(y[:], m.bank[4][:, 0:D], m.b2[:, u, :], ALU.add).then_inc(y_copied, 1)

                def biases(i, u):
                    dve.wait_ge(b1_in[u], 16 * i + 16)
                    hold(dve, b2_in[u], 16 * i + 16, m.passed)
                experts(dve, biases, multiply)

            @block.tensor
            def _(pe):
                pe.sem_inc(y_done, 1)

                def turn(j):
                    pe.wait_ge(x_in, 16 * j + 16)
                    above(pe, turned_copied, j)
                    for k in range(KD):
                        mm = pe.transpose(m.bank[3][:, k * SLOT:(k + 1) * SLOT], xg[:, k * 128:(k + 1) * 128], m.ident)
                    mm.then_inc(turned, 1)

                def tile(j, u):
                    pe.wait_ge(turned_copied, j + 1)
                    for c in range(C):
                        pe.wait_ge(act_done, C * j + c + 1)
                        for i in range(4):
                            part = (i // 2) * HM + 2 * c + i % 2
                            for k in range(KD):
                                mm = pe.matmul(m.bank[c][:, i * SLOT:(i + 1) * SLOT], m.w1[:, u, k, part * 128:(part + 1) * 128],
                                               xgT[:, k, :], start=k == 0, stop=k == KD - 1)
                        mm.then_inc(h_done, 1)
                    turn(j + 1)
                    pe.wait_ge(y_copied, j + 1)
                    for k in range(HM):
                        if k % 2 == 0:
                            pe.wait_ge(act_done, C * (j + 1) + k // 2 + 1)
                        mm = pe.matmul(m.bank[4][:, 0:D], act_e[:, k, :], m.w2[:, u, k, :], start=k == 0, stop=k == HM - 1)
                    mm.then_inc(y_done, 1)

                def weights(i, u):
                    pe.wait_ge(w1_in[u], 16 * i + 16)
                    hold(pe, w2_in[u], 16 * i + 16, m.passed)
                turn(0)
                experts(pe, weights, tile)
    m.close_phase()


def soft_attention_phase(nc, d, m):
    sem = m.open_phase(nc)
    with ExitStack() as ctx:
        def sb(name, shape, dt=F32):
            return ctx.enter_context(nc.sbuf_tensor(name, shape, dt))

        yg = sb("yg", [S, 2, B, D])
        v = sb("v1", [KW, 2, KT, D])
        qd = sb("qd1", [128, 2, KD, HG, S])
        oT = sb("oT1", [128, 2, G, S])
        maskr = sb("maskr1", [S, 2, KEYS], U8)
        bias = sb("bias1", [S, 2, KEYS])
        PR = 4
        sm = sb("sm", [S, PR, KEYS])
        p = sb("p", [S, PR, KEYS])
        pT = sb("pT", [KW, PR, KT, S])
        mx, nm = sb("mx", [S, PR]), sb("nm", [S, PR])
        rsum, rinv = sb("hsum", [S, 2, H]), sb("hinv", [S, 2, H])
        rT = sb("rT", [H, 2, S])

        got = [sem(f"got{t}") for t in range(B)]
        added, ready = sem("added"), sem("x_ready")
        row_stat, row_mv, row_dev, row_rstd, rows_done, turned, turned_copied = (sem(n + "1") for n in
            ("row_stat", "row_mv", "row_dev", "row_rstd", "rows_done", "turned", "turned_copied"))
        ctx_in, kv_done, kv_copied = [sem("kctx0"), sem("kctx1")], sem("kv_done1"), sem("kv_copied1")
        q_done, q_copied, qd_done, rows_zero = sem("q_done1"), sem("q_copied1"), sem("qd_done1"), sem("rows_zero1")
        mask_in = [sem("mask1_in0"), sem("mask1_in1")]
        v_copied, bias_done, score_done, max_done, nmax_done, exp_done = (sem(n + "1") for n in
            ("v_copied", "bias_done", "score_done", "max_done", "nmax_done", "exp_done"))
        pT_done, pT_copied, pv_done = sem("pT_done1"), sem("pT_copied1"), sem("pv_done1")
        rinv_done, rT_done, rT_copied, rb_done, norm_done = (sem(n + "1") for n in
            ("rinv_done", "rT_done", "rT_copied", "rb_done", "norm_done"))
        o_copied, proj_done, x_done = sem("o_copied1"), sem("proj_done1"), sem("x_done1")
        rest = ContextProjection(m, d, 2, B - 2, m.bank[2:6], ctx_in, kv_done, kv_copied)

        with nc.Block() as block:
            @block.sync
            def _(sp):
                rest.load(sp)

                def mask(b, u):
                    hold(sp, bias_done, b - 1, m.passed)
                    ms = d["mask1"][b:b + 1] if isinstance(b, int) else d["mask1"][bass.ds(b, 1)]
                    sp.dma_start(maskr[:, u, :], ms.rearrange("a q k -> (a q) k")).then_inc(mask_in[u], 16)
                pairs(sp, mask)

            @block.gpsimd
            def _(pool):
                for t in range(B):
                    for c in range(2):
                        pool.indirect_dma_start(out=yg[:, c, t, :], out_offset=None, in_=m.y_d,
                                                in_offset=bass.IndirectOffsetOnAxis(ap=m.pos[:, c, t:t + 1], axis=0)).then_inc(got[t], 16)
                m.clear_spent(pool)

                def batch(b, u):
                    for k in range(KD):
                        above(pool, score_done, H * (b - 1))
                        q = m.qT[:, k, b * S:(b + 1) * S] if isinstance(b, int) else m.qT[:, k, bass.ds(b * S, S)]
                        pool.tensor_tensor(qd[:, u, k, :, :], spread_over(q, 1, HG),
                                           spread_over(m.const[:, C_HEAD:C_HEAD + HG], 2, S), ALU.mult).then_inc(qd_done, 1)
                    above(pool, pv_done, H * (b - 1))
                    pool.tensor_copy(v[:, u, :, :], at(m.v, b).rearrange("p a t n -> p (a t) n")).then_inc(v_copied, 1)
                pool.wait_ge(q_copied, 2 * KD)
                pool.wait_ge(kv_copied, 4 * (B - 2))
                pairs(pool, batch)

            @block.scalar
            def _(act):
                with act.Fori(0, B - 3) as i:
                    rest.copy(act, i)
                deviations(act, m, row_mv, row_dev)
                rest.copy(act, B - 3)
                copy_turned(act, m, m.bank[0:2], turned, turned_copied)
                for n in range(2 * KD):
                    act.wait_ge(q_done, n + 1)
                    act.activation(m.qT[:, n % KD, (n // KD) * 4 * S:(n // KD + 1) * 4 * S], m.bank[n % 2][:, 0:4 * S],
                                   ACT.Copy).then_inc(q_copied, 1)

                def turn_sums(b, u):
                    act.wait_ge(rT_done, b + 1)
                    act.activation(rT[:, u, :], m.bank[7][:H, 0:S], ACT.Copy).then_inc(rT_copied, 1)

                def batch(b, u):
                    for h in range(H):
                        n = H * b + h
                        act.wait_ge(nmax_done, n + 1)
                        above(act, pT_done, n - PR + 1)
                        act.activation(p[:, h % PR, :], sm[:, h % PR, :], ACT.Exp, bias=nm[:, h % PR:h % PR + 1],
                                       scale=SCALE, accum_out=rsum[:, u, h:h + 1]).then_inc(exp_done, 1)
                        if h == 3 and not known(b, 0):
                            turn_sums(b - 1, 1 - u)
                pairs(act, batch)
                turn_sums(B - 1, 1)

            @block.vector
            def _(dve):
                for t in range(B):
                    dve.wait_ge(got[t], 32)
                    dve.scalar_tensor_tensor(out=m.ys[:, t, :], in0=yg[:, 0, t, :], scalar=m.wts[:, 0, t:t + 1], in1=m.ys[:, t, :],
                                             op0=ALU.mult, op1=ALU.add).then_inc(added, 1)
                    dve.wait_ge(added, 2 * t + 1)
                    dve.scalar_tensor_tensor(out=m.ys[:, t, :], in0=yg[:, 1, t, :], scalar=m.wts[:, 1, t:t + 1], in1=m.ys[:, t, :],
                                             op0=ALU.mult, op1=ALU.add).then_inc(added, 1)
                    dve.wait_ge(added, 2 * t + 2)
                    dve.scalar_tensor_tensor(out=m.x[:, t, :], in0=m.ys[:, t, :], scalar=m.gates[:S, 2:3], in1=m.x[:, t, :],
                                             op0=ALU.mult, op1=ALU.add).then_inc(ready, 16 // B)
                normalise_rows(dve, m, row_stat, row_mv, row_dev, row_rstd, rows_done, ready)
                dve.memset(m.bank[6][:], 0.0).then_inc(rows_zero, 1)

                def turn_mask(b, u):
                    dve.wait_ge(mask_in[u], 8 * (b - u) + 16)
                    dve.tensor_scalar(bias[:, u, :], maskr[:, u, :], 0.0, NEG1, ALU.is_gt, ALU.mult).then_inc(bias_done, 1)

                def maximum(b, u, h):
                    n = H * b + h
                    above(dve, exp_done, n - PR + 1)
                    hold(dve, score_done, n + 1, m.passed)
                    dve.tensor_tensor_reduce(sm[:, h % PR, :], m.bank[h % 4][:S, 0:KEYS], bias[:, u, :], 1.0, NEG_MAX,
                                             ALU.add, ALU.max, mx[:, h % PR:h % PR + 1]).then_inc(max_done, 1)

                def negate(n, h):
                    dve.wait_ge(max_done, n + 1)
                    dve.tensor_scalar(nm[:, h % PR:h % PR + 1], mx[:, h % PR:h % PR + 1], -SCALE, None, ALU.mult).then_inc(nmax_done, 1)

                def copy_probs(n, slot, bank):
                    dve.wait_ge(pT_done, n + 1)
                    above(dve, pv_done, n - PR + 1)
                    dve.tensor_copy(pT[:, slot, :, :], m.bank[bank][:KW, 0:KT * S].rearrange("p (t n) -> p t n", t=KT)).then_inc(pT_copied, 1)

                def invert_sums(b, u):
                    dve.wait_ge(exp_done, H * (b + 1))
                    dve.reciprocal(rinv[:, u, :], rsum[:, u, :]).then_inc(rinv_done, 1)

                def copy_out(b, u):
                    dve.wait_ge(pv_done, H * (b + 1))
                    dve.tensor_copy(oT[:, u, :, :], m.bank[6][:, 0:G * S].rearrange("p (g n) -> p g n", g=G)).then_inc(o_copied, 1)

                def divide(b, u):
                    dve.wait_ge(rb_done, b + 1)
                    dve.wait_ge(o_copied, b + 1)
                    dve.tensor_tensor(oT[:, u, :, :], m.bank[7][:, 0:G * S].rearrange("p (g n) -> p g n", g=G), oT[:, u, :, :],
                                      ALU.mult).then_inc(norm_done, 1)

                def residual(b, u):
                    dve.wait_ge(proj_done, b + 1)
                    xb = at(m.x, b).rearrange("p a n -> p (a n)")
                    dve.scalar_tensor_tensor(out=xb, in0=m.bank[7][:S, 0:D], scalar=m.gates[:S, 1:2], in1=xb,
                                             op0=ALU.mult, op1=ALU.add).then_inc(x_done, 1)

                turn_mask(0, 0)

                def batch(b, u):
                    dve.wait_ge(bias_done, b + 1)
                    for h in range(H):
                        n = H * b + h
                        maximum(b, u, h)
                        if h >= 2 or not known(b, 0):
                            copy_probs(n - 2, (h - 2) % PR, 4 + h % 2)
                        negate(n, h)
                        if not known(b, 0):
                            if h == 1:
                                invert_sums(b - 1, 1 - u)
                            if h == 2:
                                copy_out(b - 1, 1 - u)
                            if h == 5:
                                divide(b - 1, 1 - u)
                            if h == 7:
                                residual(b - 1, 1 - u)
                        if h == 12 and not known(b, B - 1):
                            turn_mask(b + 1, 1 - u)
                pairs(dve, batch)
                for h in range(2):
                    copy_probs(H * B - 2 + h, (h + 2) % PR, 4 + h)
                invert_sums(B - 1, 1)
                copy_out(B - 1, 1)
                divide(B - 1, 1)
                residual(B - 1, 1)

            @block.tensor
            def _(pe):
                rest.project(pe)
                transpose_rows(pe, m, m.bank[0:2], rows_done, turned, turned_copied)
                pe.wait_ge(turned_copied, B)
                for n in range(2 * KD):
                    above(pe, q_copied, n - 1)
                    for k in range(KD):
                        mm = pe.matmul(m.bank[n % 2][:, 0:4 * S], m.wq1[:, k, (n % KD) * 128:(n % KD + 1) * 128],
                                       m.xT[:, k, (n // KD) * 4 * S:(n // KD + 1) * 4 * S], start=k == 0, stop=k == KD - 1)
                    mm.then_inc(q_done, 1)
                pe.wait_ge(q_copied, 2 * KD)
                pe.wait_ge(kv_copied, 4 * (B - 2))
                pe.wait_ge(rows_zero, 1)

                def scores(b, u, h):
                    if h == 0:
                        pe.wait_ge(qd_done, KD * (b + 1))
                    above(pe, max_done, H * b + h - 3)
                    pe.matmul(m.bank[h % 4][:S, 0:KEYS], qd[:, u, h // HG, h % HG, :],
                              at(m.kT[:, h // HG, :, :], b).rearrange("p a n -> p (a n)"), start=True, stop=True).then_inc(score_done, 1)

                def turn_probs(n, h):
                    pe.wait_ge(exp_done, n + 1)
                    above(pe, pT_copied, n - 1)
                    for t in range(KT):
                        mm = pe.transpose(m.bank[4 + h % 2][:KW, t * S:(t + 1) * S], p[:, h % PR, t * KW:(t + 1) * KW], m.ident[:S, :S])
                    mm.then_inc(pT_done, 1)

                def values(b, u, h):
                    if h == 0:
                        pe.wait_ge(v_copied, b + 1)
                        above(pe, o_copied, b)
                    pe.wait_ge(pT_copied, H * b + h + 1)
                    g, j = h // 4, h % 4
                    for t in range(KT):
                        mm = pe.matmul(m.bank[6][32 * j:32 * j + DH, g * S:(g + 1) * S], v[:, u, t, h * DH:(h + 1) * DH],
                                       pT[:, h % PR, t, :], start=t == 0, stop=t == KT - 1, tile_position=(0, 32 * j))
                    mm.then_inc(pv_done, 1)

                def turn_sums(b, u):
                    pe.wait_ge(rinv_done, b + 1)
                    above(pe, x_done, b)
                    pe.transpose(m.bank[7][:H, 0:S], rinv[:, u, :], m.ident[:S, :S]).then_inc(rT_done, 1)

                def spread_sums(b, u):
                    pe.wait_ge(rT_copied, b + 1)
                    for g in range(G):
                        mm = pe.matmul(m.bank[7][:, g * S:(g + 1) * S], m.const[:H, C_SPREAD + g * 128:C_SPREAD + (g + 1) * 128],
                                       rT[:, u, :], start=True, stop=True)
                    mm.then_inc(rb_done, 1)

                def project_out(b, u):
                    pe.wait_ge(norm_done, b + 1)
                    for g in range(G):
                        mm = pe.matmul(m.bank[7][:S, 0:D], oT[:, u, g, :], m.wo1[:, g, :], start=g == 0, stop=g == G - 1)
                    mm.then_inc(proj_done, 1)

                def batch(b, u):
                    first = known(b, 0)
                    for h in range(H):
                        scores(b, u, h)
                        if h >= 2 or not first:
                            turn_probs(H * b + h - 2, (h - 2) % H)
                        if h >= 3:
                            values(b, u, h - 3)
                        elif not first:
                            values(b - 1, 1 - u, H + h - 3)
                        if not first:
                            if h == 3:
                                turn_sums(b - 1, 1 - u)
                            if h == 5:
                                spread_sums(b - 1, 1 - u)
                            if h == 7:
                                project_out(b - 1, 1 - u)
                pairs(pe, batch)
                for h in range(2):
                    turn_probs(H * B - 2 + h, H - 2 + h)
                    values(B - 1, 1, H - 3 + h)
                values(B - 1, 1, H - 1)
                turn_sums(B - 1, 1)
                spread_sums(B - 1, 1)
                project_out(B - 1, 1)
    m.close_phase()


def gated_phase(nc, d, m):
    sem = m.open_phase(nc)
    with ExitStack() as ctx:
        def sb(name, shape, dt=F32):
            return ctx.enter_context(nc.sbuf_tensor(name, shape, dt))

        EP = E1 // 2
        vg, vd = sb("vg", [128, KD, E1 * R1]), sb("vd", [128, EP, 2, D])
        we, wp = sb("we", [128, KD, E1 * D]), sb("wp", [128, KD, D])
        bb = sb("bb", [E1 + 1, D])
        xe = sb("xe", [128, EP, B * S])
        diff = sb("diff", [S, 2, 2, D])
        junk = sb("junk", [S, 2, D])
        r2, res = sb("r2", [S, B, E1]), sb("res", [S, B, E1])
        rmin, rsum, rinv = sb("rmin", [S, B]), sb("rsum", [S, B]), sb("rinv", [S, B])
        gap, ex, rw = sb("gap1", [S, B, E1]), sb("ex1", [S, B, E1]), sb("rw", [S, B, E1])
        top, topi, topf = sb("top1", [S, B, 8]), sb("topi1", [S, B, 8], U32), sb("topf1", [S, B, 2])
        hot = sb("hot1", [S, 2, B, E1])
        over, overb, onesb = sb("over1", [S, B, E1]), sb("overb", [S, B, E1], BF16), sb("ones1", [S, S], BF16)
        cnt, some, none = sb("cnt", [S, 1]), sb("some", [S, 1]), sb("none", [S, 1])
        mask, fw, sw, swz = sb("chosen1", [S, B, E1]), sb("fw", [S, B, E1]), sb("sw", [S, B]), sb("swz", [S, B])
        w9, w9T = sb("w9", [S, B, E1 + 1]), sb("w9T", [E1 + 1, B, S])
        acc, res_out = sb("acc", [S, 2, D]), sb("res_out", [S, 2, D])

        w_in, vd_zero, vd_in = sem("gw_in"), sem("vd_zero"), sem("vd_in")
        row_stat, row_mv, row_dev, row_rstd, rows_done, turned, turned_copied = (sem("g" + n) for n in
            ("row_stat", "row_mv", "row_dev", "row_rstd", "rows_done", "turned", "turned_copied"))
        xe_done, xe_copied, proj_done, diff_done, sq_done = (sem(n) for n in
            ("xe_done", "xe_copied", "gproj_done", "diff_done", "sq_done"))
        gap_done, ex_done, over_done, cnt_done, w_done, wT_done, wT_copied = (sem(n) for n in
            ("ggap_done", "gex_done", "over_done", "cnt_done", "w_done", "wT_done", "wT_copied"))
        base_done, base_copied, e_done, e_added, tile_done = (sem(n) for n in
            ("base_done", "base_copied", "e_done", "e_added", "tile_done"))
        step, res_done = sem("gate_step"), sem("res_done")
        out_done = [sem("out_done0"), sem("out_done1")]

        with nc.Block() as block:
            @block.sync
            def _(sp):
                sp.dma_start(vg[:], d["VgT"].rearrange("(k p) n -> p k n", p=128)).then_inc(w_in, 16)
                sp.wait_ge(vd_zero, 1)
                for a in range(2):
                    sp.dma_start(vd[64 * a:64 * a + 64, :, a, :], d["VgR"].rearrange("(q a r) n -> a r q n", a=2, r=R1)[a]).then_inc(vd_in, 16)
                sp.dma_start(wp[:], d["WpT"].rearrange("(k p) n -> p k n", p=128)).then_inc(w_in, 16)
                sp.dma_start(we[:], d["WeT"].rearrange("(k p) n -> p k n", p=128)).then_inc(w_in, 16)
                sp.dma_start(bb[0:E1, :], d["L1_ffn_be"]).then_inc(w_in, 16)
                sp.dma_start(bb[E1:E1 + 1, :], d["L1_ffn_bp"].partition_broadcast(1)).then_inc(w_in, 16)
                for t in range(B):
                    sp.wait_ge(tile_done, t + 1)
                    sp.dma_start(d["out"][t], m.x[:, t, :]).then_inc(out_done[t % 2], 16)
                for u in range(2):
                    sp.wait_ge(out_done[u], 16 * B // 2)

            @block.gpsimd
            def _(pool):
                pool.memset(vd[:], 0.0).then_inc(vd_zero, 1)

            @block.scalar
            def _(act):
                deviations(act, m, row_mv, row_dev)
                copy_turned(act, m, m.bank[0:2], turned, turned_copied)
                for n in range(2 * EP):
                    act.wait_ge(xe_done, n + 1)
                    act.activation(xe[:, n % EP, (n // EP) * 4 * S:(n // EP + 1) * 4 * S], m.bank[2 + n % 2][:, 0:4 * S],
                                   ACT.Copy).then_inc(xe_copied, 1)
                for n in range(B * EP):
                    act.wait_ge(diff_done, n + 1)
                    for a in range(2):
                        ins = act.activation(junk[:, a, :], diff[:, n % 2, a, :], ACT.Square,
                                             accum_out=r2[:, n // EP, 2 * (n % EP) + a:2 * (n % EP) + a + 1])
                        ins.then_inc(sq_done, 1)
                        act.wait_ge(sq_done, 2 * n + a + 1)
                act.activation(res[:], r2[:], ACT.Sqrt).then_inc(res_done, 1)
                act.wait_ge(gap_done, 1)
                act.activation(ex[:], gap[:], ACT.Exp, scale=-1.0).then_inc(ex_done, 1)
                act.wait_ge(wT_done, 1)
                act.activation(w9T[:, 0:4, :], m.bank[0][:E1 + 1, 0:4 * S].rearrange("p (t n) -> p t n", t=4), ACT.Copy).then_inc(wT_copied, 1)
                act.activation(w9T[:, 4:8, :], m.bank[1][:E1 + 1, 0:4 * S].rearrange("p (t n) -> p t n", t=4), ACT.Copy).then_inc(wT_copied, 1)
                for t in range(B):
                    act.wait_ge(base_done, t + 1)
                    above(act, tile_done, t - 1)
                    act.activation(acc[:, t % 2, :], m.bank[2 + t % 2][:S, 0:D], ACT.Copy).then_inc(base_copied, 1)

            @block.vector
            def _(dve):
                count = [0]

                def then(ins):
                    ins.then_inc(step, 1)
                    count[0] += 1
                    dve.wait_ge(step, count[0])

                dve.memset(onesb[:], 1.0).then_inc(over_done, 1)
                dve.memset(w9[:], 1.0).then_inc(over_done, 1)
                normalise_rows(dve, m, row_stat, row_mv, row_dev, row_rstd, rows_done)
                dve.wait_ge(rows_done, B)
                for n in range(B * EP):
                    dve.wait_ge(proj_done, n + 1)
                    above(dve, sq_done, 2 * (n - 1))
                    dve.tensor_tensor(diff[:, n % 2, :, :], m.bank[4 + n % 4][:S, :].rearrange("p (a n) -> p a n", a=2),
                                      spread_over(m.xn[:, n // EP, :], 1, 2), ALU.subtract).then_inc(diff_done, 1)
                dve.wait_ge(res_done, 1)
                then(dve.tensor_reduce(rmin[:], res[:], AX.X, ALU.min))
                dve.tensor_tensor(gap[:], res[:], spread_over(rmin[:], 2, E1), ALU.subtract).then_inc(gap_done, 1)
                dve.wait_ge(ex_done, 1)
                then(dve.tensor_reduce(rsum[:], ex[:], AX.X, ALU.add))
                then(dve.reciprocal(rinv[:], rsum[:]))
                then(dve.tensor_tensor(rw[:], ex[:], spread_over(rinv[:], 2, E1), ALU.mult))
                then(dve.tensor_scalar(over[:], rw[:], 1.0 / E1, None, ALU.is_gt))
                dve.tensor_copy(overb[:], over[:]).then_inc(over_done, 1)
                for t in range(B):
                    ins = dve.max(top[:, t, :], rw[:, t, :])
                then(ins)
                for t in range(B):
                    ins = dve.max_index(topi[:, t, :], top[:, t, :], rw[:, t, :])
                then(ins)
                then(dve.tensor_copy(topf[:], topi[:, :, 0:2]))
                for c in range(2):
                    then(dve.tensor_tensor(hot[:, c, :, :], spread_over(m.const[:S, C_IOTA:C_IOTA + E1], 1, B),
                                           spread_over(topf[:, :, c], 2, E1), ALU.is_equal))
                dve.wait_ge(cnt_done, 1)
                then(dve.tensor_reduce(cnt[:], m.bank[2][:S, 0:B * E1], AX.X, ALU.max))
                then(dve.tensor_scalar(some[:], cnt[:], 0.0, None, ALU.is_gt))
                then(dve.tensor_scalar(none[:], cnt[:], 0.0, None, ALU.is_equal))
                then(dve.tensor_scalar(mask[:], over[:], some[:, 0:1], None, ALU.mult))
                then(dve.scalar_tensor_tensor(out=mask[:], in0=hot[:, 0, :, :], scalar=none[:, 0:1], in1=mask[:],
                                              op0=ALU.mult, op1=ALU.add))
                then(dve.tensor_tensor(fw[:], rw[:], mask[:], ALU.mult))
                then(dve.tensor_tensor(mask[:], hot[:, 0, :, :], hot[:, 1, :, :], ALU.add))
                then(dve.tensor_tensor(fw[:], fw[:], mask[:], ALU.mult))
                then(dve.tensor_reduce(sw[:], fw[:], AX.X, ALU.add))
                then(dve.tensor_scalar(swz[:], sw[:], 0.0, None, ALU.is_equal))
                then(dve.tensor_tensor(sw[:], sw[:], swz[:], ALU.add))
                then(dve.reciprocal(rinv[:], sw[:]))
                dve.tensor_tensor(w9[:, :, 0:E1], fw[:], spread_over(rinv[:], 2, E1), ALU.mult).then_inc(w_done, 1)
                dve.wait_ge(w_done, 1)
                n = 0
                for t in range(B):
                    dve.wait_ge(base_copied, t + 1)
                    for q in range(EP):
                        dve.wait_ge(e_done, EP * t + q + 1)
                        for a in range(2):
                            e = 2 * q + a
                            ins = dve.scalar_tensor_tensor(out=acc[:, t % 2, :], in0=m.bank[4 + q][:S, a * D:(a + 1) * D],
                                                           scalar=w9[:, t, e:e + 1], in1=acc[:, t % 2, :], op0=ALU.mult, op1=ALU.add)
                            ins.then_inc(e_added, 1)
                            n += 1
                            dve.wait_ge(e_added, n)
                    dve.scalar_tensor_tensor(out=m.x[:, t, :], in0=acc[:, t % 2, :], scalar=m.gates[:S, 3:4], in1=m.x[:, t, :],
                                             op0=ALU.mult, op1=ALU.add).then_inc(tile_done, 1)

            @block.tensor
            def _(pe):
                transpose_rows(pe, m, m.bank[0:2], rows_done, turned, turned_copied)
                pe.wait_ge(turned_copied, B)
                pe.wait_ge(w_in, 80)
                for n in range(2 * EP):
                    above(pe, xe_copied, n - 1)
                    for k in range(KD):
                        mm = pe.matmul(m.bank[2 + n % 2][:, 0:4 * S], vg[:, k, (n % EP) * 128:(n % EP + 1) * 128],
                                       m.xT[:, k, (n // EP) * 4 * S:(n // EP + 1) * 4 * S], start=k == 0, stop=k == KD - 1)
                    mm.then_inc(xe_done, 1)
                pe.wait_ge(vd_in, 32)
                pe.wait_ge(xe_copied, 2 * EP)
                for n in range(B * EP):
                    above(pe, diff_done, n - 3)
                    pe.matmul(m.bank[4 + n % 4][:S, :], xe[:, n % EP, (n // EP) * S:(n // EP + 1) * S], vd[:, n % EP, :, :],
                              start=True, stop=True).then_inc(proj_done, 1)
                pe.wait_ge(over_done, 3)
                pe.matmul(m.bank[2][:S, 0:B * E1], onesb[:], overb[:].rearrange("p t e -> p (t e)"), start=True, stop=True).then_inc(cnt_done, 1)
                pe.wait_ge(w_done, 1)
                for t in range(B):
                    mm = pe.transpose(m.bank[t // 4][:E1 + 1, (t % 4) * S:(t % 4 + 1) * S], w9[:, t, :], m.ident[:S, :S])
                mm.then_inc(wT_done, 1)
                pe.wait_ge(wT_copied, 2)
                for t in range(B):
                    above(pe, base_copied, t - 1)
                    for k in range(KD):
                        pe.matmul(m.bank[2 + t % 2][:S, 0:D], m.xT[:, k, t * S:(t + 1) * S], wp[:, k, :], start=k == 0, stop=False)
                    pe.matmul(m.bank[2 + t % 2][:S, 0:D], w9T[:, t, :], bb[:], start=False, stop=True).then_inc(base_done, 1)
                    for q in range(EP):
                        above(pe, e_added, 2 * (EP * (t - 1) + q + 1))
                        for k in range(KD):
                            mm = pe.matmul(m.bank[4 + q][:S, :], m.xT[:, k, t * S:(t + 1) * S], we[:, k, q * 2 * D:(q + 1) * 2 * D],
                                           start=k == 0, stop=k == KD - 1)
                        mm.then_inc(e_done, 1)


def kernel(x, ctx_1024, mask_Bx1xSxS2_ik1, mask_BxSxS2_bk1, g_xattn, g_ffn,
           L0_xattn_Wq, L0_xattn_bq, L0_xattn_Wk, L0_xattn_bk, L0_xattn_Wv, L0_xattn_bv, L0_xattn_Wo,
           L0_ffn_Ws1, L0_ffn_bs1, L0_ffn_Ws2, L0_ffn_bs2, L0_ffn_We1, L0_ffn_be1, L0_ffn_We2, L0_ffn_be2,
           L0_ffn_Wr, L0_ffn_br, L1_xattn_Wq, L1_xattn_Wk, L1_xattn_Wv, L1_xattn_Wo,
           L1_ffn_Wp, L1_ffn_bp, L1_ffn_We, L1_ffn_be, L1_ffn_Vg):
    import numpy as np
    import concourse.bacc as bacc
    from concourse.bass_utils import run_bass_kernel_spmd

    a = np.asarray
    arrays = {
        "x": a(x),
        "ctxT": a(ctx_1024).transpose(0, 2, 1),
        "mask0": a(mask_Bx1xSxS2_ik1)[:, 0].transpose(0, 2, 1),
        "mask1": a(mask_BxSxS2_bk1),
        "g_xattn": a(g_xattn),
        "g_ffn": a(g_ffn),
        "L0_xattn_WqT": a(L0_xattn_Wq).T, "L0_xattn_WkT": a(L0_xattn_Wk).T,
        "L0_xattn_WvT": a(L0_xattn_Wv).T, "L0_xattn_WoT": a(L0_xattn_Wo).T,
        "bqT": a(L0_xattn_bq).reshape(KD, 128).T, "bkT": a(L0_xattn_bk).reshape(KD, 128).T, "L0_xattn_bv": a(L0_xattn_bv),
        "L1_xattn_WqT": a(L1_xattn_Wq).T, "L1_xattn_WkT": a(L1_xattn_Wk).T,
        "L1_xattn_WvT": a(L1_xattn_Wv).T, "L1_xattn_WoT": a(L1_xattn_Wo).T,
        "L0_ffn_Ws1": a(L0_ffn_Ws1), "bs1T": a(L0_ffn_bs1).reshape(2 * SM, 128).T, "L0_ffn_Ws2": a(L0_ffn_Ws2), "L0_ffn_bs2": a(L0_ffn_bs2),
        "L0_ffn_We1": a(L0_ffn_We1), "L0_ffn_We2": a(L0_ffn_We2), "L0_ffn_be2": a(L0_ffn_be2),
        "be1T": a(L0_ffn_be1).reshape(E0, 2 * HM, 128).transpose(0, 2, 1),
        "L0_ffn_Wr": a(L0_ffn_Wr), "L0_ffn_br": a(L0_ffn_br),
        "WpT": a(L1_ffn_Wp).T, "L1_ffn_bp": a(L1_ffn_bp), "L1_ffn_be": a(L1_ffn_be),
        "WeT": a(L1_ffn_We).transpose(2, 0, 1).reshape(D, E1 * D),
        "VgT": a(L1_ffn_Vg).transpose(1, 0, 2).reshape(D, E1 * R1),
        "VgR": a(L1_ffn_Vg).transpose(0, 2, 1).reshape(E1 * R1, D),
        "const": constants(),
    }
    arrays = {"in_" + k: np.ascontiguousarray(v) for k, v in arrays.items()}
    nc = bacc.Bacc("TRN2", target_bir_lowering=False, num_devices=1)
    d = {k[3:]: nc.dram_tensor(k, v.shape, mybir.dt.from_np(v.dtype), kind="ExternalInput").ap() for k, v in arrays.items()}
    d["out"] = nc.dram_tensor("out", (B, S, D), F32, kind="ExternalOutput").ap()
    build(nc, d)
    r = run_bass_kernel_spmd(nc, [arrays], core_ids=[0])
    return r.results[0]["out"]
```

```python
from contextlib import ExitStack

import concourse.bass as bass
from concourse import mybir

F32 = mybir.dt.float32
F32R = mybir.dt.float32r
BF16 = mybir.dt.bfloat16
I32 = mybir.dt.int32
U32 = mybir.dt.uint32
U8 = mybir.dt.uint8
ALU = mybir.AluOpType
ACT = mybir.ActivationFunctionType
AX = mybir.AxisListType

B = 8
S = 112
D = 256
KD = D // 128
KEYS = 375
KT = 3
KW = KEYS // KT
H = 16
DH = D // H
G = 4
SCALE = float(DH) ** -0.5
EPS = 1e-5
NEG1 = -1e30
FAR = 3e38
NQ = 4
HQ = H // NQ
E0 = 12
HR = 768
HM = HR // 128
HS = 512
SM = HS // 128
TAU = 1.5
SLOT = 128
ET = 2 * B * S // SLOT + E0
TB = 5
XROWS = ET + 2
ZR = 4
THR = -(-B * S // SLOT)
E1 = 8
R1 = 64
EP = E1 // 2

C_ID = 0
C_TRI = C_ID + 128
C_HEADQ = C_TRI + S
C_SPREAD = C_HEADQ + HQ
C_IOTA = C_SPREAD + G * 128
C_THR = C_IOTA + E0
C_LOW = C_THR + THR
C_EPS = C_LOW + E0 * E0
C_END = C_EPS + 1

LATER = 13 * 16


def constants():
    import numpy as np
    c = np.zeros((128, C_END), np.float32)
    c[:, C_ID:C_ID + 128] = np.eye(128)
    c[:S, C_TRI:C_TRI + S] = np.triu(np.ones((S, S)), 1)
    for h in range(HQ):
        for a in range(2):
            c[64 * a + h * DH:64 * a + (h + 1) * DH, C_HEADQ + h] = 1
    for g in range(G):
        for j in range(4):
            c[4 * g + j, C_SPREAD + g * 128 + 32 * j:C_SPREAD + g * 128 + 32 * j + 32] = 1
    c[:, C_IOTA:C_IOTA + E0] = np.arange(E0)
    c[:, C_THR:C_THR + THR] = np.arange(THR) * SLOT
    c[:, C_LOW:C_LOW + E0 * E0] = np.tril(np.ones((E0, E0)), -1).reshape(-1)
    c[:, C_EPS] = EPS
    return c


def above(eng, sem, value):
    if not isinstance(value, int) or value > 0:
        eng.wait_ge(sem, value)


def hold(eng, sem, value, passed):
    if not isinstance(value, int) or value > 0:
        eng.wait_ge(sem, value)
        eng.sem_inc(passed, 1)


def pairs(eng, body, n=B // 2):
    for u in range(2):
        body(u, u)
    with eng.Fori(1, n - 1) as i:
        for u in range(2):
            body(2 * i + u, u)
    for u in range(2):
        body(2 * (n - 1) + u, u)


def known(b, value):
    return isinstance(b, int) and b == value


def at(ap, b):
    return ap[:, b:b + 1] if isinstance(b, int) else ap[:, bass.ds(b, 1)]


def spread_over(ap, axis, n):
    a = ap.unsqueeze(axis)
    shape = list(a.shape)
    shape[axis] = n
    return a.broadcast_to(shape)


class Memory:

    def __init__(self):
        self.live = None
        self.spent = None

    def open_phase(self, nc):
        self.spent, self.live = self.live, (ExitStack(), [])
        stack, handles = self.live

        def sem(name):
            handles.append(stack.enter_context(nc.semaphore(name)))
            return handles[-1]
        return sem

    def clear_spent(self, pool):
        if self.spent is not None:
            for s in self.spent[1]:
                pool.sem_clear(s)

    def close_phase(self):
        if self.spent is not None:
            self.spent[0].close()


def build(nc, d, phases=6):
    with ExitStack() as ctx:
        def sb(name, shape, dt=F32, stack=ctx):
            return stack.enter_context(nc.sbuf_tensor(name, shape, dt))

        m = Memory()
        m.x = sb("x", [S, B, D])
        m.xn = sb("xn", [S, B, D])
        m.xT = sb("xT", [128, KD, B * S])
        m.stat = sb("stat", [S, B, 6])
        m.mv = sb("mv", [S, B, 2])
        m.dev = sb("dev", [S, B])
        m.rstd = sb("rstd", [S, B])
        m.const = sb("const", [128, C_END])
        m.gates = sb("gates", [128, 4])
        m.graw = sb("graw", [128, 4])
        m.ws1, m.ws2, m.wr = sb("ws1", [128, KD, 2 * HS]), sb("ws2", [128, SM, D]), sb("wr", [128, KD, E0])
        m.bs1, m.bs2, m.br = sb("bs1", [128, 2 * SM]), sb("bs2", [S, D]), sb("br", [S, E0])
        m.wq1, m.wk1, m.wv1 = sb("wq1", [128, KD, 2 * D]), sb("wk1", [128, KD, D]), sb("wv1", [128, KD, D])
        m.wo1 = sb("wo1", [128, G, D])
        m.ctxT = sb("ctxT", [128, 2, KD, KEYS])
        m.xe_last = sb("xe_last", [128, 4 * S])
        m.bank = [ctx.enter_context(nc.psum_tensor(f"bank{i}", [128, 512], F32)) for i in range(8)]
        m.passed = ctx.enter_context(nc.semaphore("passed"))
        m.ctx_in = [ctx.enter_context(nc.semaphore(f"ctx{u}_in")) for u in range(2)]
        m.kv_done, m.kv_copied = ctx.enter_context(nc.semaphore("kv_done")), ctx.enter_context(nc.semaphore("kv_copied"))
        m.rows_in, m.turned, m.turned_copied = (ctx.enter_context(nc.semaphore(n)) for n in ("slots_in", "slots_turned", "slots_copied"))
        m.later_in = ctx.enter_context(nc.semaphore("later_in"))
        m.expert_in = [[ctx.enter_context(nc.semaphore(f"{n}{u}_in")) for u in range(2)] for n in ("w1_", "b1_", "w2_", "b2_")]
        m.ident = m.const[:, C_ID:C_ID + 128]

        silu_attention_phase(nc, d, m)
        if phases > 1:
            with ExitStack() as kv:
                m.kT = sb("kT", [128, KD, B, KEYS], F32, kv)
                m.v = sb("v", [KW, B, KT, D], F32, kv)
                m.ys = sb("ys", [S, B, D], F32, kv)
                m.wts = sb("wts", [S, 2, B], F32, kv)
                m.pos = sb("pos", [S, 2, B], U32, kv)
                m.first_tile = sb("first_tile", [1, E0 + 2], I32, kv)
                m.first_tiles = sb("first_tiles", [1, E0 // 2], I32, kv)
                m.xg_d = nc.dram_tensor("xg", [((1 << TB) + 2) * SLOT, D], F32, kind="Internal").ap()
                m.y_d = nc.dram_tensor("y", [(1 << TB) * SLOT, D], F32, kind="Internal").ap()
                with ExitStack() as ex:
                    m.w1, m.w2 = sb("w1", [128, 2, KD, 2 * HR], F32, ex), sb("w2", [128, 2, HM, D], F32, ex)
                    m.b1, m.b2 = sb("b1", [128, 2, 2 * HM], F32, ex), sb("b2", [128, 2, D], F32, ex)
                    m.xg, m.xgT = sb("xg_rows", [128, D], F32, ex), sb("xgT", [128, KD, SLOT], F32, ex)
                    route_phase(nc, d, m)
                    expert_phase(nc, d, m)
                soft_attention_phase(nc, d, m)
        if phases > 4:
            gated_phase(nc, d, m)
        else:
            with nc.semaphore("x_out") as x_out, nc.Block() as block:
                @block.sync
                def _(sp):
                    sp.dma_start(d["out"].rearrange("b s n -> s b n"), m.x[:]).then_inc(x_out, 16)
                    sp.wait_ge(x_out, 16)
        m.close_phase()
        m.live[0].close()


def load_expert_first(eng, d, m, e, u):
    w1_in = m.expert_in[0]
    src = d["L0_ffn_We1"][e:e + 1] if isinstance(e, int) else d["L0_ffn_We1"][bass.ds(e, 1)]
    eng.dma_start(m.w1[:, u, :, :], src.rearrange("a (k p) n -> p (a k) n", p=128)).then_inc(w1_in[u], 16)


def load_expert_rest(eng, d, m, e, u):
    def of(ap):
        return ap[e:e + 1] if isinstance(e, int) else ap[bass.ds(e, 1)]
    b1_in, w2_in, b2_in = m.expert_in[1:]
    eng.dma_start(m.b1[:, u, :], of(d["be1T"]).rearrange("a p n -> (a p) n")).then_inc(b1_in[u], 16)
    eng.dma_start(m.w2[:, u, :, :], of(d["L0_ffn_We2"]).rearrange("a (k p) n -> p (a k) n", p=128)).then_inc(w2_in[u], 16)
    eng.dma_start(m.b2[:, u, :], of(d["L0_ffn_be2"]).rearrange("a n -> (a n)").partition_broadcast(128)).then_inc(b2_in[u], 16)


def load_context(sp, d, m, b, u):
    hold(sp, m.kv_done, 4 * (b - 1), m.passed)
    src = d["ctxT"][b:b + 1] if isinstance(b, int) else d["ctxT"][bass.ds(b, 1)]
    sp.dma_start(m.ctxT[:, u, :, :], src.rearrange("a (k p) n -> p (a k) n", p=128)).then_inc(m.ctx_in[u], 16)


def project_context(pe, m, b, u, banks):
    pe.wait_ge(m.ctx_in[u], 8 * (b - u) + 16)
    for part in range(4):
        above(pe, m.kv_copied, 4 * (b - 1) + part + 1)
        bank = banks[part]
        if part < 2:
            for t in ((0, 1) if part == 0 else (2,)):
                for k in range(KD):
                    mm = pe.matmul(bank[:KW, (t % 2) * D:(t % 2 + 1) * D], m.ctxT[:, u, k, t * KW:(t + 1) * KW],
                                   m.wv1[:, k, :], start=k == 0, stop=k == KD - 1)
        else:
            for k in range(KD):
                mm = pe.matmul(bank[:, 0:KEYS], m.wk1[:, k, (part - 2) * 128:(part - 1) * 128], m.ctxT[:, u, k, :],
                               start=k == 0, stop=k == KD - 1)
        mm.then_inc(m.kv_done, 1)


def copy_context(act, m, b, banks):
    vb = m.v[:, b:b + 1] if isinstance(b, int) else m.v[:, bass.ds(b, 1)]
    kb = [m.kT[:, k, b:b + 1, :] if isinstance(b, int) else m.kT[:, k, bass.ds(b, 1), :] for k in range(KD)]
    for part in range(4):
        act.wait_ge(m.kv_done, 4 * b + part + 1)
        if part == 0:
            dst, src = vb[:, :, 0:2, :].rearrange("p a t n -> p (a t) n"), banks[0][:KW, :].rearrange("p (t n) -> p t n", t=2)
        elif part == 1:
            dst, src = vb[:, :, 2, :].rearrange("p a n -> p (a n)"), banks[1][:KW, 0:D]
        else:
            dst, src = kb[part - 2].rearrange("p a n -> p (a n)"), banks[part][:, 0:KEYS]
        act.activation(dst, src, ACT.Copy).then_inc(m.kv_copied, 1)


def normalise_rows(dve, m, row_stat, row_mv, row_dev, row_rstd, rows_done, x_loaded=None):
    if x_loaded is not None:
        dve.wait_ge(x_loaded, 16)
    for t in range(B):
        dve.bn_stats(m.stat[:, t, :], m.x[:, t, :]).then_inc(row_stat, 1)
    for t in range(B):
        dve.wait_ge(row_stat, t + 1)
        dve.bn_aggr(m.mv[:, t, :], m.stat[:, t, :]).then_inc(row_mv, 1)
    dve.wait_ge(row_dev, 1)
    dve.reciprocal(m.rstd[:], m.dev[:]).then_inc(row_rstd, 1)
    dve.wait_ge(row_rstd, 1)
    for t in range(B):
        dve.tensor_scalar(m.xn[:, t, :], m.x[:, t, :], m.mv[:, t, 0:1], m.rstd[:, t:t + 1],
                          ALU.subtract, ALU.mult).then_inc(rows_done, 1)


def deviations(act, m, row_mv, row_dev):
    act.wait_ge(row_mv, B)
    act.activation(m.dev[:], m.mv[:, :, 1], ACT.Sqrt, bias=m.const[:S, C_EPS:C_EPS + 1]).then_inc(row_dev, 1)


def transpose_rows(pe, m, banks, rows_done, turned, turned_copied):
    for t in range(B):
        pe.wait_ge(rows_done, t + 1)
        above(pe, turned_copied, t - 1)
        for k in range(KD):
            mm = pe.transpose(banks[t % 2][:, k * S:(k + 1) * S], m.xn[:, t, k * 128:(k + 1) * 128], m.ident[:S, :S])
        mm.then_inc(turned, 1)


def copy_turned(act, m, banks, turned, turned_copied):
    for t in range(B):
        act.wait_ge(turned, t + 1)
        act.activation(m.xT[:, :, t * S:(t + 1) * S], banks[t % 2][:, 0:KD * S].rearrange("p (k n) -> p k n", k=KD),
                       ACT.Copy).then_inc(turned_copied, 1)


def silu_attention_phase(nc, d, m):
    sem = m.open_phase(nc)
    with ExitStack() as ctx:
        def sb(name, shape, dt=F32):
            return ctx.enter_context(nc.sbuf_tensor(name, shape, dt))

        wq, wk, wv = sb("wq", [128, KD, 2 * D]), sb("wk", [128, KD, D]), sb("wv", [128, KD, D])
        wo = sb("wo", [128, G, D])
        bq, bk = sb("bq", [128, NQ]), sb("bk", [128, KD])
        bv = sb("bv", [KW, D])
        ctxT = sb("ctxT0", [128, 2, KD, KEYS])
        ks = sb("ks0", [128, 2, NQ, KEYS], F32R)
        kl = sb("kl0", [128, 2, KD, KEYS], F32R)
        q2 = sb("q2", [128, 2, NQ, B * S], F32R)
        v = sb("v0", [KW, 2, KT, D])
        qd = sb("qd0", [128, 2, 2, NQ, HQ, S], F32R)
        oT = sb("oT0", [128, 2, G, S])
        maskr = sb("maskr0", [KW, 2, KT, S], I32)
        keep = sb("keep0", [KW, 2, KT, S])
        AR = 6
        attn = sb("attn", [KW, AR, 4, S])
        warm = sb("warm", [128, 1])
        C = G * KT

        wv_in, wk_in, wq_in, bqk_in, bv_in, wo_zero, wo_in = (sem(n) for n in
            ("wv_in", "wk_in", "wq_in", "bqk_in", "bv_in", "wo_zero", "wo_in"))
        x_in, const_in, g_in, gates_done, rows_zero = (sem(n) for n in ("x_in", "const_in", "g_in", "gates_done", "rows_zero"))
        ctx_in = [sem("ctx_in0"), sem("ctx_in1")]
        mask_in = [sem("mask_in0"), sem("mask_in1")]
        row_stat, row_mv, row_dev, row_rstd, rows_done, turned, turned_copied = (sem(n) for n in
            ("row_stat", "row_mv", "row_dev", "row_rstd", "rows_done", "turned", "turned_copied"))
        q_done, qh_copied, ql_copied, qdh_done, qdl_done = (sem(n) for n in ("q_done", "qh_copied", "ql_copied", "qdh_done", "qdl_done"))
        v_done, v_copied, k_done, kh_done, kl_done = (sem(n) for n in ("v_done", "v_copied", "k_done", "kh_done", "kl_done"))
        ks_in = [sem("ks_in0"), sem("ks_in1")]
        keep_done, score_done, silu_done, attn_done, pv_done = (sem(n) for n in
            ("keep_done", "score_done", "silu_done", "attn_done", "pv_done"))
        o_copied, proj_done, x_done = sem("o_copied"), sem("proj_done"), sem("x_done")

        with nc.Block() as block:
            @block.sync
            def _(sp):
                sp.dma_start(wk[:], d["L0_xattn_WkT"].rearrange("(k p) n -> p k n", p=128)).then_inc(wk_in, 16)

                def context(b, u):
                    hold(sp, v_done, 2 * (b - 1), m.passed)
                    cs = d["ctxT"][b:b + 1] if isinstance(b, int) else d["ctxT"][bass.ds(b, 1)]
                    sp.dma_start(ctxT[:, u, :, :], cs.rearrange("a (k p) n -> p (a k) n", p=128)).then_inc(ctx_in[u], 16)
                    hold(sp, keep_done, b - 1, m.passed)
                    ms = d["mask0"][b:b + 1] if isinstance(b, int) else d["mask0"][bass.ds(b, 1)]
                    sp.dma_start(maskr[:, u, :, :], ms.rearrange("a (t p) q -> p (a t) q", p=KW)).then_inc(mask_in[u], 16)

                def stack_low(b, u):
                    hold(sp, kl_done, KD * (b + 1), m.passed)
                    sp.dma_start(ks[64:128, u, 0::2, :].bitcast(F32), kl[0:64, u, :, :].bitcast(F32)).then_inc(ks_in[u], 16)
                    sp.dma_start(ks[0:64, u, 1::2, :].bitcast(F32), kl[64:128, u, :, :].bitcast(F32)).then_inc(ks_in[u], 16)

                def batch(b, u):
                    stack_low(b, u)
                    if not (known(b, B - 2) or known(b, B - 1)):
                        context(b + 2, u)
                context(0, 0)
                context(1, 1)
                pairs(sp, batch)
                for u in range(2):
                    sp.wait_ge(ks_in[u], 32 * (B // 2))
                load_context(sp, d, m, 0, 0)
                load_context(sp, d, m, 1, 1)

            @block.gpsimd
            def _(pool):
                pool.memset(wo[:], 0.0).then_inc(wo_zero, 1)
                pool.memset(m.wo1[:], 0.0).then_inc(wo_zero, 1)
                pool.wait_ge(wo_zero, 2)
                for j in range(4):
                    src = d["L0_xattn_WoT"].rearrange("(g j r) n -> j r g n", j=4, r=DH)[j]
                    pool.dma_start(wo[32 * j:32 * j + DH, :, :], src).then_inc(wo_in, 16)

                def spread_low(b, u):
                    for g in range(NQ):
                        above(pool, score_done, C * (b - 1))
                        q = q2[:, 1, g, b * S:(b + 1) * S] if isinstance(b, int) else q2[:, 1, g, bass.ds(b * S, S)]
                        pool.tensor_tensor(qd[:, u, 1, g, :, :], spread_over(q, 1, HQ),
                                           spread_over(m.const[:, C_HEADQ:C_HEADQ + HQ], 2, S), ALU.mult).then_inc(qdl_done, 1)
                    if known(b, 1):
                        load_later_weights()
                        pool.wait_ge(ql_copied, 2 * NQ)

                def load_later_weights():
                    for dst, src in ((m.wk1, "L1_xattn_WkT"), (m.wv1, "L1_xattn_WvT"), (m.wq1, "L1_xattn_WqT"),
                                     (m.wr, "L0_ffn_Wr"), (m.ws1, "L0_ffn_Ws1"), (m.ws2, "L0_ffn_Ws2")):
                        pool.dma_start(dst[:], d[src].rearrange("(k p) n -> p k n", p=128)).then_inc(m.later_in, 16)
                    pool.dma_start(m.br[:], d["L0_ffn_br"].partition_broadcast(S)).then_inc(m.later_in, 16)
                    pool.dma_start(m.bs2[:], d["L0_ffn_bs2"].partition_broadcast(S)).then_inc(m.later_in, 16)
                    pool.dma_start(m.bs1[:], d["bs1T"]).then_inc(m.later_in, 16)
                    for j in range(4):
                        src = d["L1_xattn_WoT"].rearrange("(g j r) n -> j r g n", j=4, r=DH)[j]
                        pool.dma_start(m.wo1[32 * j:32 * j + DH, :, :], src).then_inc(m.later_in, 16)
                pool.wait_ge(ql_copied, NQ)
                pool.wait_ge(const_in, 16)
                pairs(pool, spread_low)
                pool.wait_ge(m.later_in, LATER)

            @block.scalar
            def _(act):
                act.dma_start(m.x[:], d["x"].rearrange("b s n -> s b n")).then_inc(x_in, 16)
                act.dma_start(m.const[:], d["const"]).then_inc(const_in, 16)
                act.dma_start(bq[:], d["bqT"]).then_inc(bqk_in, 16)
                act.dma_start(bk[:], d["bkT"]).then_inc(bqk_in, 16)
                act.dma_start(bv[:], d["L0_xattn_bv"].partition_broadcast(KW)).then_inc(bv_in, 16)
                act.dma_start(wq[:], d["L0_xattn_WqT"].rearrange("(k p) n -> p k n", p=128)).then_inc(wq_in, 16)
                act.dma_start(wv[:], d["L0_xattn_WvT"].rearrange("(k p) n -> p k n", p=128)).then_inc(wv_in, 16)
                act.dma_start(m.graw[:, 0:2], d["g_xattn"].partition_broadcast(128)).then_inc(g_in, 16)
                act.dma_start(m.graw[:, 2:4], d["g_ffn"].partition_broadcast(128)).then_inc(g_in, 16)
                act.wait_ge(const_in, 16)
                deviations(act, m, row_mv, row_dev)
                act.wait_ge(bqk_in, 32)

                def high_keys(b, u):
                    for k in range(KD):
                        act.wait_ge(k_done, KD * b + k + 1)
                        for a in range(2):
                            rows = slice(64 * a, 64 * a + 64)
                            ins = act.activation(ks[rows, u, 2 * k + a, :], m.bank[3 + k][rows, 0:KEYS], ACT.Identity, bias=bk[rows, k:k + 1])
                        ins.then_inc(kh_done, 1)

                def spread_high(b, u):
                    above(act, score_done, C * (b - 1))
                    q = q2[:, 0, :, b * S:(b + 1) * S] if isinstance(b, int) else q2[:, 0, :, bass.ds(b * S, S)]
                    for j in range(HQ):
                        ins = act.activation(qd[:, u, 0, :, j, :], q, ACT.Copy, scale=m.const[:, C_HEADQ + j:C_HEADQ + j + 1])
                    ins.then_inc(qdh_done, 1)

                copy_turned(act, m, m.bank[0:2], turned, turned_copied)
                high_keys(0, 0)
                act.wait_ge(g_in, 32)
                act.activation(m.gates[:], m.graw[:], ACT.Tanh).then_inc(gates_done, 1)
                act.activation(warm[:], m.graw[:, 0:1], ACT.Silu)
                for n in range(2 * NQ):
                    act.wait_ge(q_done, n + 1)
                    act.activation(q2[:, 0, n % NQ, (n // NQ) * 4 * S:(n // NQ + 1) * 4 * S], m.bank[n % 3][:, 0:4 * S],
                                   ACT.Identity, bias=bq[:, n % NQ:n % NQ + 1]).then_inc(qh_copied, 1)
                    if n == NQ:
                        act.wait_ge(qh_copied, NQ)
                        spread_high(0, 0)

                def silu_batch(b, u):
                    for c in range(C):
                        act.wait_ge(score_done, C * b + c + 1)
                        above(act, pv_done, G * b + c // KT - 1)
                        act.activation(attn[:, c % AR, :, :], m.bank[c % 3][:KW, 0:4 * S].rearrange("p (j n) -> p j n", j=4),
                                       ACT.Silu, scale=SCALE).then_inc(silu_done, 1)
                        if c == 2 * KT - 1 and not known(b, B - 1):
                            high_keys(b + 1, 1 - u)
                            spread_high(b + 1, 1 - u)
                pairs(act, silu_batch)

            @block.vector
            def _(dve):
                normalise_rows(dve, m, row_stat, row_mv, row_dev, row_rstd, rows_done, x_in)
                for i in (5, 6):
                    dve.memset(m.bank[i][:], 0.0).then_inc(rows_zero, 1)

                def turn_mask(b, u):
                    dve.wait_ge(mask_in[u], 8 * (b - u) + 16)
                    dve.tensor_scalar(keep[:, u, :, :], maskr[:, u, :, :], 0.0, None, ALU.not_equal).then_inc(keep_done, 1)

                def copy_values(b, u):
                    for t in range(KT):
                        dve.wait_ge(v_done, 2 * b + t // 2 + 1)
                        ins = dve.tensor_tensor(v[:, u, t, :], m.bank[3 + t // 2][:KW, (t % 2) * D:(t % 2 + 1) * D], bv[:], ALU.add)
                        if t > 0:
                            ins.then_inc(v_copied, 1)

                def mask_chunks(b, u, g):
                    for t in range(KT):
                        slot = attn[:, (g * KT + t) % AR, :, :]
                        dve.wait_ge(silu_done, C * b + g * KT + t + 1)
                        dve.tensor_tensor(slot, slot, spread_over(keep[:, u, t, :], 1, 4), ALU.mult).then_inc(attn_done, 1)

                def low_keys(b, u):
                    for k in range(KD):
                        dve.wait_ge(kh_done, KD * b + k + 1)
                        for a in range(2):
                            rows = slice(64 * a, 64 * a + 64)
                            ins = dve.scalar_tensor_tensor(out=kl[rows, u, k, :], in0=m.bank[3 + k][rows, 0:KEYS], scalar=bk[rows, k:k + 1],
                                                           in1=ks[rows, u, 2 * k + a, :].bitcast(F32), op0=ALU.add, op1=ALU.subtract)
                        ins.then_inc(kl_done, 1)

                dve.wait_ge(bv_in, 16)
                low_keys(0, 0)
                for n in range(2 * NQ):
                    if n == NQ:
                        copy_values(0, 0)
                    dve.wait_ge(qh_copied, n + 1)
                    half = slice((n // NQ) * 4 * S, (n // NQ + 1) * 4 * S)
                    dve.scalar_tensor_tensor(out=q2[:, 1, n % NQ, half], in0=m.bank[n % 3][:, 0:4 * S], scalar=bq[:, n % NQ:n % NQ + 1],
                                             in1=q2[:, 0, n % NQ, half].bitcast(F32), op0=ALU.add, op1=ALU.subtract).then_inc(ql_copied, 1)
                turn_mask(0, 0)
                dve.wait_ge(gates_done, 1)

                def residual(b):
                    dve.wait_ge(proj_done, b + 1)
                    xb = at(m.x, b).rearrange("p a n -> p (a n)")
                    dve.scalar_tensor_tensor(out=xb, in0=m.bank[7][:S, 0:D], scalar=m.gates[:S, 0:1], in1=xb,
                                             op0=ALU.mult, op1=ALU.add).then_inc(x_done, 1)

                def batch(b, u):
                    more = not known(b, B - 1)
                    dve.wait_ge(keep_done, b + 1)
                    mask_chunks(b, u, 0)
                    mask_chunks(b, u, 1)
                    if not known(b, 0):
                        residual(b - 1)
                    if more:
                        low_keys(b + 1, 1 - u)
                        turn_mask(b + 1, 1 - u)
                    mask_chunks(b, u, 2)
                    if more:
                        copy_values(b + 1, 1 - u)
                    mask_chunks(b, u, 3)
                    dve.wait_ge(pv_done, G * (b + 1))
                    dve.tensor_copy(oT[:, u, :, :], m.bank[5 + u][:, 0:G * S].rearrange("p (g n) -> p g n", g=G)).then_inc(o_copied, 1)
                pairs(dve, batch)
                residual(B - 1)

            @block.tensor
            def _(pe):
                def project_keys(b, u):
                    pe.wait_ge(ctx_in[u], 8 * (b - u) + 16)
                    for half in range(KD):
                        above(pe, v_copied, 2 * (b - 1) + half + 1)
                        for k in range(KD):
                            mm = pe.matmul(m.bank[3 + half][:, 0:KEYS], wk[:, k, half * 128:(half + 1) * 128], ctxT[:, u, k, :],
                                           start=k == 0, stop=k == KD - 1)
                        mm.then_inc(k_done, 1)

                def project_values(b, u):
                    for t in range(KT):
                        if t != 1:
                            pe.wait_ge(kl_done, KD * b + t // 2 + 1)
                        for k in range(KD):
                            mm = pe.matmul(m.bank[3 + t // 2][:KW, (t % 2) * D:(t % 2 + 1) * D], ctxT[:, u, k, t * KW:(t + 1) * KW],
                                           wv[:, k, :], start=k == 0, stop=k == KD - 1)
                        if t > 0:
                            mm.then_inc(v_done, 1)

                pe.wait_ge(wk_in, 16)
                project_keys(0, 0)
                pe.wait_ge(const_in, 16)
                transpose_rows(pe, m, m.bank[0:2], rows_done, turned, turned_copied)
                pe.wait_ge(wq_in, 16)
                pe.wait_ge(turned_copied, B)
                for n in range(2 * NQ):
                    if n == NQ:
                        pe.wait_ge(wv_in, 16)
                        project_values(0, 0)
                    above(pe, ql_copied, n - 2)
                    g = n % NQ
                    for k in range(KD):
                        mm = pe.matmul(m.bank[n % 3][:, 0:4 * S], wq[:, k, g * 128:(g + 1) * 128],
                                       m.xT[:, k, (n // NQ) * 4 * S:(n // NQ + 1) * 4 * S], start=k == 0, stop=k == KD - 1)
                    mm.then_inc(q_done, 1)
                pe.wait_ge(ql_copied, 2 * NQ)
                pe.wait_ge(wo_in, 64)
                pe.wait_ge(rows_zero, 2)

                def scores(b, u, g):
                    if g == 0:
                        pe.wait_ge(ks_in[u], 16 * (b - u) + 32)
                        pe.wait_ge(qdh_done, b + 1)
                        pe.wait_ge(qdl_done, NQ * (b + 1))
                    for t in range(KT):
                        c = g * KT + t
                        above(pe, silu_done, C * b + c - 2)
                        for part in range(2):
                            mm = pe.matmul(m.bank[c % 3][:KW, 0:4 * S], ks[:, u, g, t * KW:(t + 1) * KW],
                                           qd[:, u, part, g, :, :], start=part == 0, stop=part == 1)
                        mm.then_inc(score_done, 1)

                def values(b, u, g):
                    if g == 0:
                        pe.wait_ge(v_copied, 2 * (b + 1))
                        above(pe, o_copied, b - 1)
                    pe.wait_ge(attn_done, C * b + (g + 1) * KT)
                    for t in range(KT):
                        for j in range(4):
                            mm = pe.matmul(m.bank[5 + u][32 * j:32 * j + DH, g * S:(g + 1) * S],
                                           v[:, u, t, (4 * g + j) * DH:(4 * g + j + 1) * DH], attn[:, (g * KT + t) % AR, j, :],
                                           start=t == 0, stop=t == KT - 1, tile_position=(0, 32 * j))
                    mm.then_inc(pv_done, 1)

                def project_out(b, u):
                    pe.wait_ge(o_copied, b + 1)
                    above(pe, x_done, b)
                    for g in range(G):
                        mm = pe.matmul(m.bank[7][:S, 0:D], oT[:, u, g, :], wo[:, g, :], start=g == 0, stop=g == G - 1)
                    mm.then_inc(proj_done, 1)

                def batch(b, u):
                    more = not known(b, B - 1)
                    scores(b, u, 1)
                    if not known(b, 0):
                        project_out(b - 1, 1 - u)
                    if more:
                        project_keys(b + 1, 1 - u)
                    values(b, u, 0)
                    scores(b, u, 2)
                    values(b, u, 1)
                    if more:
                        project_values(b + 1, 1 - u)
                    scores(b, u, 3)
                    values(b, u, 2)
                    if more:
                        scores(b + 1, 1 - u, 0)
                    values(b, u, 3)
                scores(0, 0, 0)
                pairs(pe, batch)
                project_out(B - 1, 1)
    m.close_phase()


def route_phase(nc, d, m):
    sem = m.open_phase(nc)
    wr, br, ws1, bs1, ws2, bs2, ys, wts, pos, xg_d = m.wr, m.br, m.ws1, m.bs1, m.ws2, m.bs2, m.ys, m.wts, m.pos, m.xg_d
    with ExitStack() as ctx:
        def sb(name, shape, dt=F32):
            return ctx.enter_context(nc.sbuf_tensor(name, shape, dt))

        zeros = sb("zeros", [SLOT, ZR * D])
        gel = sb("gel", [128, 2, 4 * S])
        act_s = sb("act_s", [128, SM, B * S])
        logit = sb("logit", [S, B, E0])
        top = sb("top", [S, B, 8])
        topi = sb("topi", [S, B, 8], U32)
        topf = sb("topf", [S, B, 2])
        gap, ex, den = sb("gap", [S, B]), sb("ex", [S, B]), sb("den", [S, B])
        hot = sb("hot", [S, 2, B, E0])
        both = sb("both", [S, B, E0], BF16)
        trib, onesb = sb("trib", [S, S], BF16), sb("onesb", [S, 128], BF16)
        run = sb("run", [128, B + 1, E0])
        three = sb("three", [1, E0 // 2])
        over, tiles = sb("over", [128, E0, THR]), sb("tiles", [128, E0])
        low, start, end = sb("low", [128, E0, E0]), sb("start", [128, E0]), sb("end", [128, E0])
        base, picked, posf = sb("base", [S, B, E0]), sb("picked", [S, 2, B, E0]), sb("posf", [S, 2, B])

        zero_done, zero_out, scattered = sem("rzero_done"), sem("rzero_out"), sem("scattered")
        row_stat, row_mv, row_dev, row_rstd, rows_done, turned, turned_copied = (sem("r" + n) for n in
            ("row_stat", "row_mv", "row_dev", "row_rstd", "rows_done", "turned", "turned_copied"))
        logit_done, gap_done, ex_done, both_done, count_done, pos_done = (sem(n) for n in
            ("logit_done", "gap_done", "ex_done", "both_done", "count_done", "pos_done"))
        step = sem("route_step")
        h_done, gelu_done, act_done, y_done, y_copied = (sem(n) for n in
            ("sh_done", "sgelu_done", "sact_done", "sy_done", "sy_copied"))

        with nc.Block() as block:
            @block.sync
            def _(sp):
                for e in range(2):
                    load_expert_first(sp, d, m, e, e)
                    load_expert_rest(sp, d, m, e, e)
                sp.wait_ge(zero_done, 1)
                xz = xg_d[0:XROWS * SLOT, :].rearrange("(c p r) n -> c p (r n)", p=SLOT, r=ZR)
                for c in range(XROWS // ZR):
                    sp.dma_start(xz[c], zeros[:]).then_inc(zero_out, 16)
                sp.wait_ge(scattered, 16 * 2 * B)
                load_slots(sp, m, 0)

            @block.gpsimd
            def _(pool):
                m.clear_spent(pool)
                pool.memset(zeros[:], 0.0).then_inc(zero_done, 1)
                pool.wait_ge(zero_out, 16 * (XROWS // ZR))
                pool.wait_ge(pos_done, 1)
                for t in range(B):
                    for c in range(2):
                        pool.indirect_dma_start(out=xg_d, out_offset=bass.IndirectOffsetOnAxis(ap=pos[:, c, t:t + 1], axis=0),
                                                in_=m.xn[:, t, :], in_offset=None).then_inc(scattered, 16)
                pool.wait_ge(scattered, 16 * 2 * B)

            @block.scalar
            def _(act):
                deviations(act, m, row_mv, row_dev)
                copy_context(act, m, 0, m.bank[2:6])
                copy_turned(act, m, m.bank[0:2], turned, turned_copied)
                copy_context(act, m, 1, m.bank[2:6])
                act.wait_ge(gap_done, 1)
                act.activation(ex[:], gap[:], ACT.Exp).then_inc(ex_done, 1)
                for n in range(2 * SM):
                    act.wait_ge(h_done, n + 1)
                    above(act, act_done, n - 1)
                    act.activation(gel[:, n % 2, :], m.bank[3 + 2 * (n % 2)][:, 0:4 * S], ACT.Gelu,
                                   bias=bs1[:, SM + n % SM:SM + n % SM + 1]).then_inc(gelu_done, 1)
                copy_turned_slots(act, m, 0)

            @block.vector
            def _(dve):
                count = [0]

                def then(ins):
                    ins.then_inc(step, 1)
                    count[0] += 1
                    dve.wait_ge(step, count[0])

                dve.tensor_copy(trib[:], m.const[:S, C_TRI:C_TRI + S]).then_inc(both_done, 1)
                dve.memset(onesb[:], 1.0).then_inc(both_done, 1)
                dve.memset(run[:, 0, :], 0.0).then_inc(both_done, 1)
                normalise_rows(dve, m, row_stat, row_mv, row_dev, row_rstd, rows_done)
                dve.wait_ge(logit_done, 1)
                then(dve.tensor_tensor(logit[:], m.bank[7][:S, 0:B * E0].rearrange("p (t e) -> p t e", t=B),
                                       spread_over(br[:], 1, B), ALU.add))
                then(dve.tensor_scalar(logit[:], logit[:], 1.0 / TAU, None, ALU.mult))
                for t in range(B):
                    ins = dve.max(top[:, t, :], logit[:, t, :])
                then(ins)
                dve.tensor_tensor(gap[:], top[:, :, 1], top[:, :, 0], ALU.subtract).then_inc(gap_done, 1)
                for t in range(B):
                    ins = dve.max_index(topi[:, t, :], top[:, t, :], logit[:, t, :])
                then(ins)
                then(dve.tensor_copy(topf[:], topi[:, :, 0:2]))
                for c in range(2):
                    then(dve.tensor_tensor(hot[:, c, :, :], spread_over(m.const[:S, C_IOTA:C_IOTA + E0], 1, B),
                                           spread_over(topf[:, :, c], 2, E0), ALU.is_equal))
                dve.tensor_tensor(both[:], hot[:, 0, :, :], hot[:, 1, :, :], ALU.add).then_inc(both_done, 1)
                dve.wait_ge(ex_done, 1)
                then(dve.tensor_scalar(den[:], ex[:], 1.0, None, ALU.add))
                then(dve.reciprocal(wts[:, 0, :], den[:]))
                then(dve.tensor_tensor(wts[:, 1, :], ex[:], wts[:, 0, :], ALU.mult))
                dve.wait_ge(count_done, 1)
                for t in range(B):
                    then(dve.tensor_tensor(run[:, t + 1, :], m.bank[6][:, t * E0:(t + 1) * E0], run[:, t, :], ALU.add))
                then(dve.tensor_tensor(over[:], spread_over(run[:, B, :], 2, THR),
                                       spread_over(m.const[:, C_THR:C_THR + THR], 1, E0), ALU.is_gt))
                then(dve.tensor_reduce(tiles[:], over[:], AX.X, ALU.add))
                then(dve.tensor_scalar(tiles[:], tiles[:], 1.0, None, ALU.max))
                then(dve.tensor_tensor(low[:], spread_over(tiles[:], 1, E0),
                                       m.const[:, C_LOW:C_LOW + E0 * E0].rearrange("p (a b) -> p a b", a=E0), ALU.mult))
                then(dve.tensor_reduce(start[:], low[:], AX.X, ALU.add))
                then(dve.tensor_tensor(end[:], start[:], tiles[:], ALU.add))
                then(dve.tensor_tensor(base[:], m.bank[7][:S, 128:128 + B * E0].rearrange("p (t e) -> p t e", t=B),
                                       run[:S, 0:B, :], ALU.add))
                then(dve.scalar_tensor_tensor(out=base[:], in0=spread_over(start[:S, :], 1, B), scalar=float(SLOT), in1=base[:],
                                              op0=ALU.mult, op1=ALU.add))
                then(dve.tensor_tensor(picked[:], hot[:], spread_over(base[:], 1, 2), ALU.mult))
                then(dve.tensor_reduce(posf[:], picked[:], AX.X, ALU.add))
                dve.tensor_copy(pos[:], posf[:]).then_inc(pos_done, 1)
                then(dve.tensor_copy(m.first_tile[:, 0:E0], start[0:1, :]))
                then(dve.tensor_copy(m.first_tile[:, E0:E0 + 1], end[0:1, E0 - 1:E0]))
                then(dve.tensor_scalar(m.first_tile[:, E0 + 1:E0 + 2], end[0:1, E0 - 1:E0], -1.0, float(ET + 1), ALU.mult, ALU.add))
                then(dve.scalar_tensor_tensor(out=three[:], in0=start[0:1, 1::2], scalar=float(1 << TB), in1=start[0:1, 0::2], op0=ALU.mult, op1=ALU.add))
                then(dve.scalar_tensor_tensor(out=three[:], in0=end[0:1, 1::2], scalar=float(1 << 2 * TB), in1=three[:], op0=ALU.mult, op1=ALU.add))
                then(dve.tensor_copy(m.first_tiles[:], three[:]))
                for n in range(2 * SM):
                    dve.wait_ge(gelu_done, n + 1)
                    dve.scalar_tensor_tensor(out=act_s[:, n % SM, (n // SM) * 4 * S:(n // SM + 1) * 4 * S],
                                             in0=m.bank[2 + 2 * (n % 2)][:, 0:4 * S], scalar=bs1[:, n % SM:n % SM + 1],
                                             in1=gel[:, n % 2, :], op0=ALU.add, op1=ALU.mult).then_inc(act_done, 1)
                for t in range(B):
                    dve.wait_ge(y_done, t + 1)
                    dve.tensor_tensor(ys[:, t, :], m.bank[t % 2][:S, 0:D], bs2[:], ALU.add).then_inc(y_copied, 1)

            @block.tensor
            def _(pe):
                project_context(pe, m, 0, 0, m.bank[2:6])
                transpose_rows(pe, m, m.bank[0:2], rows_done, turned, turned_copied)
                pe.wait_ge(turned_copied, B)
                for t in range(B):
                    for k in range(KD):
                        mm = pe.matmul(m.bank[7][:S, t * E0:(t + 1) * E0], m.xT[:, k, t * S:(t + 1) * S], wr[:, k, :],
                                       start=k == 0, stop=k == KD - 1)
                mm.then_inc(logit_done, 1)

                project_context(pe, m, 1, 1, m.bank[2:6])

                def hidden(n):
                    above(pe, act_done, n - 1)
                    half, part = n // SM, n % SM
                    for a in range(2):
                        for k in range(KD):
                            mm = pe.matmul(m.bank[2 + 2 * (n % 2) + a][:, 0:4 * S],
                                           ws1[:, k, (a * SM + part) * 128:(a * SM + part + 1) * 128],
                                           m.xT[:, k, half * 4 * S:(half + 1) * 4 * S], start=k == 0, stop=k == KD - 1)
                    mm.then_inc(h_done, 1)
                pe.wait_ge(both_done, 4)
                flat = both[:].rearrange("p t e -> p (t e)")
                pe.matmul(m.bank[7][:S, 128:128 + B * E0], trib[:], flat, start=True, stop=True)
                pe.matmul(m.bank[6][:, 0:B * E0], onesb[:], flat, start=True, stop=True).then_inc(count_done, 1)
                pe.wait_ge(m.kv_copied, 8)
                for n in range(2 * SM):
                    hidden(n)
                pe.wait_ge(act_done, 2 * SM)
                for t in range(B):
                    above(pe, y_copied, t - 1)
                    for k in range(SM):
                        mm = pe.matmul(m.bank[t % 2][:S, 0:D], act_s[:, k, t * S:(t + 1) * S], ws2[:, k, :],
                                       start=k == 0, stop=k == SM - 1)
                    mm.then_inc(y_done, 1)
                    if t == B // 2:
                        turn_slots(pe, m, 0)
    m.close_phase()


def load_slots(eng, m, j):
    rows = m.xg_d[j * SLOT:(j + 1) * SLOT, :] if isinstance(j, int) else m.xg_d[bass.ds(j * SLOT, SLOT), :]
    eng.dma_start(m.xg[:], rows).then_inc(m.rows_in, 16)


def turn_slots(pe, m, j):
    pe.wait_ge(m.rows_in, 16 * j + 16)
    above(pe, m.turned_copied, j)
    for k in range(KD):
        mm = pe.transpose(m.bank[3][:, k * SLOT:(k + 1) * SLOT], m.xg[:, k * 128:(k + 1) * 128], m.ident)
    mm.then_inc(m.turned, 1)


def copy_turned_slots(act, m, j):
    act.wait_ge(m.turned, j + 1)
    act.activation(m.xgT[:], m.bank[3][:, 0:KD * SLOT].rearrange("p (k n) -> p k n", k=KD), ACT.Copy).then_inc(m.turned_copied, 1)
    load_slots(act, m, j + 1)


def expert_phase(nc, d, m):
    sem = m.open_phase(nc)
    with ExitStack() as ctx:
        def sb(name, shape, dt=F32):
            return ctx.enter_context(nc.sbuf_tensor(name, shape, dt))

        C = HM // 2
        gel, act_e = sb("gel_e", [128, C, 2, SLOT]), sb("act_e", [128, HM, SLOT])
        y, none = sb("y_rows", [128, D]), sb("no_rows", [128, D])

        h_done, gelu_done, act_done, y_done, y_copied, y_out = (sem("e" + n) for n in
            ("h_done", "gelu_done", "act_done", "y_done", "y_copied", "y_out"))
        none_done, none_out = sem("none_done"), sem("none_out")
        w1_in, b1_in, w2_in, b2_in = m.expert_in
        m.y_out = y_out

        def experts(eng, expert, tile, after=None):
            def pair(i, more):
                three = eng.value_load(m.first_tiles[0:1, bass.ds(i, 1)], min_val=0, max_val=(1 << 3 * TB) - 1)
                bounds = [three & (1 << TB) - 1, (three >> TB) & (1 << TB) - 1, three >> 2 * TB]
                for u in range(2):
                    expert(i, u)
                    with eng.Fori(bounds[u], bounds[u + 1]) as j:
                        tile(j, u)
                    if more and after is not None:
                        after(i, u)

            with eng.Fori(0, E0 // 2 - 1) as i:
                pair(i, True)
            pair(E0 // 2 - 1, False)

        with nc.Block() as block:
            @block.sync
            def _(sp):
                sp.sem_inc(y_out, 16)
                load_context(sp, d, m, 2, 0)
                load_context(sp, d, m, 3, 1)

                def store(j, u):
                    hold(sp, y_copied, j + 2, m.passed)
                    sp.dma_start(m.y_d[bass.ds(j * SLOT, SLOT), :], y[:]).then_inc(y_out, 16)
                experts(sp, lambda i, u: None, store, lambda i, u: load_expert_rest(sp, d, m, 2 * i + u + 2, u))

            @block.gpsimd
            def _(pool):
                m.clear_spent(pool)
                pool.memset(none[:], 0.0).then_inc(none_done, 1)
                pool.wait_ge(none_done, 1)
                end = pool.value_load(m.first_tile[0:1, E0:E0 + 1], min_val=1, max_val=ET)
                with pool.Fori(end, ET + 1) as j:
                    pool.dma_start(m.y_d[bass.ds(j * SLOT, SLOT), :], none[:]).then_inc(none_out, 16)
                spare = pool.value_load(m.first_tile[0:1, E0 + 1:E0 + 2], min_val=1, max_val=ET + 1)
                pool.wait_ge(none_out, 16 * spare)

            @block.scalar
            def _(act):
                def gelus(j, u):
                    for c in range(C):
                        act.wait_ge(h_done, C * j + c + 1)
                        act.wait_ge(act_done, C * j + c + 1)
                        for i in range(2):
                            ins = act.activation(gel[:, c, i, :], m.bank[c][:, (2 + i) * SLOT:(3 + i) * SLOT], ACT.Gelu,
                                                 bias=m.b1[:, u, HM + 2 * c + i:HM + 2 * c + i + 1])
                        ins.then_inc(gelu_done, 1)
                    copy_turned_slots(act, m, j + 1)
                experts(act, lambda i, u: hold(act, b1_in[u], 16 * i + 16, m.passed), gelus,
                        lambda i, u: load_expert_first(act, d, m, 2 * i + u + 2, u))
                end = act.value_load(m.first_tile[0:1, E0:E0 + 1], min_val=1, max_val=ET)
                hold(act, m.rows_in, 16 * end + 32, m.passed)

            @block.vector
            def _(dve):
                dve.sem_inc(act_done, C)
                dve.sem_inc(y_copied, 1)

                def multiply(j, u):
                    for c in range(C):
                        dve.wait_ge(gelu_done, C * j + c + 1)
                        dve.wait_ge(y_done, j + 1)
                        for i in range(2):
                            ins = dve.scalar_tensor_tensor(out=act_e[:, 2 * c + i, :], in0=m.bank[c][:, i * SLOT:(i + 1) * SLOT],
                                                           scalar=m.b1[:, u, 2 * c + i:2 * c + i + 1], in1=gel[:, c, i, :],
                                                           op0=ALU.add, op1=ALU.mult)
                        ins.then_inc(act_done, 1)
                    dve.wait_ge(y_done, j + 2)
                    dve.wait_ge(y_out, 16 * j + 16)
                    dve.tensor_tensor(y[:], m.bank[4][:, 0:D], m.b2[:, u, :], ALU.add).then_inc(y_copied, 1)

                def biases(i, u):
                    dve.wait_ge(b1_in[u], 16 * i + 16)
                    hold(dve, b2_in[u], 16 * i + 16, m.passed)
                experts(dve, biases, multiply)

            @block.tensor
            def _(pe):
                pe.sem_inc(y_done, 1)

                def tile(j, u):
                    pe.wait_ge(m.turned_copied, j + 1)
                    for c in range(C):
                        pe.wait_ge(act_done, C * j + c + 1)
                        for i in range(4):
                            part = (i // 2) * HM + 2 * c + i % 2
                            for k in range(KD):
                                mm = pe.matmul(m.bank[c][:, i * SLOT:(i + 1) * SLOT], m.w1[:, u, k, part * 128:(part + 1) * 128],
                                               m.xgT[:, k, :], start=k == 0, stop=k == KD - 1)
                        mm.then_inc(h_done, 1)
                    turn_slots(pe, m, j + 1)
                    pe.wait_ge(y_copied, j + 1)
                    for k in range(HM):
                        if k % 2 == 0:
                            pe.wait_ge(act_done, C * (j + 1) + k // 2 + 1)
                        mm = pe.matmul(m.bank[4][:, 0:D], act_e[:, k, :], m.w2[:, u, k, :], start=k == 0, stop=k == HM - 1)
                    mm.then_inc(y_done, 1)

                def weights(i, u):
                    pe.wait_ge(w1_in[u], 16 * i + 16)
                    hold(pe, w2_in[u], 16 * i + 16, m.passed)
                experts(pe, weights, tile)
    m.close_phase()


def soft_attention_phase(nc, d, m):
    sem = m.open_phase(nc)
    with ExitStack() as ctx:
        def sb(name, shape, dt=F32):
            return ctx.enter_context(nc.sbuf_tensor(name, shape, dt))

        v = sb("v1", [KW, 2, KT, D])
        EVEN = KEYS + KEYS % 2
        ks = sb("ks1", [128, 2, NQ, EVEN], F32R)
        kl = m.ws1[:].rearrange("p k n -> p (k n)")[:, 0:2 * KD * KEYS].bitcast(F32R).rearrange("p (u k n) -> p u k n", u=2, k=KD)
        q2 = sb("q21", [128, 2, NQ, B * S], F32R)
        qd = sb("qd1", [128, 2, 2, NQ, HQ, S], F32R)
        yg = qd[:S].rearrange("p a b g j n -> p (a b g j n)")[:, 0:2 * B * D].bitcast(F32).rearrange("p (c t n) -> p c t n", c=2, t=B)
        oT = sb("oT1", [128, 2, G, S])
        maskr = sb("maskr1", [S, 2, KEYS], U8)
        bias = sb("bias1", [S, 2, KEYS])
        PR = 4
        sm = m.xn[:].rearrange("p t n -> p (t n)")[:, 0:PR * KEYS].rearrange("p (r n) -> p r n", r=PR)
        p = m.ys[:].rearrange("p t n -> p (t n)")[:, 0:PR * KEYS].rearrange("p (r n) -> p r n", r=PR)
        pT = sb("pT", [KW, PR, KT, S])
        least = sb("least", [S, PR])
        rsum, rinv = sb("hsum", [S, 2, H]), sb("hinv", [S, 2, H])
        rT = sb("rT", [H, 2, S])

        got = [sem(f"got{t}") for t in range(B)]
        added, ready = sem("added"), sem("x_ready")
        row_stat, row_mv, row_dev, row_rstd, rows_done, turned, turned_copied = (sem(n + "1") for n in
            ("row_stat", "row_mv", "row_dev", "row_rstd", "rows_done", "turned", "turned_copied"))
        q_done, qh_copied, ql_copied, qdh_done, qdl_done, kh_done, kl_done, rows_zero = (sem(n + "1") for n in
            ("q_done", "qh_copied", "ql_copied", "qdh_done", "qdl_done", "kh_done", "kl_done", "rows_zero"))
        pad_zero = sem("pad_zero1")
        ks_in, v_in = [sem("ks1_in0"), sem("ks1_in1")], [sem("v1_in0"), sem("v1_in1")]
        mask_in = [sem("mask1_in0"), sem("mask1_in1")]
        bias_done, score_done, max_done, exp_done = (sem(n + "1") for n in
            ("bias_done", "score_done", "max_done", "exp_done"))
        pT_done, pT_copied, pTa_copied, pv_done = sem("pT_done1"), sem("pT_copied1"), sem("pTa_copied1"), sem("pv_done1")
        rinv_done, rT_done, rT_copied, rb_done, norm_done = (sem(n + "1") for n in
            ("rinv_done", "rT_done", "rT_copied", "rb_done", "norm_done"))
        o_copied, proj_done, x_done = sem("o_copied1"), sem("proj_done1"), sem("x_done1")

        def keys(b, k):
            return m.kT[:, k, b, :] if isinstance(b, int) else m.kT[:, k, bass.ds(b, 1), :].rearrange("p a n -> p (a n)")

        ovbank = [m.bank[6], m.bank[3]]
        qbank = [m.bank[i] for i in (0, 1, 7)]
        TL, VL = 3, 5
        COPY, DIVIDE, PROJECT, ADD, MASK = VL, VL + 2, (VL + 4, VL + 6), VL + 8, H - 1
        KEYS_HIGH, SPREAD = (1, 3), (9, 10, 12, 13)
        flat = [ap[:].rearrange(f"{names} -> p ({names[2:]})") for ap, names in
                ((m.ctxT, "p u k n"), (m.ws1, "p k n"), (m.wq1, "p k n"), (m.ws2, "p k n"))]
        m.vg = flat[0][:, 0:KD * E1 * R1].rearrange("p (k n) -> p k n", k=KD)
        first = [flat[1][:, q * 4 * S:(q + 1) * 4 * S] for q in range(EP)]
        second = [flat[0][:, KD * E1 * R1:KD * E1 * R1 + 4 * S], m.xe_last[:]] + [
            ap[:].rearrange("p k n -> p (k n)")[:, 0:4 * S] for ap in (m.wk1, m.wv1)]
        m.xe = [first, second]
        m.vd = [f[:, i * 2 * D:(i + 1) * 2 * D].rearrange("p (a n) -> p a n", a=2) for f in flat[2:] for i in range(2)]
        vg_in, vd_zero, vd_in, xe_done, xe_copied = (sem(n) for n in ("vg_in", "vd_zero", "vd_in", "xe_done", "xe_copied"))
        stat2, mv2, dev2, rstd2, rows2, turned2, turned2_copied = (sem("g" + n) for n in
            ("row_stat", "row_mv", "row_dev", "row_rstd", "rows_done", "turned", "turned_copied"))
        HB = B // 2

        AH = sorted((h - TL) % H for h in (5, 8, 11, 14))

        def wait_probs_copied(eng, b, h):
            if h < 0:
                b, h = b - 1, h + H
            if isinstance(b, int) and b < 0:
                return
            if h in AH:
                eng.wait_ge(pTa_copied, len(AH) * b + AH.index(h) + 1)
            else:
                eng.wait_ge(pT_copied, (H - len(AH)) * b + len([i for i in range(h + 1) if i not in AH]))

        with nc.Block() as block:
            @block.sync
            def _(sp):
                with sp.Fori(2, B // 2) as i:
                    for u in range(2):
                        load_context(sp, d, m, 2 * i + u, u)

                def mask(b, u):
                    hold(sp, bias_done, b - 1, m.passed)
                    ms = d["mask1"][b:b + 1] if isinstance(b, int) else d["mask1"][bass.ds(b, 1)]
                    sp.dma_start(maskr[:, u, :], ms.rearrange("a q k -> (a q) k")).then_inc(mask_in[u], 16)

                def parts(b, u):
                    hold(sp, kl_done, 2 * (b + 1), m.passed)
                    sp.dma_start(ks[64:128, u, 0::2, 0:KEYS].bitcast(F32), kl[0:64, u, :, :].bitcast(F32)).then_inc(ks_in[u], 16)
                    sp.dma_start(ks[0:64, u, 1::2, 0:KEYS].bitcast(F32), kl[64:128, u, :, :].bitcast(F32)).then_inc(ks_in[u], 16)
                    hold(sp, pv_done, H * (b - 1), m.passed)
                    sp.dma_start(v[:, u, :, :], at(m.v, b).rearrange("p a t n -> p (a t) n")).then_inc(v_in[u], 16)

                def batch(b, u):
                    mask(b, u)
                    parts(b, u)
                pairs(sp, batch)
                sp.wait_ge(m.kv_done, 4 * B)
                sp.dma_start(m.vg, d["VgT"].rearrange("(k p) n -> p k n", p=128)).then_inc(vg_in, 16)
                sp.wait_ge(vd_zero, EP)
                for e in range(E1):
                    a = e % 2
                    sp.dma_start(m.vd[e // 2][64 * a:64 * a + 64, a, :], d["VgR"][e * R1:(e + 1) * R1, :]).then_inc(vd_in, 16)
                sp.wait_ge(vd_in, 16 * E1)

            @block.gpsimd
            def _(pool):
                end = pool.value_load(m.first_tile[0:1, E0:E0 + 1], min_val=1, max_val=ET)
                hold(pool, m.y_out, 16 * end + 16, m.passed)
                for t in range(B):
                    for c in range(2):
                        pool.indirect_dma_start(out=yg[:, c, t, :], out_offset=None, in_=m.y_d[0:(ET + 1) * SLOT, :],
                                                in_offset=bass.IndirectOffsetOnAxis(ap=m.pos[:, c, t:t + 1], axis=0)).then_inc(got[t], 16)
                m.clear_spent(pool)
                pool.memset(ks[:, :, :, KEYS:EVEN].bitcast(F32), 0.0).then_inc(pad_zero, 1)

                def low_keys(b, u):
                    pool.wait_ge(kh_done, 2 * (b + 1))
                    for k in range(KD):
                        pool.tensor_tensor(kl[:, u, k, :], keys(b, k), ks[:, u, 2 * k, 0:KEYS].bitcast(F32), ALU.subtract).then_inc(kl_done, 1)

                def spread_low(b, u):
                    for g in range(NQ):
                        above(pool, score_done, H * (b - 1))
                        q = q2[:, 1, g, b * S:(b + 1) * S] if isinstance(b, int) else q2[:, 1, g, bass.ds(b * S, S)]
                        pool.tensor_tensor(qd[:, u, 1, g, :, :], spread_over(q, 1, HQ),
                                           spread_over(m.const[:, C_HEADQ:C_HEADQ + HQ], 2, S), ALU.mult).then_inc(qdl_done, 1)

                for t in range(B):
                    pool.wait_ge(got[t], 32)

                def batch(b, u):
                    low_keys(b, u)
                    if known(b, 0):
                        pool.wait_ge(ql_copied, NQ)
                    if known(b, 1):
                        pool.wait_ge(ql_copied, 2 * NQ)
                    spread_low(b, u)
                pairs(pool, batch)
                for q in range(EP):
                    pool.memset(m.vd[q], 0.0).then_inc(vd_zero, 1)

            @block.scalar
            def _(act):
                def high_keys(b, u, k):
                    act.activation(ks[:, u, 2 * k:2 * k + 2, 0:KEYS], spread_over(keys(b, k), 1, 2), ACT.Copy).then_inc(kh_done, 1)

                def spread_high(b, u, j):
                    q = q2[:, 0, :, b * S:(b + 1) * S] if isinstance(b, int) else q2[:, 0, :, bass.ds(b * S, S)]
                    act.activation(qd[:, u, 0, :, j, :], q, ACT.Copy, scale=m.const[:, C_HEADQ + j:C_HEADQ + j + 1]).then_inc(qdh_done, 1)

                for k in range(KD):
                    high_keys(0, 0, k)
                with act.Fori(2, B - 2) as b:
                    copy_context(act, m, b, m.bank[2:6])
                deviations(act, m, row_mv, row_dev)
                copy_context(act, m, B - 2, m.bank[2:6])
                copy_turned(act, m, m.bank[0:2], turned, turned_copied)
                for n in range(2 * NQ):
                    act.wait_ge(q_done, n + 1)
                    act.activation(q2[:, 0, n % NQ, (n // NQ) * 4 * S:(n // NQ + 1) * 4 * S], qbank[n % 3][:, 0:4 * S],
                                   ACT.Copy).then_inc(qh_copied, 1)
                    if n == NQ - 1:
                        act.wait_ge(qh_copied, NQ)
                        for j in range(HQ):
                            spread_high(0, 0, j)
                        copy_context(act, m, B - 1, m.bank[2:6])
                act.wait_ge(qh_copied, 2 * NQ)

                def turn_sums(b, u):
                    act.wait_ge(rT_done, b + 1)
                    act.activation(rT[:, u, :], m.bank[7][:H, 0:S], ACT.Copy).then_inc(rT_copied, 1)

                def copy_probs(n, slot, bank):
                    act.wait_ge(pT_done, n + 1)
                    above(act, pv_done, n - PR + 1)
                    act.activation(pT[:, slot, :, :], m.bank[bank][:KW, 0:KT * S].rearrange("p (t n) -> p t n", t=KT),
                                   ACT.Copy).then_inc(pTa_copied, 1)

                def batch(b, u):
                    for h in range(H):
                        n = H * b + h
                        act.wait_ge(max_done, n + 1)
                        above(act, pT_done, n - PR + 1)
                        act.activation(p[:, h % PR, :], sm[:, h % PR, :], ACT.Exp, bias=least[:, h % PR:h % PR + 1],
                                       scale=-1.0, accum_out=rsum[:, u, h:h + 1]).then_inc(exp_done, 1)
                        if h == 3 and not known(b, 0):
                            turn_sums(b - 1, 1 - u)
                        if (h - TL) % H in AH and (h >= TL or not known(b, 0)):
                            copy_probs(n - TL, (h - TL) % PR, 4 + (h - TL) % 2)
                        if not known(b, B - 1):
                            if h in KEYS_HIGH:
                                high_keys(b + 1, 1 - u, KEYS_HIGH.index(h))
                            if h in SPREAD:
                                spread_high(b + 1, 1 - u, SPREAD.index(h))
                pairs(act, batch)
                for h in range(TL):
                    if (h - TL) % H in AH:
                        copy_probs(H * B - TL + h, (h - TL) % PR, 4 + (h - TL) % 2)
                turn_sums(B - 1, 1)

                def half_deviations(half):
                    act.wait_ge(mv2, HB * (half + 1))
                    ts = slice(HB * half, HB * (half + 1))
                    act.activation(m.dev[:, ts], m.mv[:, ts, 1], ACT.Sqrt, bias=m.const[:S, C_EPS:C_EPS + 1]).then_inc(dev2, 1)
                half_deviations(0)
                for half in range(2):
                    for t in range(HB * half, HB * (half + 1)):
                        act.wait_ge(turned2, t + 1)
                        act.activation(m.xT[:, :, t * S:(t + 1) * S], m.bank[t % 2][:, 0:KD * S].rearrange("p (k n) -> p k n", k=KD),
                                       ACT.Copy).then_inc(turned2_copied, 1)
                    for q in range(EP):
                        n = half * EP + q
                        act.wait_ge(xe_done, n + 1)
                        act.activation(m.xe[half][q], m.bank[2 + n % 2][:, 0:4 * S], ACT.Copy).then_inc(xe_copied, 1)
                        if n == 0:
                            half_deviations(1)

            @block.vector
            def _(dve):
                for t in range(B):
                    dve.wait_ge(got[t], 32)
                    dve.scalar_tensor_tensor(out=m.ys[:, t, :], in0=yg[:, 0, t, :], scalar=m.wts[:, 0, t:t + 1], in1=m.ys[:, t, :],
                                             op0=ALU.mult, op1=ALU.add).then_inc(added, 1)
                    dve.wait_ge(added, 2 * t + 1)
                    dve.scalar_tensor_tensor(out=m.ys[:, t, :], in0=yg[:, 1, t, :], scalar=m.wts[:, 1, t:t + 1], in1=m.ys[:, t, :],
                                             op0=ALU.mult, op1=ALU.add).then_inc(added, 1)
                    dve.wait_ge(added, 2 * t + 2)
                    dve.scalar_tensor_tensor(out=m.x[:, t, :], in0=m.ys[:, t, :], scalar=m.gates[:S, 2:3], in1=m.x[:, t, :],
                                             op0=ALU.mult, op1=ALU.add).then_inc(ready, 16 // B)
                normalise_rows(dve, m, row_stat, row_mv, row_dev, row_rstd, rows_done, ready)
                dve.memset(ovbank[0][:], 0.0).then_inc(rows_zero, 1)
                for n in range(2 * NQ):
                    dve.wait_ge(qh_copied, n + 1)
                    half = slice((n // NQ) * 4 * S, (n // NQ + 1) * 4 * S)
                    dve.tensor_tensor(q2[:, 1, n % NQ, half], qbank[n % 3][:, 0:4 * S], q2[:, 0, n % NQ, half].bitcast(F32),
                                      ALU.subtract).then_inc(ql_copied, 1)
                dve.wait_ge(m.kv_copied, 4 * B)
                dve.memset(ovbank[1][:], 0.0).then_inc(rows_zero, 1)

                def turn_mask(b, u):
                    dve.wait_ge(mask_in[u], 8 * (b - u) + 16)
                    dve.tensor_scalar(bias[:, u, :], maskr[:, u, :], 0.0, NEG1, ALU.is_gt, ALU.mult).then_inc(bias_done, 1)

                def maximum(b, u, h):
                    n = H * b + h
                    above(dve, exp_done, n - PR + 1)
                    hold(dve, score_done, n + 1, m.passed)
                    dve.tensor_tensor_reduce(sm[:, h % PR, :], m.bank[(H * u + h) % 3][:S, 0:KEYS], bias[:, u, :], -SCALE, FAR,
                                             ALU.add, ALU.min, least[:, h % PR:h % PR + 1]).then_inc(max_done, 1)

                def copy_probs(n, slot, bank):
                    dve.wait_ge(pT_done, n + 1)
                    above(dve, pv_done, n - PR + 1)
                    dve.tensor_copy(pT[:, slot, :, :], m.bank[bank][:KW, 0:KT * S].rearrange("p (t n) -> p t n", t=KT)).then_inc(pT_copied, 1)

                def invert_sums(b, u):
                    dve.wait_ge(exp_done, H * (b + 1))
                    dve.reciprocal(rinv[:, u, :], rsum[:, u, :]).then_inc(rinv_done, 1)

                def copy_out(b, u):
                    dve.wait_ge(pv_done, H * (b + 1))
                    dve.tensor_copy(oT[:, u, :, :], ovbank[u][:, 0:G * S].rearrange("p (g n) -> p g n", g=G)).then_inc(o_copied, 1)

                def divide(b, u):
                    dve.wait_ge(rb_done, b + 1)
                    dve.wait_ge(o_copied, b + 1)
                    dve.tensor_tensor(oT[:, u, :, :], m.bank[7][:, 0:G * S].rearrange("p (g n) -> p g n", g=G), oT[:, u, :, :],
                                      ALU.mult).then_inc(norm_done, 1)

                def residual(b, u):
                    dve.wait_ge(proj_done, b + 1)
                    xb = at(m.x, b).rearrange("p a n -> p (a n)")
                    dve.scalar_tensor_tensor(out=xb, in0=m.bank[7][:S, 0:D], scalar=m.gates[:S, 1:2], in1=xb,
                                             op0=ALU.mult, op1=ALU.add).then_inc(x_done, 1)

                turn_mask(0, 0)

                def batch(b, u):
                    dve.wait_ge(bias_done, b + 1)
                    for h in range(H):
                        n = H * b + h
                        maximum(b, u, h)
                        if (h - TL) % H not in AH and (h >= TL or not known(b, 0)):
                            copy_probs(n - TL, (h - TL) % PR, 4 + (h - TL) % 2)
                        if not known(b, 0):
                            if h == 1:
                                invert_sums(b - 1, 1 - u)
                            if h == COPY:
                                copy_out(b - 1, 1 - u)
                            if h == DIVIDE:
                                divide(b - 1, 1 - u)
                            if h == ADD:
                                residual(b - 1, 1 - u)
                        if h == MASK and not known(b, B - 1):
                            turn_mask(b + 1, 1 - u)
                pairs(dve, batch)
                for h in range(TL):
                    if (h - TL) % H not in AH:
                        copy_probs(H * B - TL + h, (h - TL) % PR, 4 + (h - TL) % 2)
                invert_sums(B - 1, 1)
                copy_out(B - 1, 1)

                def half_stats(half):
                    dve.wait_ge(x_done, B if half else HB)
                    for t in range(HB * half, HB * (half + 1)):
                        dve.bn_stats(m.stat[:, t, :], m.x[:, t, :]).then_inc(stat2, 1)
                    for t in range(HB * half, HB * (half + 1)):
                        dve.wait_ge(stat2, t + 1)
                        dve.bn_aggr(m.mv[:, t, :], m.stat[:, t, :]).then_inc(mv2, 1)

                def half_rows(half):
                    dve.wait_ge(dev2, half + 1)
                    ts = slice(HB * half, HB * (half + 1))
                    dve.reciprocal(m.rstd[:, ts], m.dev[:, ts]).then_inc(rstd2, 1)
                    dve.wait_ge(rstd2, half + 1)
                    for t in range(HB * half, HB * (half + 1)):
                        dve.tensor_scalar(m.xn[:, t, :], m.x[:, t, :], m.mv[:, t, 0:1], m.rstd[:, t:t + 1],
                                          ALU.subtract, ALU.mult).then_inc(rows2, 1)
                half_stats(0)
                divide(B - 1, 1)
                half_rows(0)
                residual(B - 1, 1)
                half_stats(1)
                half_rows(1)

            @block.tensor
            def _(pe):
                with pe.Fori(1, B // 2 - 1) as i:
                    for u in range(2):
                        project_context(pe, m, 2 * i + u, u, m.bank[2:6])
                project_context(pe, m, B - 2, 0, m.bank[2:6])
                transpose_rows(pe, m, m.bank[0:2], rows_done, turned, turned_copied)
                pe.wait_ge(turned_copied, B)
                def project_queries(half):
                    for g in range(NQ):
                        n = half * NQ + g
                        above(pe, ql_copied, n - 2)
                        for k in range(KD):
                            mm = pe.matmul(qbank[n % 3][:, 0:4 * S], m.wq1[:, k, g * 128:(g + 1) * 128],
                                           m.xT[:, k, half * 4 * S:(half + 1) * 4 * S], start=k == 0, stop=k == KD - 1)
                        mm.then_inc(q_done, 1)
                project_queries(0)
                project_context(pe, m, B - 1, 1, m.bank[2:6])
                project_queries(1)
                pe.wait_ge(ql_copied, 2 * NQ)
                pe.wait_ge(m.kv_copied, 4 * B)
                pe.wait_ge(rows_zero, 2)
                pe.wait_ge(pad_zero, 1)

                def scores(b, u, h):
                    if h == 0:
                        pe.wait_ge(ks_in[u], 16 * (b - u) + 32)
                        pe.wait_ge(qdh_done, HQ * (b + 1))
                        pe.wait_ge(qdl_done, NQ * (b + 1))
                    above(pe, max_done, H * b + h - (1 if u == 0 and h < 2 else 2))
                    for part in range(2):
                        mm = pe.matmul(m.bank[(H * u + h) % 3][:S, 0:EVEN], qd[:, u, part, h // HQ, h % HQ, :], ks[:, u, h // HQ, :],
                                       start=part == 0, stop=part == 1)
                    mm.then_inc(score_done, 1)

                def turn_probs(b, h):
                    pe.wait_ge(exp_done, H * b + h + 1)
                    wait_probs_copied(pe, b, h - 2)
                    for t in range(KT):
                        mm = pe.transpose(m.bank[4 + h % 2][:KW, t * S:(t + 1) * S], p[:, h % PR, t * KW:(t + 1) * KW], m.ident[:S, :S])
                    mm.then_inc(pT_done, 1)

                def values(b, u, h):
                    if h == 0:
                        pe.wait_ge(v_in[u], 8 * (b - u) + 16)
                        above(pe, o_copied, b - 1)
                    wait_probs_copied(pe, b, h)
                    g, j = h // 4, h % 4
                    for t in range(KT):
                        mm = pe.matmul(ovbank[u][32 * j:32 * j + DH, g * S:(g + 1) * S], v[:, u, t, h * DH:(h + 1) * DH],
                                       pT[:, h % PR, t, :], start=t == 0, stop=t == KT - 1, tile_position=(0, 32 * j))
                    mm.then_inc(pv_done, 1)

                def turn_sums(b, u):
                    pe.wait_ge(rinv_done, b + 1)
                    above(pe, x_done, b)
                    pe.transpose(m.bank[7][:H, 0:S], rinv[:, u, :], m.ident[:S, :S]).then_inc(rT_done, 1)

                def spread_sums(b, u):
                    pe.wait_ge(rT_copied, b + 1)
                    for g in range(G):
                        mm = pe.matmul(m.bank[7][:, g * S:(g + 1) * S], m.const[:H, C_SPREAD + g * 128:C_SPREAD + (g + 1) * 128],
                                       rT[:, u, :], start=True, stop=True)
                    mm.then_inc(rb_done, 1)

                def project_out(b, u, half):
                    if half == 0:
                        pe.wait_ge(norm_done, b + 1)
                    for g in range(half * G // 2, (half + 1) * G // 2):
                        mm = pe.matmul(m.bank[7][:S, 0:D], oT[:, u, g, :], m.wo1[:, g, :], start=g == 0, stop=g == G - 1)
                    if half == 1:
                        mm.then_inc(proj_done, 1)

                def batch(b, u):
                    first = known(b, 0)
                    for h in range(H):
                        scores(b, u, h)
                        if h >= TL or not first:
                            turn_probs(b if h >= TL else b - 1, (h - TL) % H)
                        if h >= VL:
                            values(b, u, h - VL)
                        elif not first:
                            values(b - 1, 1 - u, H + h - VL)
                        if not first:
                            if h == 3:
                                turn_sums(b - 1, 1 - u)
                            if h == 5:
                                spread_sums(b - 1, 1 - u)
                            for i in range(2):
                                if h == PROJECT[i]:
                                    project_out(b - 1, 1 - u, i)
                pairs(pe, batch)
                for h in range(VL):
                    if h < TL:
                        turn_probs(B - 1, H - TL + h)
                    values(B - 1, 1, H - VL + h)
                turn_sums(B - 1, 1)
                spread_sums(B - 1, 1)
                for half in range(2):
                    project_out(B - 1, 1, half)

                for half in range(2):
                    for t in range(HB * half, HB * (half + 1)):
                        pe.wait_ge(rows2, t + 1)
                        above(pe, turned2_copied, t - 1)
                        for k in range(KD):
                            mm = pe.transpose(m.bank[t % 2][:, k * S:(k + 1) * S], m.xn[:, t, k * 128:(k + 1) * 128], m.ident[:S, :S])
                        mm.then_inc(turned2, 1)
                    pe.wait_ge(turned2_copied, HB * (half + 1))
                    if half == 0:
                        pe.wait_ge(vg_in, 16)
                    for q in range(EP):
                        n = half * EP + q
                        above(pe, xe_copied, n - 1)
                        for k in range(KD):
                            mm = pe.matmul(m.bank[2 + n % 2][:, 0:4 * S], m.vg[:, k, q * 128:(q + 1) * 128],
                                           m.xT[:, k, half * 4 * S:(half + 1) * 4 * S], start=k == 0, stop=k == KD - 1)
                        mm.then_inc(xe_done, 1)
    m.close_phase()


def gated_phase(nc, d, m):
    sem = m.open_phase(nc)
    with ExitStack() as ctx:
        def sb(name, shape, dt=F32):
            return ctx.enter_context(nc.sbuf_tensor(name, shape, dt))

        we, wp = sb("we", [128, KD, E1 * D]), sb("wp", [128, KD, D])
        weh, wel = sb("weh", [128, KD, E1 * D], F32R), sb("wel", [128, KD, E1 * D], F32R)
        xTh, xTl = sb("xTh", [128, KD, B * S], F32R), sb("xTl", [128, KD, B * S], F32R)
        bb = sb("bb", [E1 + 1, D])
        diff = sb("diff", [S, 2, 2, D])
        junk = sb("junk", [S, 2, D])
        r2, res = sb("r2", [S, B, E1]), sb("res", [S, B, E1])
        rmin, rsum, rinv = sb("rmin", [S, B]), sb("rsum", [S, B]), sb("rinv", [S, B])
        gap, ex, rw = sb("gap1", [S, B, E1]), sb("ex1", [S, B, E1]), sb("rw", [S, B, E1])
        top, topi, topf = sb("top1", [S, B, 8]), sb("topi1", [S, B, 8], U32), sb("topf1", [S, B, 2])
        hot = sb("hot1", [S, 2, B, E1])
        over, overb, onesb = sb("over1", [S, B, E1]), sb("overb", [S, B, E1], BF16), sb("ones1", [S, S], BF16)
        cnt, some, none = sb("cnt", [S, 1]), sb("some", [S, 1]), sb("none", [S, 1])
        mask, fw, sw, swz = sb("chosen1", [S, B, E1]), sb("fw", [S, B, E1]), sb("sw", [S, B]), sb("swz", [S, B])
        w9, w9T = sb("w9", [S, B, E1 + 1]), sb("w9T", [E1 + 1, B, S])
        acc = sb("acc", [S, 2, D])

        wp_in, we_in = sem("wp_in"), sem("we_in")
        high_done, low_done = sem("high_done"), sem("low_done")
        proj_done, diff_done, sq_done = sem("gproj_done"), sem("diff_done"), sem("sq_done")
        gap_done, ex_done, over_done, cnt_done, w_done, wT_done, wT_copied = (sem(n) for n in
            ("ggap_done", "gex_done", "over_done", "cnt_done", "w_done", "wT_done", "wT_copied"))
        base_done, base_copied, e_done, e_added, tile_done = (sem(n) for n in
            ("base_done", "base_copied", "e_done", "e_added", "tile_done"))
        step, res_done = sem("gate_step"), sem("res_done")
        out_done = [sem("out_done0"), sem("out_done1")]

        def part(n):
            return slice((n % EP) * (E1 * D // EP), (n % EP + 1) * (E1 * D // EP))

        with nc.Block() as block:
            @block.sync
            def _(sp):
                sp.dma_start(we[:], d["WeT"].rearrange("(k p) n -> p k n", p=128)).then_inc(we_in, 16)
                sp.dma_start(wp[:], d["WpT"].rearrange("(k p) n -> p k n", p=128)).then_inc(wp_in, 16)
                sp.dma_start(bb[0:E1, :], d["L1_ffn_be"]).then_inc(wp_in, 16)
                sp.dma_start(bb[E1:E1 + 1, :], d["L1_ffn_bp"].partition_broadcast(1)).then_inc(wp_in, 16)
                for t in range(B):
                    sp.wait_ge(tile_done, t + 1)
                    sp.dma_start(d["out"][t], m.x[:, t, :]).then_inc(out_done[t % 2], 16)
                for u in range(2):
                    sp.wait_ge(out_done[u], 16 * B // 2)

            @block.gpsimd
            def _(pool):
                for k in range(KD):
                    pool.tensor_copy(xTh[:, k, :], m.xT[:, k, :]).then_inc(high_done, 1)
                pool.wait_ge(we_in, 16)
                for n in range(2 * EP):
                    pool.tensor_copy(weh[:, n // EP, part(n)], we[:, n // EP, part(n)]).then_inc(high_done, 1)

            @block.scalar
            def _(act):
                for n in range(B * EP):
                    act.wait_ge(diff_done, n + 1)
                    for a in range(2):
                        ins = act.activation(junk[:, a, :], diff[:, n % 2, a, :], ACT.Square,
                                             accum_out=r2[:, n // EP, 2 * (n % EP) + a:2 * (n % EP) + a + 1])
                        ins.then_inc(sq_done, 1)
                        act.wait_ge(sq_done, 2 * n + a + 1)
                act.activation(res[:], r2[:], ACT.Sqrt).then_inc(res_done, 1)
                act.wait_ge(gap_done, 1)
                act.activation(ex[:], gap[:], ACT.Exp, scale=-1.0).then_inc(ex_done, 1)
                act.wait_ge(wT_done, 1)
                act.activation(w9T[:, 0:4, :], m.bank[0][:E1 + 1, 0:4 * S].rearrange("p (t n) -> p t n", t=4), ACT.Copy).then_inc(wT_copied, 1)
                act.activation(w9T[:, 4:8, :], m.bank[1][:E1 + 1, 0:4 * S].rearrange("p (t n) -> p t n", t=4), ACT.Copy).then_inc(wT_copied, 1)
                for t in range(B):
                    act.wait_ge(base_done, t + 1)
                    above(act, tile_done, t - 1)
                    act.activation(acc[:, t % 2, :], m.bank[3 - t % 2][:S, 0:D], ACT.Copy).then_inc(base_copied, 1)

            @block.vector
            def _(dve):
                count = [0]

                def then(ins):
                    ins.then_inc(step, 1)
                    count[0] += 1
                    dve.wait_ge(step, count[0])

                dve.memset(onesb[:], 1.0).then_inc(over_done, 1)
                dve.memset(w9[:], 1.0).then_inc(over_done, 1)
                LOW = (7, 10) + tuple(range(14, 14 + 4 * EP, 2))

                def low(i):
                    dve.wait_ge(high_done, i + 1)
                    n = i - KD
                    w, h, l = ((m.xT[:, i, :], xTh[:, i, :], xTl[:, i, :]) if i < KD else
                               (we[:, n // EP, part(n)], weh[:, n // EP, part(n)], wel[:, n // EP, part(n)]))
                    dve.tensor_tensor(l, w, h.bitcast(F32), ALU.subtract).then_inc(low_done, 1)

                for n in range(B * EP):
                    dve.wait_ge(proj_done, n + 1)
                    above(dve, sq_done, 2 * (n - 1))
                    dve.tensor_tensor(diff[:, n % 2, :, :], m.bank[4 + n % 4][:S, :].rearrange("p (a n) -> p a n", a=2),
                                      spread_over(m.xn[:, n // EP, :], 1, 2), ALU.subtract).then_inc(diff_done, 1)
                    if n in LOW:
                        low(LOW.index(n))
                dve.wait_ge(res_done, 1)
                then(dve.tensor_reduce(rmin[:], res[:], AX.X, ALU.min))
                dve.tensor_tensor(gap[:], res[:], spread_over(rmin[:], 2, E1), ALU.subtract).then_inc(gap_done, 1)
                dve.wait_ge(ex_done, 1)
                then(dve.tensor_reduce(rsum[:], ex[:], AX.X, ALU.add))
                then(dve.reciprocal(rinv[:], rsum[:]))
                then(dve.tensor_tensor(rw[:], ex[:], spread_over(rinv[:], 2, E1), ALU.mult))
                then(dve.tensor_scalar(over[:], rw[:], 1.0 / E1, None, ALU.is_gt))
                dve.tensor_copy(overb[:], over[:]).then_inc(over_done, 1)
                for t in range(B):
                    ins = dve.max(top[:, t, :], rw[:, t, :])
                then(ins)
                for t in range(B):
                    ins = dve.max_index(topi[:, t, :], top[:, t, :], rw[:, t, :])
                then(ins)
                then(dve.tensor_copy(topf[:], topi[:, :, 0:2]))
                for c in range(2):
                    then(dve.tensor_tensor(hot[:, c, :, :], spread_over(m.const[:S, C_IOTA:C_IOTA + E1], 1, B),
                                           spread_over(topf[:, :, c], 2, E1), ALU.is_equal))
                dve.wait_ge(cnt_done, 1)
                then(dve.tensor_reduce(cnt[:], m.bank[2][:S, 0:B * E1], AX.X, ALU.max))
                then(dve.tensor_scalar(some[:], cnt[:], 0.0, None, ALU.is_gt))
                then(dve.tensor_scalar(none[:], cnt[:], 0.0, None, ALU.is_equal))
                then(dve.tensor_scalar(mask[:], over[:], some[:, 0:1], None, ALU.mult))
                then(dve.scalar_tensor_tensor(out=mask[:], in0=hot[:, 0, :, :], scalar=none[:, 0:1], in1=mask[:],
                                              op0=ALU.mult, op1=ALU.add))
                then(dve.tensor_tensor(fw[:], rw[:], mask[:], ALU.mult))
                then(dve.tensor_tensor(mask[:], hot[:, 0, :, :], hot[:, 1, :, :], ALU.add))
                then(dve.tensor_tensor(fw[:], fw[:], mask[:], ALU.mult))
                then(dve.tensor_reduce(sw[:], fw[:], AX.X, ALU.add))
                then(dve.tensor_scalar(swz[:], sw[:], 0.0, None, ALU.is_equal))
                then(dve.tensor_tensor(sw[:], sw[:], swz[:], ALU.add))
                then(dve.reciprocal(rinv[:], sw[:]))
                dve.tensor_tensor(w9[:, :, 0:E1], fw[:], spread_over(rinv[:], 2, E1), ALU.mult).then_inc(w_done, 1)
                dve.wait_ge(w_done, 1)
                n = 0
                for t in range(B):
                    dve.wait_ge(base_copied, t + 1)
                    for q in range(EP):
                        dve.wait_ge(e_done, EP * t + q + 1)
                        for a in range(2):
                            e = 2 * q + a
                            ins = dve.scalar_tensor_tensor(out=acc[:, t % 2, :], in0=m.bank[4 + q][:S, a * D:(a + 1) * D],
                                                           scalar=w9[:, t, e:e + 1], in1=acc[:, t % 2, :], op0=ALU.mult, op1=ALU.add)
                            ins.then_inc(e_added, 1)
                            n += 1
                            dve.wait_ge(e_added, n)
                    dve.scalar_tensor_tensor(out=m.x[:, t, :], in0=acc[:, t % 2, :], scalar=m.gates[:S, 3:4], in1=m.x[:, t, :],
                                             op0=ALU.mult, op1=ALU.add).then_inc(tile_done, 1)

            @block.tensor
            def _(pe):
                for n in range(B * EP):
                    above(pe, diff_done, n - 3)
                    pe.matmul(m.bank[4 + n % 4][:S, :], m.xe[n // EP // 4][n % EP][:, (n // EP % 4) * S:(n // EP % 4 + 1) * S], m.vd[n % EP],
                              start=True, stop=True).then_inc(proj_done, 1)

                def experts(t, pairs_of_experts=range(EP)):
                    for q in pairs_of_experts:
                        above(pe, e_added, 2 * (EP * (t - 1) + q + 1))
                        n = 0
                        for xs, ws in ((xTh, weh), (xTh, wel), (xTl, weh)):
                            for k in range(KD):
                                mm = pe.matmul(m.bank[4 + q][:S, :], xs[:, k, t * S:(t + 1) * S], ws[:, k, q * 2 * D:(q + 1) * 2 * D],
                                               start=n == 0, stop=n == 3 * KD - 1)
                                n += 1
                        mm.then_inc(e_done, 1)

                pe.wait_ge(low_done, 2 * EP + KD)
                pe.wait_ge(diff_done, B * EP)
                experts(0, range(0, EP // 2 + 1))
                pe.wait_ge(over_done, 3)
                pe.matmul(m.bank[2][:S, 0:B * E1], onesb[:], overb[:].rearrange("p t e -> p (t e)"), start=True, stop=True).then_inc(cnt_done, 1)
                experts(0, range(EP // 2 + 1, EP))

                def pretrained(t):
                    for k in range(KD):
                        pe.matmul(m.bank[3 - t % 2][:S, 0:D], m.xT[:, k, t * S:(t + 1) * S], wp[:, k, :], start=k == 0, stop=False)
                pe.wait_ge(wp_in, 48)
                pretrained(0)
                pe.wait_ge(w_done, 1)
                for t in range(B):
                    mm = pe.transpose(m.bank[t // 4][:E1 + 1, (t % 4) * S:(t % 4 + 1) * S], w9[:, t, :], m.ident[:S, :S])
                mm.then_inc(wT_done, 1)
                pretrained(1)
                pe.wait_ge(wT_copied, 2)
                for t in range(B):
                    above(pe, base_copied, t - 1)
                    if t > 1:
                        pretrained(t)
                    pe.matmul(m.bank[3 - t % 2][:S, 0:D], w9T[:, t, :], bb[:], start=False, stop=True).then_inc(base_done, 1)
                    if t > 0:
                        experts(t)


def kernel(x, ctx_1024, mask_Bx1xSxS2_ik1, mask_BxSxS2_bk1, g_xattn, g_ffn,
           L0_xattn_Wq, L0_xattn_bq, L0_xattn_Wk, L0_xattn_bk, L0_xattn_Wv, L0_xattn_bv, L0_xattn_Wo,
           L0_ffn_Ws1, L0_ffn_bs1, L0_ffn_Ws2, L0_ffn_bs2, L0_ffn_We1, L0_ffn_be1, L0_ffn_We2, L0_ffn_be2,
           L0_ffn_Wr, L0_ffn_br, L1_xattn_Wq, L1_xattn_Wk, L1_xattn_Wv, L1_xattn_Wo,
           L1_ffn_Wp, L1_ffn_bp, L1_ffn_We, L1_ffn_be, L1_ffn_Vg):
    import numpy as np
    import concourse.bacc as bacc
    from concourse.bass_utils import run_bass_kernel_spmd

    a = np.asarray
    arrays = {
        "x": a(x),
        "ctxT": a(ctx_1024).transpose(0, 2, 1),
        "mask0": a(mask_Bx1xSxS2_ik1)[:, 0].transpose(0, 2, 1),
        "mask1": a(mask_BxSxS2_bk1),
        "g_xattn": a(g_xattn),
        "g_ffn": a(g_ffn),
        "L0_xattn_WqT": np.tile(a(L0_xattn_Wq).T.reshape(D, NQ, 1, D // NQ), (1, 1, 2, 1)).reshape(D, 2 * D),
        "L0_xattn_WkT": a(L0_xattn_Wk).T,
        "L0_xattn_WvT": a(L0_xattn_Wv).T, "L0_xattn_WoT": a(L0_xattn_Wo).T,
        "bqT": np.tile(a(L0_xattn_bq).reshape(NQ, 64).T, (2, 1)), "bkT": a(L0_xattn_bk).reshape(KD, 128).T, "L0_xattn_bv": a(L0_xattn_bv),
        "L1_xattn_WqT": np.tile(a(L1_xattn_Wq).T.reshape(D, NQ, 1, D // NQ), (1, 1, 2, 1)).reshape(D, 2 * D),
        "L1_xattn_WkT": a(L1_xattn_Wk).T,
        "L1_xattn_WvT": a(L1_xattn_Wv).T, "L1_xattn_WoT": a(L1_xattn_Wo).T,
        "L0_ffn_Ws1": a(L0_ffn_Ws1), "bs1T": a(L0_ffn_bs1).reshape(2 * SM, 128).T, "L0_ffn_Ws2": a(L0_ffn_Ws2), "L0_ffn_bs2": a(L0_ffn_bs2),
        "L0_ffn_We1": a(L0_ffn_We1), "L0_ffn_We2": a(L0_ffn_We2), "L0_ffn_be2": a(L0_ffn_be2),
        "be1T": a(L0_ffn_be1).reshape(E0, 2 * HM, 128).transpose(0, 2, 1),
        "L0_ffn_Wr": a(L0_ffn_Wr), "L0_ffn_br": a(L0_ffn_br),
        "WpT": a(L1_ffn_Wp).T, "L1_ffn_bp": a(L1_ffn_bp), "L1_ffn_be": a(L1_ffn_be),
        "WeT": a(L1_ffn_We).transpose(2, 0, 1).reshape(D, E1 * D),
        "VgT": a(L1_ffn_Vg).transpose(1, 0, 2).reshape(D, E1 * R1),
        "VgR": a(L1_ffn_Vg).transpose(0, 2, 1).reshape(E1 * R1, D),
        "const": constants(),
    }
    arrays = {"in_" + k: np.ascontiguousarray(v) for k, v in arrays.items()}
    nc = bacc.Bacc("TRN2", target_bir_lowering=False, num_devices=1)
    d = {k[3:]: nc.dram_tensor(k, v.shape, mybir.dt.from_np(v.dtype), kind="ExternalInput").ap() for k, v in arrays.items()}
    d["out"] = nc.dram_tensor("out", (B, S, D), F32, kind="ExternalOutput").ap()
    build(nc, d)
    r = run_bass_kernel_spmd(nc, [arrays], core_ids=[0])
    return r.results[0]["out"]
```
